# Optimizing a Trainium2 kernel written in Bass

```python
import numpy as np
import jax
import jax.numpy as jnp

def _softmax(x, axis=-1):
    return jax.nn.softmax(x, axis=axis)

def _gelu(x):
    return jax.nn.gelu(x, approximate=True)

def _silu(x):
    return jax.nn.silu(x)

def _sigmoid(x):
    return jax.nn.sigmoid(x)

def _layernorm(x, axis=-1, eps=1e-05):
    m = jnp.mean(x, axis=axis, keepdims=True)
    v = jnp.var(x, axis=axis, keepdims=True)
    return (x - m) / jnp.sqrt(v + eps)

def _scatter_add(tgt, idx, src, axis=0):
    return tgt.at[idx].add(src)

def _segment_sum(src, seg, n):
    return jax.ops.segment_sum(src, seg, n)
kernel_name = 'mk_decoder_postln_d2_seqx_r8_16acaa'

def setup_inputs(seed: int=0):
    np.random.seed(seed)
    _w = jnp.asarray

    def _rec_inputs():
        import jax
        import jax.numpy as jnp
        _rk = jax.random.key(seed)
        x = 7.22e-05 + 1 * jax.random.normal(jax.random.fold_in(_rk, 1), (8, 256, 128), jnp.float32)
        _lenS = 256 - jax.random.randint(jax.random.fold_in(_rk, 7), (8,), 0, max(1, 256 // 4) + 1, jnp.int32)
        _lenS2 = 256 - jax.random.randint(jax.random.fold_in(_rk, 8), (8,), 0, max(1, 256 // 4) + 1, jnp.int32)
        _ctx_1024P = jax.random.normal(jax.random.fold_in(_rk, 11), (8, 16, 128), jnp.float32)
        _ctx_1024c = jax.random.dirichlet(jax.random.fold_in(_rk, 511), 0.3 * jnp.ones((16,), jnp.float32), (8, 256))
        _ctx_1024t = jnp.einsum('bsk,bkd->bsd', _ctx_1024c, _ctx_1024P)
        _ctx_1024t = _ctx_1024t * jax.lax.rsqrt(jnp.mean(jnp.square(_ctx_1024t)) + 1e-12) * 0.953939
        ctx_1024 = 4.13588e-05 + 0.999923 * (_ctx_1024t + 0.3 * jax.random.normal(jax.random.fold_in(_rk, 611), (8, 256, 128), jnp.float32))
        _validS = jnp.arange(256)[None, :] < _lenS[:, None]
        _validS2 = jnp.arange(256)[None, :] < _lenS2[:, None]
        _causal = jnp.tril(jnp.ones((256, 256), dtype=bool))
        mask_BxSxS2_bf1 = jnp.ones((8, 256, 256), dtype=bool)
        return (x, ctx_1024, mask_BxSxS2_bf1)
    x, ctx_1024, mask_BxSxS2_bf1 = _rec_inputs()

    def _L0_attn_setup():
        import jax, jax.numpy as jnp
        import numpy as np
        DIM = 128
        HID = 512
        NUM_HEADS = 4
        WINDOW = 64
        NUM_PM = 64
        NEG = -1e+30

        def _swa(x_in, wq, wk, wv, wo):
            B, S, D = x_in.shape
            h, dh = (NUM_HEADS, D // NUM_HEADS)
            q = (x_in @ wq.T).reshape(B, S, h, dh).transpose(0, 2, 1, 3)
            k = (x_in @ wk.T).reshape(B, S, h, dh).transpose(0, 2, 1, 3)
            v = (x_in @ wv.T).reshape(B, S, h, dh).transpose(0, 2, 1, 3)
            i = jnp.arange(S)[:, None]
            j = jnp.arange(S)[None, :]
            mask = (j <= i) & (j > i - WINDOW)
            logits = jnp.einsum('bhqd,bhkd->bhqk', q, k) / np.sqrt(dh).astype(np.float32)
            logits = jnp.where(mask, logits, NEG)
            attn = jax.nn.softmax(logits, axis=-1)
            out = jnp.einsum('bhqk,bhkd->bhqd', attn, v)
            out = out.transpose(0, 2, 1, 3).reshape(B, S, D)
            return out @ wo.T

        def _mlp(w1, b1, w2, b2, x):
            return jax.nn.silu(x @ w1.T + b1) @ w2.T + b2
        key = jax.random.key(seed)
        ks = jax.random.split(key, 12)
        B, S = (2, 256)
        sc = 0.02
        n = lambda k, shape, s=sc: jax.random.normal(k, shape, jnp.float32) * s
        return {'x': n(ks[0], (B, S, DIM), 1.0), 'mem': n(ks[1], (NUM_PM, DIM), 1.0), 'wq': n(ks[2], (DIM, DIM)), 'wk': n(ks[3], (DIM, DIM)), 'wv': n(ks[4], (DIM, DIM)), 'wo': n(ks[5], (DIM, DIM)), 'w1': n(ks[6], (HID, DIM)), 'b1': jnp.zeros((HID,), jnp.float32), 'w2': n(ks[7], (DIM, HID)), 'b2': jnp.zeros((DIM,), jnp.float32), 'lin1': n(ks[8], (DIM, DIM)), 'lin2': n(ks[9], (DIM, DIM)), 'alpha': jnp.float32(0.0001), 'theta': jnp.float32(0.0001)}
    _L0_attn_all = _L0_attn_setup()
    _L0_attn_in = {k: v for k, v in _L0_attn_all.items() if k in ('mem', 'wq', 'wk', 'wv', 'wo', 'w1', 'b1', 'w2', 'b2', 'lin1', 'lin2', 'alpha', 'theta')}
    del _L0_attn_all

    def _L0_xattn_setup():
        import jax, jax.numpy as jnp
        import numpy as np
        N_HEADS = 16
        HIDDEN = 128
        KEY_SIZE = HIDDEN // N_HEADS
        key = jax.random.key(seed)
        ks = jax.random.split(key, 12)
        B, S, H = (4, 256, HIDDEN)
        scale = 1.0 / np.sqrt(H)
        inp = {'query': jax.random.normal(ks[0], (B, S, H), jnp.float32), 'key': jax.random.normal(ks[1], (B, S, H), jnp.float32), 'value': jax.random.normal(ks[2], (B, S, H), jnp.float32), 'mask': jnp.ones((B, S, S), dtype=bool)}
        for i, name in enumerate(['wq', 'wk', 'wv', 'wo']):
            inp[name] = jax.random.normal(ks[3 + i], (H, H), jnp.float32) * scale
            inp['b' + name[1]] = jnp.zeros((H,), jnp.float32)
        return inp
    _L0_xattn_all = _L0_xattn_setup()
    _L0_xattn_in = {k: v for k, v in _L0_xattn_all.items() if k in ('wq', 'bq', 'wk', 'bk', 'wv', 'bv', 'wo', 'bo')}
    del _L0_xattn_all

    def _L0_ffn_setup():
        import jax, jax.numpy as jnp
        import numpy as np
        NUM_EXPERTS = 8
        TOP_K = 2
        CAP_RATIO = 1.25
        INIT_STD = 0.02
        key = jax.random.key(seed)
        k1, k2, k3, k4 = jax.random.split(key, 4)
        B, T, H, F = (4, 256, 128, 512)
        x = jax.random.normal(k1, (B, T, H), jnp.float32)
        router_w = jax.random.normal(k2, (NUM_EXPERTS, H), jnp.float32) * INIT_STD
        w1 = jax.random.normal(k3, (NUM_EXPERTS, H, F), jnp.float32) * INIT_STD
        w2 = jax.random.normal(k4, (NUM_EXPERTS, F, H), jnp.float32) * INIT_STD
        return {'x': x, 'router_w': router_w, 'w1': w1, 'w2': w2}
    _L0_ffn_all = _L0_ffn_setup()
    _L0_ffn_in = {k: v for k, v in _L0_ffn_all.items() if k in ('router_w', 'w1', 'w2')}
    del _L0_ffn_all

    def _L1_attn_setup():
        import jax, jax.numpy as jnp
        import numpy as np
        B, S, D = (4, 256, 128)

        def _xavier(key, shape):
            bound = float(np.sqrt(6.0 / (shape[0] + shape[1])))
            return jax.random.uniform(key, shape, dtype=jnp.float32, minval=-bound, maxval=bound)
        key = jax.random.key(seed)
        k0, k1, k2, k3 = jax.random.split(key, 4)
        return {'embeddings': jax.random.normal(k0, (B, S, D), dtype=jnp.float32), 'W_Q': _xavier(k1, (D, D)), 'W_K': _xavier(k2, (D, D)), 'W_V': _xavier(k3, (D, D))}
    _L1_attn_all = _L1_attn_setup()
    _L1_attn_in = {k: v for k, v in _L1_attn_all.items() if k in ('W_Q', 'W_K', 'W_V')}
    del _L1_attn_all

    def _L1_xattn_setup():
        import jax, jax.numpy as jnp
        import numpy as np
        B, S, E, NH = (1, 256, 128, 8)
        DH = E // NH
        EPS = 1e-06
        LN_EPS = 1e-05
        key = jax.random.key(seed)
        ks = jax.random.split(key, 8)
        q = jax.random.normal(ks[0], (B, S, E), dtype=jnp.float32)
        k = jax.random.normal(ks[1], (B, S, E), dtype=jnp.float32)
        v = jax.random.normal(ks[2], (B, S, E), dtype=jnp.float32)
        scale = 1.0 / np.sqrt(3 * E)
        igate_w = jax.random.normal(ks[3], (NH, 3 * E), dtype=jnp.float32) * scale
        igate_b = jax.random.normal(ks[4], (NH,), dtype=jnp.float32) * 0.1
        fgate_w = jax.random.normal(ks[5], (NH, 3 * E), dtype=jnp.float32) * scale
        fgate_b = jnp.linspace(3.0, 6.0, NH, dtype=jnp.float32)
        out_w = 1.0 + 0.1 * jax.random.normal(ks[6], (E,), dtype=jnp.float32)
        return {'q': q, 'k': k, 'v': v, 'igate_w': igate_w, 'igate_b': igate_b, 'fgate_w': fgate_w, 'fgate_b': fgate_b, 'out_w': out_w}
    _L1_xattn_all = _L1_xattn_setup()
    _L1_xattn_in = {k: v for k, v in _L1_xattn_all.items() if k in ('igate_w', 'igate_b', 'fgate_w', 'fgate_b', 'out_w')}
    del _L1_xattn_all

    def _L1_ffn_setup():
        import jax, jax.numpy as jnp
        import numpy as np
        NEG_INF = -1e+30
        K = 2
        key = jax.random.key(seed)
        ks = jax.random.split(key, 5)
        B, S, D, O, E = (8, 256, 128, 128, 8)
        scale = 1.0 / np.sqrt(D)
        return {'x': jax.random.normal(ks[0], (B, S, D), dtype=jnp.float32), 'gate_w': jax.random.normal(ks[1], (E, D), dtype=jnp.float32) * scale, 'gate_b': jnp.zeros((E,), dtype=jnp.float32), 'expert_w': jax.random.normal(ks[2], (E, O, D), dtype=jnp.float32) * scale, 'expert_b': jnp.zeros((E, O), dtype=jnp.float32)}
    _L1_ffn_all = _L1_ffn_setup()
    _L1_ffn_in = {k: v for k, v in _L1_ffn_all.items() if k in ('gate_w', 'gate_b', 'expert_w', 'expert_b')}
    del _L1_ffn_all
    return {'x': x, 'ctx_1024': ctx_1024, 'mask_BxSxS2_bf1': mask_BxSxS2_bf1, 'L0_attn_mem': _L0_attn_in['mem'], 'L0_attn_wq': _L0_attn_in['wq'], 'L0_attn_wk': _L0_attn_in['wk'], 'L0_attn_wv': _L0_attn_in['wv'], 'L0_attn_wo': _L0_attn_in['wo'], 'L0_attn_w1': _L0_attn_in['w1'], 'L0_attn_b1': _L0_attn_in['b1'], 'L0_attn_w2': _L0_attn_in['w2'], 'L0_attn_b2': _L0_attn_in['b2'], 'L0_attn_lin1': _L0_attn_in['lin1'], 'L0_attn_lin2': _L0_attn_in['lin2'], 'L0_attn_alpha': _L0_attn_in['alpha'], 'L0_attn_theta': _L0_attn_in['theta'], 'L0_xattn_wq': _L0_xattn_in['wq'], 'L0_xattn_bq': _L0_xattn_in['bq'], 'L0_xattn_wk': _L0_xattn_in['wk'], 'L0_xattn_bk': _L0_xattn_in['bk'], 'L0_xattn_wv': _L0_xattn_in['wv'], 'L0_xattn_bv': _L0_xattn_in['bv'], 'L0_xattn_wo': _L0_xattn_in['wo'], 'L0_xattn_bo': _L0_xattn_in['bo'], 'L0_ffn_router_w': _L0_ffn_in['router_w'], 'L0_ffn_w1': _L0_ffn_in['w1'], 'L0_ffn_w2': _L0_ffn_in['w2'], 'L1_attn_W_Q': _L1_attn_in['W_Q'], 'L1_attn_W_K': _L1_attn_in['W_K'], 'L1_attn_W_V': _L1_attn_in['W_V'], 'L1_xattn_igate_w': _L1_xattn_in['igate_w'], 'L1_xattn_igate_b': _L1_xattn_in['igate_b'], 'L1_xattn_fgate_w': _L1_xattn_in['fgate_w'], 'L1_xattn_fgate_b': _L1_xattn_in['fgate_b'], 'L1_xattn_out_w': _L1_xattn_in['out_w'], 'L1_ffn_gate_w': _L1_ffn_in['gate_w'], 'L1_ffn_gate_b': _L1_ffn_in['gate_b'], 'L1_ffn_expert_w': _L1_ffn_in['expert_w'], 'L1_ffn_expert_b': _L1_ffn_in['expert_b']}

def reference(x, ctx_1024, mask_BxSxS2_bf1, L0_attn_mem, L0_attn_wq, L0_attn_wk, L0_attn_wv, L0_attn_wo, L0_attn_w1, L0_attn_b1, L0_attn_w2, L0_attn_b2, L0_attn_lin1, L0_attn_lin2, L0_attn_alpha, L0_attn_theta, L0_xattn_wq, L0_xattn_bq, L0_xattn_wk, L0_xattn_bk, L0_xattn_wv, L0_xattn_bv, L0_xattn_wo, L0_xattn_bo, L0_ffn_router_w, L0_ffn_w1, L0_ffn_w2, L1_attn_W_Q, L1_attn_W_K, L1_attn_W_V, L1_xattn_igate_w, L1_xattn_igate_b, L1_xattn_fgate_w, L1_xattn_fgate_b, L1_xattn_out_w, L1_ffn_gate_w, L1_ffn_gate_b, L1_ffn_expert_w, L1_ffn_expert_b):
    import jax
    import jax.numpy as jnp

    def _L0_attn_ref(x, mem, wq, wk, wv, wo, w1, b1, w2, b2, lin1, lin2, alpha, theta):
        import jax, jax.numpy as jnp
        import numpy as np
        DIM = 128
        HID = 512
        NUM_HEADS = 4
        WINDOW = 64
        NUM_PM = 64
        NEG = -1e+30

        def _swa(x_in, wq, wk, wv, wo):
            B, S, D = x_in.shape
            h, dh = (NUM_HEADS, D // NUM_HEADS)
            q = (x_in @ wq.T).reshape(B, S, h, dh).transpose(0, 2, 1, 3)
            k = (x_in @ wk.T).reshape(B, S, h, dh).transpose(0, 2, 1, 3)
            v = (x_in @ wv.T).reshape(B, S, h, dh).transpose(0, 2, 1, 3)
            i = jnp.arange(S)[:, None]
            j = jnp.arange(S)[None, :]
            mask = (j <= i) & (j > i - WINDOW)
            logits = jnp.einsum('bhqd,bhkd->bhqk', q, k) / np.sqrt(dh).astype(np.float32)
            logits = jnp.where(mask, logits, NEG)
            attn = jax.nn.softmax(logits, axis=-1)
            out = jnp.einsum('bhqk,bhkd->bhqd', attn, v)
            out = out.transpose(0, 2, 1, 3).reshape(B, S, D)
            return out @ wo.T

        def _mlp(w1, b1, w2, b2, x):
            return jax.nn.silu(x @ w1.T + b1) @ w2.T + b2
        B, S, D = x.shape
        pm = jnp.broadcast_to(mem[None], (B, NUM_PM, D))
        x_in = jnp.concatenate([pm, x], axis=1)
        out_swa = _swa(x_in, wq, wk, wv, wo)
        k_flat = x_in.reshape(-1, D)
        v_flat = out_swa.reshape(-1, D)

        def loss_fn(params):
            pred = _mlp(*params, k_flat)
            return 0.5 * jnp.sum((pred - v_flat) ** 2)
        grads = jax.grad(loss_fn)((w1, b1, w2, b2))
        upd = jax.tree_util.tree_map(lambda p, g: (1.0 - alpha) * p - theta * g, (w1, b1, w2, b2), grads)
        out_mem = _mlp(*upd, k_flat).reshape(x_in.shape)
        g1 = jax.nn.sigmoid(out_swa @ lin1.T)
        g2 = jax.nn.sigmoid(out_mem @ lin2.T)
        out_merged = g1 * out_swa + g2 * out_mem
        return out_merged[:, NUM_PM:, :]

    def _L0_xattn_ref(query, key, value, mask, wq, bq, wk, bk, wv, bv, wo, bo):
        import jax, jax.numpy as jnp
        import numpy as np
        N_HEADS = 16
        HIDDEN = 128
        KEY_SIZE = HIDDEN // N_HEADS
        B, S, H = query.shape

        def proj(x, w, b):
            y = jnp.einsum('bsh,oh->bso', x, w) + b
            return y.reshape(B, -1, N_HEADS, KEY_SIZE).transpose(0, 2, 1, 3)
        q = proj(query, wq, bq)
        k = proj(key, wk, bk)
        v = proj(value, wv, bv)
        scores = jnp.einsum('bhqd,bhkd->bhqk', q, k) / np.sqrt(KEY_SIZE)
        scores = jnp.where(mask[:, None, :, :], scores, -1000000000.0)
        attn = jax.nn.softmax(scores, axis=-1)
        x = jnp.einsum('bhqk,bhkd->bhqd', attn, v)
        x = x.transpose(0, 2, 1, 3).reshape(B, -1, H)
        return jnp.einsum('bsh,oh->bso', x, wo) + bo

    def _L0_ffn_ref(x, router_w, w1, w2):
        import jax, jax.numpy as jnp
        import numpy as np
        NUM_EXPERTS = 8
        TOP_K = 2
        CAP_RATIO = 1.25
        INIT_STD = 0.02
        B, T, H = x.shape
        E, K = (NUM_EXPERTS, TOP_K)
        xf = x.reshape(-1, H)
        N = xf.shape[0]
        P = N * K
        capacity = int(CAP_RATio * N * K / E) + 1 if False else int(CAP_RATIO * N * K / E) + 1
        logits = xf @ router_w.T
        probs = jax.nn.softmax(logits, axis=-1)
        k_probs, k_idx = jax.lax.top_k(probs, K)
        k_probs = k_probs / jnp.sum(k_probs, axis=-1, keepdims=True)
        flat_e = k_idx.reshape(-1)
        onehot = jax.nn.one_hot(flat_e, E, dtype=jnp.int32)
        rank = jnp.take_along_axis(jnp.cumsum(onehot, axis=0) - 1, flat_e[:, None], axis=1)[:, 0]
        keep = rank < capacity
        slot = jnp.minimum(rank, capacity - 1)
        token_id = jnp.arange(P) // K
        dispatched = jnp.where(keep[:, None], xf[token_id], 0.0)
        buf = jnp.zeros((E, capacity, H), x.dtype).at[flat_e, slot].add(dispatched)
        h = jax.nn.silu(jnp.einsum('ech,ehf->ecf', buf, w1))
        out_buf = jnp.einsum('ecf,efh->ech', h, w2)
        pair_out = out_buf[flat_e, slot] * keep[:, None].astype(x.dtype)
        combined = jnp.sum(pair_out.reshape(N, K, H) * k_probs[..., None], axis=1)
        return combined.reshape(B, T, H) + x

    def _L1_attn_ref(embeddings, W_Q, W_K, W_V):
        import jax, jax.numpy as jnp
        import numpy as np
        B, S, D = (4, 256, 128)

        def _xavier(key, shape):
            bound = float(np.sqrt(6.0 / (shape[0] + shape[1])))
            return jax.random.uniform(key, shape, dtype=jnp.float32, minval=-bound, maxval=bound)
        _, seq_len, d = embeddings.shape
        Q = embeddings @ W_Q
        K = embeddings @ W_K
        V = embeddings @ W_V
        scale = 1.0 / jnp.sqrt(jnp.float32(d))
        scores = jnp.einsum('bqd,bkd->bqk', Q, K) * scale
        causal = jnp.tril(jnp.ones((seq_len, seq_len), dtype=bool))
        scores = jnp.where(causal[None, :, :], scores, -jnp.inf)
        probs = jax.nn.softmax(scores, axis=-1)
        return jnp.einsum('bqk,bkd->bqd', probs, V)

    def _L1_xattn_ref(q, k, v, igate_w, igate_b, fgate_w, fgate_b, out_w):
        import jax, jax.numpy as jnp
        import numpy as np
        B, S, E, NH = (1, 256, 128, 8)
        DH = E // NH
        EPS = 1e-06
        LN_EPS = 1e-05
        Bq, Sq, Eq = q.shape
        nh = igate_b.shape[0]
        dh = Eq // nh
        gi = jnp.concatenate([q, k, v], axis=-1)
        ig = (gi @ igate_w.T + igate_b).transpose(0, 2, 1)
        fg = (gi @ fgate_w.T + fgate_b).transpose(0, 2, 1)
        qh = q.reshape(Bq, Sq, nh, dh).transpose(0, 2, 1, 3)
        kh = k.reshape(Bq, Sq, nh, dh).transpose(0, 2, 1, 3)
        vh = v.reshape(Bq, Sq, nh, dh).transpose(0, 2, 1, 3)
        log_f = jax.nn.log_sigmoid(fg)
        cs = jnp.cumsum(log_f, axis=-1)
        diff = cs[..., :, None] - cs[..., None, :]
        mask = jnp.tril(jnp.ones((Sq, Sq), dtype=bool))
        log_fg_mat = jnp.where(mask, diff, -jnp.inf)
        log_D = log_fg_mat + ig[..., None, :]
        max_log_D = jnp.max(log_D, axis=-1, keepdims=True)
        D = jnp.exp(log_D - max_log_D)
        qk = jnp.einsum('bhsd,bhtd->bhst', qh, kh) / jnp.sqrt(jnp.float32(dh))
        C = qk * D
        normalizer = jnp.maximum(jnp.abs(C.sum(-1, keepdims=True)), jnp.exp(-max_log_D))
        h = jnp.einsum('bhst,bhtd->bhsd', C / (normalizer + EPS), vh)
        mean = h.mean(-1, keepdims=True)
        var = ((h - mean) ** 2).mean(-1, keepdims=True)
        hn = (h - mean) / jnp.sqrt(var + LN_EPS)
        hn = hn * out_w.reshape(nh, dh)[None, :, None, :]
        return hn.transpose(0, 2, 1, 3).reshape(Bq, Sq, Eq)

    def _L1_ffn_ref(x, gate_w, gate_b, expert_w, expert_b):
        import jax, jax.numpy as jnp
        import numpy as np
        NEG_INF = -1e+30
        K = 2
        pooled = x.mean(axis=1)
        logits = pooled @ gate_w.T + gate_b
        topk_vals, _ = jax.lax.top_k(logits, K)
        min_topk = topk_vals[:, -1:]
        masked = jnp.where(logits < min_topk, -jnp.inf, logits)
        gates = jax.nn.softmax(masked, axis=-1)
        expert_out = jax.nn.gelu(jnp.einsum('bsd,eod->beso', x, expert_w) + expert_b[None, :, None, :], approximate=False)
        return jnp.einsum('be,beso->bso', gates, expert_out)
    x = _layernorm(x + _L0_attn_ref(x, L0_attn_mem, L0_attn_wq, L0_attn_wk, L0_attn_wv, L0_attn_wo, L0_attn_w1, L0_attn_b1, L0_attn_w2, L0_attn_b2, L0_attn_lin1, L0_attn_lin2, L0_attn_alpha, L0_attn_theta), axis=-1)
    x = _layernorm(x + _L0_xattn_ref(x, ctx_1024, ctx_1024, mask_BxSxS2_bf1, L0_xattn_wq, L0_xattn_bq, L0_xattn_wk, L0_xattn_bk, L0_xattn_wv, L0_xattn_bv, L0_xattn_wo, L0_xattn_bo), axis=-1)
    x = _layernorm(x + _L0_ffn_ref(x, L0_ffn_router_w, L0_ffn_w1, L0_ffn_w2), axis=-1)
    x = _layernorm(x + _L1_attn_ref(x, L1_attn_W_Q, L1_attn_W_K, L1_attn_W_V), axis=-1)
    x = _layernorm(x + _L1_xattn_ref(x, ctx_1024, ctx_1024, L1_xattn_igate_w, L1_xattn_igate_b, L1_xattn_fgate_w, L1_xattn_fgate_b, L1_xattn_out_w), axis=-1)
    x = _layernorm(x + _L1_ffn_ref(x, L1_ffn_gate_w, L1_ffn_gate_b, L1_ffn_expert_w, L1_ffn_expert_b), axis=-1)
    return x

_drawn_inputs = setup_inputs


def setup_inputs(seed=0):
    import zlib

    import numpy as np

    out = dict(_drawn_inputs(seed))
    spreads = {'L0_attn_b1': (0.0, 0.351),
     'L0_attn_b2': (0.0, 0.275),
     'L0_xattn_bq': (0.0, 0.267),
     'L0_xattn_bk': (0.0, 2.0),
     'L0_xattn_bv': (0.0, 0.1),
     'L0_xattn_bo': (0.0, 0.1),
     'L1_ffn_gate_b': (0.0, 0.482),
     'L1_ffn_expert_b': (0.0, 0.1)}
    factors = {'L0_attn_mem': 8.0,
     'L0_attn_wq': 8.0,
     'L0_attn_wk': 8.0,
     'L0_attn_wv': 8.0,
     'L0_attn_wo': 8.0,
     'L0_attn_lin1': 8.0,
     'L0_attn_lin2': 8.0,
     'L0_ffn_router_w': 12.391,
     'L1_xattn_igate_b': 64.0,
     'L0_ffn_w2': 3.694,
     'L1_attn_W_Q': 2.671}
    for name, (base, spread) in spreads.items():
        noise = np.random.default_rng([zlib.crc32(name.encode()), seed]).standard_normal(out[name].shape)
        drawn = base * np.exp(spread * noise) if base else spread * noise
        out[name] = jnp.asarray(drawn.astype(out[name].dtype))
    for name, factor in factors.items():
        out[name] = (out[name] * factor).astype(out[name].dtype)
    return out
```

```python
from contextlib import ExitStack

import concourse.bass as bass
from concourse import mybir

F32 = mybir.dt.float32
BF16 = mybir.dt.bfloat16
U8 = mybir.dt.uint8
U32 = mybir.dt.uint32
ALU = mybir.AluOpType
ACT = mybir.ActivationFunctionType
AX = mybir.AxisListType

P = 128
B, S, D = 8, 256, 128
NB = 2
STEPS = B // NB
T = NB * S
NC = T // P
QC = S // P
M = 64
KW = M + S
HID = 512
FC = HID // P
H0, DH0 = 4, 32
WIN = 64
KB = P + WIN
H1, DH1 = 16, 8
E = 8
CAP = int(1.25 * B * S * 2 / E) + 1
H2, DH2 = 8, 16
EPS = 1e-5
NEG = -float(2 ** 100)
TERMS = [(0, 0), (0, 1), (0, 2), (1, 0), (1, 1), (2, 0)]


class Signal:

    def __init__(self, sem, per=1, primed=0):
        self.sem, self.per, self.primed = sem, per, primed

    def at(self, step, n=None):
        return self.sem, step * self.per + (self.per if n is None else n) + self.primed

    def before(self, step):
        return self.sem, step * self.per + self.primed

    def prime(self, eng):
        eng.sem_inc(self.sem, self.primed)


def wait_apart(eng, passed, sem, value):
    eng.wait_ge(sem, value)
    eng.sem_inc(passed.sem, 1)


class Chain:

    def __init__(self, eng, links, step):
        self.eng, self.links, self.step, self.n = eng, links, step, 0

    def link(self, ins, apart=None):
        self.n += 1
        ins.then_inc(self.links.sem, 1)
        if apart:
            wait_apart(self.eng, apart, *self.links.at(self.step, self.n))
        else:
            self.eng.wait_ge(*self.links.at(self.step, self.n))

    def close(self):
        assert self.n == self.links.per, (self.links.sem, self.n)


def decoder_kernel(nc, a, out, parts_dram):
    with ExitStack() as ctx:
        def sb(name, shape, dt=F32, scope=ctx):
            return scope.enter_context(nc.sbuf_tensor(name, shape, dt))

        def signal(name, per=1, primed=0):
            return Signal(ctx.enter_context(nc.semaphore(name)), per, primed)

        bank = [ctx.enter_context(nc.psum_tensor(f"bank{i}", [P, 512], F32)) for i in range(8)]

        square = ["L0_attn_wqT", "L0_attn_wkT", "L0_attn_wvT", "L0_attn_woT", "L0_attn_lin1T", "L0_attn_lin2T",
                  "L0_xattn_wqT", "L0_xattn_wkT", "L0_xattn_wvT", "L0_xattn_woT",
                  "L1_attn_W_Q", "L1_attn_W_K", "L1_attn_W_V"]
        w = {n: sb("w_" + n, [P, P]) for n in square}
        w1T = sb("w1T", [P, HID])
        w2 = sb("w2", [P, HID])
        w2T = sb("w2T", [P, FC, P])
        w1T_new = sb("w1T_new", [P, HID])
        w2T_new = sb("w2T_new", [P, FC, P])
        b1 = sb("b1", [P, FC])
        b1_new = sb("b1_new", [P, FC])
        b2 = sb("b2", [P, 1])
        b2_new = sb("b2_new", [P, 1])
        b1_rows = sb("b1_rows", [P, HID])
        rate = sb("rate", [P, 4])
        router = sb("router", [P, E])
        moe_w1 = sb("moe_w1", [P, E, HID])
        moe_w2 = sb("moe_w2", [P, E, FC, P])
        x_bq = sb("x_bq", [P, 1])
        x_bk = sb("x_bk", [P, 1])
        x_bv_rows = sb("x_bv_rows", [P, P])
        x_bo_rows = sb("x_bo_rows", [P, P])
        gates_w = sb("gates_w", [P, 3, 40])
        gates_b = sb("gates_b", [40, 1])
        out_w_rows = sb("out_w_rows", [P, P])
        ffn_gw = sb("ffn_gw", [P, E])
        ffn_gb_rows = sb("ffn_gb_rows", [P, E])
        ffn_w = sb("ffn_w", [P, E * P])
        ffn_b = sb("ffn_b", [1, E * P])
        ident = sb("ident", [P, P])
        ident_b = sb("ident_b", [P, P], BF16)
        ones = sb("ones", [P, P])
        ones_b = sb("ones_b", [P, P], BF16)
        before_b = sb("before_b", [P, P], BF16)
        future_b = sb("future_b", [P, P], BF16)
        past_b = sb("past_b", [P, P], BF16)
        window = sb("window", [P, KB])
        mem_mask = sb("mem_mask", [M, M])
        head_sel = sb("head_sel", [96, H1, P], BF16)
        row_sel = sb("row_sel", [96, P], BF16)
        iota_e = sb("iota_e", [P, E])
        minus_half = sb("minus_half", [P, 32])
        vT_all = sb("vT_all", [P, STEPS * T])
        hT = sb("hT", [P, FC, T + M])

        load_w = signal("load_w", 16)
        passed = signal("passed")
        const_ready = signal("const_ready")
        pool_zero = signal("pool_zero", 14)
        dve_pro = signal("dve_pro", 3)

        x_loaded = signal("x_loaded", 32)
        mem_qk = signal("mem_qk")
        mem_q_done = signal("mem_q_done")
        mem_k_done = signal("mem_k_done")
        qkv_ready = signal("qkv_ready")
        q_copied = signal("q_copied", 1)
        v_copied = signal("v_copied", 6)
        k_copied = signal("k_copied", H0)
        NU = NB * QC + 1
        scores_a = signal("scores_a", NU)
        max_a = signal("max_a", NU)
        exp_a = signal("exp_a", NU)
        norm_a = signal("norm_a", NU)
        pT_a = signal("pT_a", NU)
        pTa_copied = signal("pTa_copied", NU)
        pTb_copied = signal("pTb_copied", NU)
        pv_a = signal("pv_a", NU)
        oT_copied = signal("oT_copied", 2)
        swa_ready = signal("swa_ready", 2)
        vT_copied = signal("vT_copied", 2)
        zT_a = signal("zT_a", FC + 1)
        hT_a = signal("hT_a", 2 * FC)
        pred_a = signal("pred_a", 1)
        e_ready = signal("e_ready", 1)
        eT_tr = signal("eT_tr", 1)
        etok_copied = signal("etok_copied", 2)
        zd_ready = signal("zd_ready", NC + 1)
        z_biased = signal("z_biased", NC + 1)
        sg_ready = signal("sg_ready", NC + 1)
        h_ready = signal("h_ready", NC + 1)
        slope_ready = signal("slope_ready", NC + 1)
        dz_ready = signal("dz_ready", NC + 1)
        bias_summed = signal("bias_summed", NC + 1, primed=1)
        grads_ready = signal("grads_ready", NC + 1, primed=1)
        grads_added = signal("grads_added", 1, primed=1)
        dve_a = signal("dve_a", 2 * NU + 1)
        act_a = signal("act_a", NC + 1)
        pool_a = signal("pool_a", 2 * (NC + 1))
        upd_pe = signal("upd_pe")
        upd_dve = signal("upd_dve")
        updated = signal("updated")

        q_stack = sb("q_stack", [P, H1 // 2, T], BF16)
        k_stack = sb("k_stack", [P, H1 // 2, 2, T], BF16)
        v_aug = sb("v_aug", [P, NC, H1, 32])
        neg_max = sb("neg_max", [96, S], BF16)
        seen = sb("seen", [P, E])
        kpad2 = sb("kpad2", [P, H2, T])
        v2_aug = sb("v2_aug", [P, NC, H2, 32])
        ones8 = sb("ones8", [8, S])
        neg_pm = sb("neg_pm", [96, T], BF16)
        fb_parts = sb("fb_parts", [96, E * P], BF16)

        b_x_loaded = signal("b_x_loaded", 32)
        b_ctx_loaded = signal("b_ctx_loaded", 64 + 16 * H2)
        x_in_used = signal("x_in_used", primed=1)
        ctx_used = signal("ctx_used", primed=1)
        zT_b = signal("zT_b", FC)
        hT_b = signal("hT_b", FC)
        out_mem = signal("out_mem")
        memT_ready = signal("memT_ready")
        lin1 = signal("lin1")
        lin_ready = signal("lin_ready")
        g_ready = signal("g_ready", 2)
        merged = signal("merged")
        merged_tr = signal("merged_tr")
        LN = 6
        var_ready = signal("var_ready", LN)
        rstd_ready = signal("rstd_ready", LN)
        x_norm = signal("x_norm", LN)
        x_tr = signal("x_tr", LN - 1)
        xt_ready = signal("xt_ready", LN - 1)
        masks_ready = signal("masks_ready")
        qk_b = signal("qk_b")
        q_b = signal("q_b")
        v_b = signal("v_b")
        kf_ready = signal("kf_ready")
        kh_ready = signal("kh_ready")
        k_parts_ready = signal("k_parts_ready")
        q_parts_ready = signal("q_parts_ready")
        parts_saved = signal("parts_saved", 32)
        q_stacked = signal("q_stacked", 16 * 12)
        k_stacked = signal("k_stacked", 16 * 12)
        v_aug_ready = signal("v_aug_ready")
        XU = NB * H1
        s_ready = signal("s_ready", XU)
        s_read = signal("s_read", XU)
        mx_tr = signal("mx_tr", NB)
        neg_max_ready = signal("neg_max_ready", NB)
        sT_ready = signal("sT_ready", XU)
        exp_ready = signal("exp_ready", XU)
        G = 4
        pv_ready = signal("pv_ready", NB * G)
        o_copied = signal("o_copied", NB * 2)
        o_tr = signal("o_tr", NB)
        o_tok_ready = signal("o_tok_ready", NB)
        o_tok_tr = signal("o_tok_tr")
        o_T_ready = signal("o_T_ready")
        wo_ready = signal("wo_ready")
        x_plus = signal("x_plus")
        r_scored = signal("r_scored")
        share_diff = signal("share_diff")
        share_exp = signal("share_exp")
        picked = signal("picked")
        ranks = signal("ranks")
        gates_ready = signal("gates_ready")
        x_twice = signal("x_twice")
        up_ready = signal("up_ready", E * FC)
        he_ready = signal("he_ready", E * FC)
        down_ready = signal("down_ready", E)
        down_added = signal("down_added", E)
        qkv_c = signal("qkv_c")
        aq_ready = signal("aq_ready", 2)
        ak_ready = signal("ak_ready")
        as_ready = signal("as_ready", NB)
        amax_ready = signal("amax_ready", NB)
        aexp_ready = signal("aexp_ready", NB)
        apT_ready = signal("apT_ready", NB)
        apT_copied = signal("apT_copied", NB)
        apv_ready = signal("apv_ready")
        pre_ready = signal("pre_ready")
        abs_ready = signal("abs_ready")
        ef_ready = signal("ef_ready")
        ln_ready = signal("ln_ready")
        pm_ready = signal("pm_ready")
        neg_pm_ready = signal("neg_pm_ready")
        cols_ready = signal("cols_ready")
        cols_copied = signal("cols_copied", 2)
        v2_ready = signal("v2_ready")
        MU = NB * H2
        eu_ready = signal("eu_ready", MU)
        decay_ready = signal("decay_ready", MU)
        c_ready = signal("c_ready", MU)
        pv2_ready = signal("pv2_ready", NB * 2)
        o5_copied = signal("o5_copied", NB)
        o5_tr = signal("o5_tr")
        var2_ready = signal("var2_ready")
        rstd2_ready = signal("rstd2_ready")
        rep_ready = signal("rep_ready")
        fl_ready = signal("fl_ready")
        fmax_ready = signal("fmax_ready")
        fe_ready = signal("fe_ready")
        FU = NC * 2
        f_ready = signal("f_ready", FU)
        f_act = signal("f_act", FU)
        f_added = signal("f_added", FU, primed=1)
        out_saved = signal("out_saved", 16, primed=16)
        fb_ready = signal("fb_ready")
        dve_b = signal("dve_b", 92)
        pool_b = signal("pool_b", 2)

        scope_a = ExitStack()
        xin = sb("xin", [P, NB, KW], scope=scope_a)
        xtok = sb("xtok", [P, NC + 1, P], scope=scope_a)
        qT_mem = sb("qT_mem", [P, M], scope=scope_a)
        kpad = sb("kpad", [P, H0, NB, KW], scope=scope_a)
        stats = sb("stats", [P, 2, 16], scope=scope_a)
        oT = sb("oT", [P, T + M], scope=scope_a)
        vT_mem = sb("vT_mem", [P, M], scope=scope_a)
        eT = sb("eT", [P, T + M], scope=scope_a)
        etok = sb("etok", [P, NC + 1, P], scope=scope_a)
        grad1 = sb("grad1", [P, HID], scope=scope_a)
        grad2 = sb("grad2", [P, HID], scope=scope_a)
        dz_sum = sb("dz_sum", [P, HID], scope=scope_a)
        e_sum = sb("e_sum", [P, P], scope=scope_a)
        stage = ExitStack()
        qT = sb("qT", [P, T], scope=stage)
        vtok = sb("vtok", [P, NB, 3, P], scope=stage)
        probs = sb("probs", [P, 2, H0, KB], scope=stage)
        probsT_a = sb("probsT_a", [P, 2, H0 * P], scope=stage)
        probsT_b = sb("probsT_b", [WIN, 2, H0 * P], scope=stage)
        stage.close()
        stage = ExitStack()
        zt = sb("zt", [P, 2, HID], scope=stage)
        sg = sb("sg", [P, 2, HID], scope=stage)
        ht = sb("ht", [P, 2, HID], scope=stage)
        sl = sb("sl", [P, 2, HID], scope=stage)
        dz = sb("dz", [P, 2, HID], scope=stage)
        stage.close()
        scope_a.close()
        scope_b = ExitStack()
        x_in = sb("x_in", [P, NC, P], scope=scope_b)
        xT_in = sb("xT_in", [P, T], scope=scope_b)
        X = sb("X", [P, NC, P], scope=scope_b)
        XT = sb("XT", [P, T], scope=scope_b)
        Y = sb("Y", [P, NC, P], scope=scope_b)
        R = sb("R", [P, NC, P], scope=scope_b)
        bn = sb("bn", [P, NC, 6], scope=scope_b)
        mv = sb("mv", [P, NC, 2], scope=scope_b)
        var_eps = sb("var_eps", [P, NC], scope=scope_b)
        rstd = sb("rstd", [P, NC], scope=scope_b)
        ctxT = sb("ctxT", [P, T], scope=scope_b)
        ctx_tok = sb("ctx_tok", [P, NC, P], scope=scope_b)
        mask_q = sb("mask_q", [P, NC, S], U8, scope=scope_b)
        mask_k = sb("mask_k", [P, NC, S], U8, scope=scope_b)
        add_q = sb("add_q", [P, NC, S], scope=scope_b)
        add_k = sb("add_k", [P, NC, S], BF16, scope=scope_b)
        q_parts = sb("q_parts", [P, 3, T], BF16, scope=scope_b)
        k_parts = sb("k_parts", [P, 3, T], BF16, scope=scope_b)
        rec = sb("rec", [P, QC, H1], scope=scope_b)
        o_tok = sb("o_tok", [P, NC, P], scope=scope_b)
        logits = sb("logits", [P, NC, E], scope=scope_b)
        top = sb("top", [P, NC, 8], scope=scope_b)
        top_i = sb("top_i", [P, NC, 8], U32, scope=scope_b)
        top_f = sb("top_f", [P, NC, 2], scope=scope_b)
        pick = sb("pick", [P, 2, NC, E], scope=scope_b)
        picked_b = sb("picked_b", [P, NC, E], BF16, scope=scope_b)
        share = sb("share", [P, 4, NC], scope=scope_b)
        rank = sb("rank", [P, NC, E], scope=scope_b)
        gate = sb("gate", [P, NC, E], scope=scope_b)
        pooled = sb("pooled", [P, NB], scope=scope_b)
        pooled_rep = sb("pooled_rep", [P, NB, P], scope=scope_b)
        fl = sb("fl", [P, NB, E], scope=scope_b)
        ftop = sb("ftop", [P, NB, 8], scope=scope_b)
        fe = sb("fe", [P, NB, E], scope=scope_b)
        fs = sb("fs", [P, 2, NB], scope=scope_b)
        fgate = sb("fgate", [P, NB, E], scope=scope_b)
        stage = ExitStack()
        memT = sb("memT", [P, T], scope=stage)
        g1 = sb("g1", [P, T], scope=stage)
        g2 = sb("g2", [P, T], scope=stage)
        qr = sb("qr", [P, T], scope=stage)
        qf, kf, kr, o_T = g1, memT, g2, g2
        mx = sb("mx", [P, QC, H1], scope=stage)
        neg_r = sb("neg_r", [16, S], scope=stage)
        neg_m = sb("neg_m", [16, S], BF16, scope=stage)
        pT = sb("pT", [P, 2, 4, QC, S], scope=stage)
        o_heads = sb("o_heads", [P, 4, S], scope=stage)
        stage.close()
        stage = ExitStack()
        he = sb("he", [P, 2, FC, T], scope=stage)
        stage.close()
        stage = ExitStack()
        aq = sb("aq", [P, T], scope=stage)
        ak = sb("ak", [P, T], scope=stage)
        av = sb("av", [P, NC, P], scope=stage)
        ap = sb("ap", [P, NB, 3, P], scope=stage)
        apT = sb("apT", [P, NB, 3 * P], scope=stage)
        ast = sb("ast", [P, 4, NC], scope=stage)
        stage.close()
        stage = ExitStack()
        gi = sb("gi", [8, T], scope=stage)
        gf = sb("gf", [8, T], scope=stage)
        gl = sb("gl", [8, T], scope=stage)
        cs = sb("cs", [8, T], scope=stage)
        ga = sb("ga", [8, T], scope=stage)
        pm = sb("pm", [8, T], scope=stage)
        gm = sb("gm", [8, T], scope=stage)
        pb2 = sb("pb2", [8, T], BF16, scope=stage)
        a_col = sb("a_col", [P, NC, H2], scope=stage)
        em_col = sb("em_col", [P, NC, H2], scope=stage)
        decay = sb("decay", [P, 2, S + P], scope=stage)
        cT = sb("cT", [P, 2, 4, S + P], scope=stage)
        o5 = add_q[:].rearrange("p (b g) s -> p b g s", b=NB)
        den = sb("den", [P, NC, H2], scope=stage)
        hh = o_tok[:].rearrange("p c (h d) -> p c h d", d=DH2)
        hm = sb("hm", [P, 3, NC * H2], scope=stage)
        hrs = sb("hrs", [P, NC * H2], scope=stage)
        gl_act = cT[:].rearrange("p g j s -> p (g j s)")[:, 0:1024].rearrange("p (n f) -> p n f", n=2)
        stage.close()
        stage = ExitStack()
        fb_row = sb("fb_row", [1, 1, E * P], scope=stage)
        fb_m = sb("fb_m", [1, E * P], BF16, scope=stage)
        stage.close()
        scope_b.close()

        block = ctx.enter_context(nc.Block())
        units = [(b, c) for b in range(NB) for c in range(QC)] + [(0, None)]

        def s_banks(u):
            return (bank[5], bank[6]) if u % 2 == 0 else (bank[0], bank[2])

        def zd_banks(c):
            return (bank[5], bank[6]) if c % 2 == 0 else (bank[4], bank[2])

        loads_w = [(w[n][:], a[n]) for n in square] + [
            (w1T[:], a["L0_attn_w1T"]), (w2[:], a["L0_attn_w2"]),
            (w2T[:], a["L0_attn_w2T"].rearrange("(k p) d -> p k d", p=P)),
            (b1[:], a["L0_attn_b1_cols"]),
            (b2[:], a["L0_attn_b2"].unsqueeze(1)),
            (b1_rows[:], a["L0_attn_b1"].partition_broadcast(P)),
            (rate[:, 0:1], a["L0_attn_alpha"].partition_broadcast(P)),
            (rate[:, 1:2], a["L0_attn_theta"].partition_broadcast(P)),
            (xtok[0:M, NC, :], a["L0_attn_mem"]),
            (xin[:, 0, 0:M], a["L0_attn_memT"]),
            (xin[:, 1, 0:M], a["L0_attn_memT"]),
        ]
        late_w = [
            (router[:], a["L0_ffn_router_wT"]),
            (moe_w1[:], a["L0_ffn_w1"].rearrange("e d f -> d e f")),
            (moe_w2[:], a["L0_ffn_w2"].rearrange("e (k p) d -> p e k d", p=P)),
            (x_bq[:], a["L0_xattn_bq"].unsqueeze(1)), (x_bk[:], a["L0_xattn_bk"].unsqueeze(1)),
            (x_bv_rows[:], a["L0_xattn_bv"].partition_broadcast(P)),
            (x_bo_rows[:], a["L0_xattn_bo"].partition_broadcast(P)),
            (gates_b[0:8, :], a["L1_xattn_igate_b"].unsqueeze(1)),
            (gates_b[32:40, :], a["L1_xattn_fgate_b"].unsqueeze(1)),
            (out_w_rows[:], a["L1_xattn_out_w"].partition_broadcast(P)),
            (ffn_gw[:], a["L1_ffn_gate_wT"]),
            (ffn_gb_rows[:], a["L1_ffn_gate_b"].partition_broadcast(P)),
            (ffn_w[:], a["L1_ffn_expert_wT"]),
            (ffn_b[:], a["L1_ffn_expert_b"].rearrange("e o -> (e o)").unsqueeze(0)),
            (gates_w[:, :, 0:8], a["L1_xattn_igate_wT"].rearrange("(j p) e -> p j e", p=P)),
            (gates_w[:, :, 32:40], a["L1_xattn_fgate_wT"].rearrange("(j p) e -> p j e", p=P)),
        ]
        late_loaded = signal("late_loaded")

        @block.sync
        def _(sp):
            out_saved.prime(sp)
            for dst, src in loads_w:
                sp.dma_start(dst, src).then_inc(load_w.sem, 16)
            with sp.Fori(0, STEPS) as i:
                sp.wait_ge(*grads_ready.before(i))
                sp.dma_start(xin[:, :, M:KW], a["xT"][:, bass.ds(i * T, T)].rearrange("d (b t) -> d b t", b=NB)).then_inc(x_loaded.sem, 16)
                sp.dma_start(xtok[:, 0:NC, :], a["x"].rearrange("b s d -> (b s) d")[bass.ds(i * T, T), :].rearrange("(c p) d -> p c d", p=P)).then_inc(x_loaded.sem, 16)
            sp.wait_ge(*updated.at(0))
            with sp.Fori(0, STEPS) as i:
                rows = bass.ds(i * T, T)
                sp.wait_ge(*x_in_used.before(i))
                sp.dma_start(xT_in[:], a["xT"][:, rows]).then_inc(b_x_loaded.sem, 16)
                sp.dma_start(x_in[:], a["x"].rearrange("b s d -> (b s) d")[rows, :].rearrange("(c p) d -> p c d", p=P)).then_inc(b_x_loaded.sem, 16)
                sp.wait_ge(*ctx_used.before(i))
                sp.dma_start(ctxT[:], a["ctxT"][:, rows]).then_inc(b_ctx_loaded.sem, 16)
                sp.dma_start(ctx_tok[:], a["ctx_1024"].rearrange("b s d -> (b s) d")[rows, :].rearrange("(c p) d -> p c d", p=P)).then_inc(b_ctx_loaded.sem, 16)
                sp.dma_start(mask_q[:], a["mask_BxSxS2_bf1"].rearrange("b q k -> (b q) k")[rows, :].rearrange("(c p) k -> p c k", p=P)).then_inc(b_ctx_loaded.sem, 16)
                sp.dma_start(mask_k[:], a["maskT"].rearrange("b k q -> (b k) q")[rows, :].rearrange("(c p) q -> p c q", p=P)).then_inc(b_ctx_loaded.sem, 16)
                for h in range(H2):
                    r = slice(DH2 * h, DH2 * h + DH2)
                    sp.dma_start(kpad2[r, h, :], a["ctxT"][r, rows]).then_inc(b_ctx_loaded.sem, 16)
                for n, (ready, parts, stacked) in enumerate([(k_parts_ready, k_parts, k_stacked), (q_parts_ready, q_parts, q_stacked)]):
                    sp.wait_ge(*ready.at(i))
                    sp.dma_start(parts_dram[n].rearrange("j d t -> d j t"), parts[:]).then_inc(parts_saved.sem, 16)
                    sp.wait_ge(*parts_saved.at(i, 16 * (n + 1)))
                    for s in range(2):
                        for r, term in enumerate(TERMS):
                            src = parts_dram[n, term[1 - n]].rearrange("(p s d) t -> s d p t", s=2, d=DH1)[s]
                            dst = slice(64 * s + DH1 * r, 64 * s + DH1 * (r + 1))
                            sp.dma_start(k_stack[dst, :, s, :] if n == 0 else q_stack[dst, :, :], src).then_inc(stacked.sem, 16)
                sp.wait_ge(*x_norm.at(i))
                sp.dma_start(out.rearrange("b s d -> (b s) d")[rows, :].rearrange("(c p) d -> p c d", p=P), Y[:]).then_inc(out_saved.sem, 16)
            sp.wait_ge(*out_saved.before(STEPS))

        @block.gpsimd
        def _(pool):
            bias_summed.prime(pool)
            for t in (ones, dz_sum, e_sum, grad1, grad2):
                pool.memset(t[:], 1.0 if t is ones else 0.0)
            pool.memset(gates_w[:], 0.0)
            pool.memset(kpad[:], 0.0)
            pool.memset(ident[:], 0.0)
            pool.memset(future_b[:], 0.0)
            pool.memset(past_b[:], 0.0)
            pool.memset(before_b[:], 1.0)
            pool.memset(window[:], 0.0)
            pool.memset(mem_mask[:], 0.0)
            pool.memset(head_sel[:], 0.0)
            pool.memset(row_sel[:], 0.0)
            pool.memset(minus_half[:], -0.5)
            pool.iota(iota_e[:], pattern=[[1, E]], base=0, channel_multiplier=0, allow_small_or_imprecise_dtypes=True)
            for t in (q_stack, k_stack, neg_max, neg_pm, kpad2, v_aug, v2_aug, seen, fb_parts):
                pool.memset(t[:], 0.0)
            pool.memset(ones8[:], 1.0)
            made = Chain(pool, pool_zero, 0)
            made.link(pool.memset(ones_b[:], 1.0))
            pool.memset(v_aug[:, :, :, DH1:DH1 + 1], 1.0)
            pool.memset(v2_aug[:, :, :, DH2:DH2 + 1], float(DH2) ** -0.5)
            for dst, src in late_w:
                pool.dma_start(dst, src).then_inc(late_loaded.sem, 16)

            def select(tile, op, fill, base, pattern, channel):
                made.link(pool.affine_select(out=tile, in_=tile, compare_op=op, fill=fill, base=base,
                                             pattern=pattern, channel_multiplier=channel))

            select(ident[:], ALU.not_equal, 1.0, 0, [[-1, P]], 1)
            select(future_b[:], ALU.is_ge, NEG, 0, [[-1, P]], 1)
            select(past_b[:], ALU.is_ge, NEG, 0, [[1, P]], -1)
            select(before_b[:], ALU.is_gt, 0.0, 0, [[1, P]], -1)
            select(mem_mask[:], ALU.is_ge, NEG, 0, [[-1, M]], 1)
            select(window[:], ALU.is_gt, NEG, 0, [[1, KB]], -1)
            select(window[:], ALU.is_ge, NEG, WIN, [[-1, KB]], 1)
            for part in range(3):
                rows = slice(32 * part, 32 * part + H1)
                select(head_sel[rows], ALU.not_equal, 1.0, 0, [[-1, H1], [0, P]], 1)
                select(row_sel[32 * part:32 * part + 1], ALU.not_equal, 1.0, 0, [[0, P]], 1)
            made.close()
            pool.tensor_copy(ident_b[:], ident[:]).then_inc(const_ready.sem, 1)

            with pool.Fori(0, STEPS) as i:
                chain = Chain(pool, pool_a, i)
                for c in range(NC + 1):
                    n, s = (P if c < NC else M), c % 2
                    pool.wait_ge(*h_ready.at(i, c + 1))
                    chain.link(pool.tensor_tensor(sl[0:n, s], sg[0:n, s], ht[0:n, s], ALU.mult))
                    chain.link(pool.tensor_tensor(sl[0:n, s], sg[0:n, s], sl[0:n, s], ALU.subtract))
                    pool.tensor_tensor(sl[0:n, s], sl[0:n, s], ht[0:n, s], ALU.add).then_inc(slope_ready.sem, 1)
                    pool.wait_ge(*dz_ready.at(i, c + 1))
                    if c == 0:
                        pool.wait_ge(*etok_copied.at(i))
                    else:
                        pool.wait_ge(*bias_summed.at(i, c))
                    if c == 0:
                        pool.wait_ge(*bias_summed.before(i))
                    pool.tensor_tensor(e_sum[0:n], e_sum[0:n], etok[0:n, c, :], ALU.add)
                    pool.tensor_tensor(dz_sum[0:n], dz_sum[0:n], dz[0:n, s], ALU.add).then_inc(bias_summed.sem, 1)
                chain.close()
            with pool.Fori(0, STEPS) as i:
                def rsqrt(n):
                    pool.wait_ge(*var_ready.at(i, n))
                    pool.tensor_tensor(rstd[:], var_eps[:], minus_half[:, 0:NC], ALU.pow).then_inc(rstd_ready.sem, 1)

                wait_apart(pool, passed, *b_ctx_loaded.at(i))
                pool.tensor_scalar(add_q[:], mask_q[:], -1.0, -NEG, ALU.add, ALU.mult)
                pool.tensor_scalar(add_k[:], mask_k[:], -1.0, -NEG, ALU.add, ALU.mult).then_inc(masks_ready.sem, 1)
                rsqrt(1)
                pool.wait_ge(*kh_ready.at(i))
                pool_chain = Chain(pool, pool_b, i)
                pool_chain.link(pool.tensor_tensor(kr[:], kf[:], k_parts[:, 0, :], ALU.subtract), passed)
                pool_chain.link(pool.tensor_copy(k_parts[:, 1, :], kr[:]))
                pool.tensor_tensor(k_parts[:, 2, :], kr[:], k_parts[:, 1, :], ALU.subtract).then_inc(k_parts_ready.sem, 1)
                pool.wait_ge(*x_norm.at(i, 1))
                pool.tensor_tensor(R[:], X[:], x_bo_rows[:].unsqueeze(1).to_broadcast([P, NC, P]), ALU.add).then_inc(x_plus.sem, 1)
                rsqrt(2)
                pool.wait_ge(*x_norm.at(i, 2))
                pool.tensor_tensor(R[:], X[:], X[:], ALU.add).then_inc(x_twice.sem, 1)
                rsqrt(3)
                rsqrt(4)
                pool.tensor_scalar(v2_aug[:, :, :, 0:DH2], ctx_tok[:].rearrange("p c (h d) -> p c h d", h=H2), float(DH2) ** -0.5, None, ALU.mult).then_inc(v2_ready.sem, 1)
                pool.wait_ge(*var2_ready.at(i))
                pool.tensor_tensor(hrs[:], hm[:, 2, :], minus_half[:, 0:NC * H2], ALU.pow).then_inc(rstd2_ready.sem, 1)
                rsqrt(5)
                rsqrt(6)
                pool_chain.close()

        @block.tensor
        def _(pe):
            grads_ready.prime(pe)
            pe.wait_ge(load_w.sem, 16 * len(loads_w))
            pe.wait_ge(*const_ready.at(0))
            pe.matmul(bank[1][:, 0:M], w["L0_attn_wqT"][:], xin[:, 0, 0:M], start=True, stop=True)
            pe.matmul(bank[1][:, M:2 * M], w["L0_attn_wkT"][:], xin[:, 0, 0:M], start=True, stop=True).then_inc(mem_qk.sem, 1)
            pe.wait_ge(*mem_q_done.at(0))
            pe.wait_ge(*mem_k_done.at(0))
            with pe.Fori(0, STEPS) as i:
                pe.wait_ge(*x_loaded.at(i))
                pe.wait_ge(*grads_added.before(i))
                pe.wait_ge(*bias_summed.before(i))
                pe.matmul(bank[0][:], w["L0_attn_wqT"][:], xin[:, :, M:KW], start=True, stop=True)
                pe.matmul(bank[2][:], w["L0_attn_wkT"][:], xin[:, :, M:KW], start=True, stop=True)
                for b in range(NB):
                    for j, (k0, n) in enumerate([(0, P), (P, P), (2 * P, M)]):
                        last = pe.matmul(bank[3 + b][0:n, j * P:(j + 1) * P], xin[:, b, k0:k0 + n],
                                         w["L0_attn_wvT"][:], start=True, stop=True)
                last.then_inc(qkv_ready.sem, 1)
                pe.wait_ge(*q_copied.at(i))
                pe.wait_ge(*k_copied.at(i))

                def scores(u):
                    b, c = units[u]
                    if u >= 2:
                        pe.wait_ge(*max_a.at(i, u - 1))
                    for h in range(H0):
                        dst = s_banks(u)[h // 2]
                        col = (h % 2) * KB
                        if c is None:
                            last = pe.matmul(dst[0:M, col:col + M], qT_mem[:], kpad[:, h, 0, 0:M], start=True, stop=True)
                        else:
                            last = pe.matmul(dst[:, col:col + KB], qT[:, b * S + c * P:b * S + (c + 1) * P],
                                             kpad[:, h, b, c * P:c * P + KB], start=True, stop=True)
                    last.then_inc(scores_a.sem, 1)

                def transposes(u):
                    b, c = units[u]
                    if u == 0:
                        pe.wait_ge(*v_copied.at(i))
                    else:
                        pe.wait_ge(*pTa_copied.at(i, u))
                        pe.wait_ge(*pTb_copied.at(i, u))
                    wait_apart(pe, passed, *norm_a.at(i, u + 1))
                    s = u % 2
                    for h in range(H0):
                        if c is None:
                            last = pe.transpose(bank[3][0:M, h * P:h * P + M], probs[0:M, s, h, 0:M], ident[0:M, 0:M])
                        else:
                            pe.transpose(bank[3][:, h * P:(h + 1) * P], probs[:, s, h, 0:P], ident[:])
                            last = pe.transpose(bank[4][0:WIN, h * P:(h + 1) * P], probs[:, s, h, P:KB], ident[:])
                    last.then_inc(pT_a.sem, 1)

                def outputs(u):
                    b, c = units[u]
                    s = u % 2
                    pe.wait_ge(*pTb_copied.at(i, u + 1))
                    wait_apart(pe, passed, *pTa_copied.at(i, u + 1))
                    for h in range(H0):
                        r = slice(DH0 * h, DH0 * h + DH0)
                        if c is None:
                            last = pe.matmul(bank[1][r, 0:M], vtok[0:M, 0, 0, r], probsT_a[0:M, s, h * P:h * P + M], start=True, stop=True)
                        else:
                            dst = bank[7][r, (b * QC + c) * P:(b * QC + c + 1) * P]
                            pe.matmul(dst, vtok[:, b, c, r], probsT_a[:, s, h * P:(h + 1) * P], start=True, stop=False)
                            last = pe.matmul(dst, vtok[0:WIN, b, c + 1, r], probsT_b[:, s, h * P:(h + 1) * P], start=False, stop=True)
                    last.then_inc(pv_a.sem, 1)

                scores(0)
                scores(1)
                for u in range(NU):
                    transposes(u)
                    if u + 2 < NU:
                        scores(u + 2)
                    outputs(u)
                pe.wait_ge(*oT_copied.at(i))
                pe.wait_ge(*max_a.at(i))
                pe.matmul(bank[0][:], w["L0_attn_woT"][:], oT[:, 0:T], start=True, stop=True).then_inc(swa_ready.sem, 1)
                pe.matmul(bank[2][:, 0:M], w["L0_attn_woT"][:], oT[:, T:T + M], start=True, stop=True).then_inc(swa_ready.sem, 1)
                for k in range(FC):
                    if k >= 2:
                        pe.wait_ge(*hT_a.at(i, k - 1))
                    pe.matmul(bank[5 + k % 2][:], w1T[:, k * P:(k + 1) * P], xin[:, :, M:KW], start=True, stop=True).then_inc(zT_a.sem, 1)
                for k in range(FC):
                    last = pe.matmul(bank[1][:, M * (k + 1):M * (k + 2)], w1T[:, k * P:(k + 1) * P], xin[:, 0, 0:M], start=True, stop=True)
                last.then_inc(zT_a.sem, 1)
                pe.wait_ge(*hT_a.at(i))
                for k in range(FC):
                    pe.matmul(bank[3][:], w2T[:, k, :], hT[:, k, 0:T], start=(k == 0), stop=(k == FC - 1))
                for k in range(FC):
                    last = pe.matmul(bank[4][:, 0:M], w2T[:, k, :], hT[:, k, T:T + M], start=(k == 0), stop=(k == FC - 1))
                last.then_inc(pred_a.sem, 1)
                pe.wait_ge(*e_ready.at(i))
                for c in range(NC):
                    pe.transpose(bank[7][:, c * P:(c + 1) * P], eT[:, c * P:(c + 1) * P], ident[:])
                pe.transpose(bank[1][0:M, 0:P], eT[:, T:T + M], ident[:]).then_inc(eT_tr.sem, 1)
                pe.wait_ge(*vT_copied.at(i))
                pe.wait_ge(*etok_copied.at(i))

                def z_and_dh(c):
                    n = P if c < NC else M
                    zb, db = zd_banks(c)
                    if c >= 2:
                        pe.wait_ge(*dz_ready.at(i, c - 1))
                    x_c = xin[:, c // QC, M + (c % QC) * P:M + (c % QC + 1) * P] if c < NC else xin[:, 0, 0:M]
                    pe.matmul(zb[0:n], x_c, w1T[:], start=True, stop=True)
                    pe.matmul(db[0:n], eT[:, c * P:c * P + n], w2[:], start=True, stop=True).then_inc(zd_ready.sem, 1)

                z_and_dh(0)
                z_and_dh(1)
                for c in range(NC + 1):
                    n, s = (P if c < NC else M), c % 2
                    pe.wait_ge(*dz_ready.at(i, c + 1))
                    pe.matmul(bank[0][:], xtok[0:n, c, :], dz[0:n, s], start=(c == 0), stop=(c == NC))
                    pe.matmul(bank[3][:], etok[0:n, c, :], ht[0:n, s], start=(c == 0), stop=(c == NC)).then_inc(grads_ready.sem, 1)
                    if c + 2 <= NC:
                        z_and_dh(c + 2)
            pe.wait_ge(*grads_added.before(STEPS))
            pe.wait_ge(*bias_summed.before(STEPS))
            for k in range(FC):
                pe.matmul(bank[1][:, k:k + 1], dz_sum[:, k * P:(k + 1) * P], ones[:, 0:1], start=True, stop=True)
            pe.matmul(bank[1][:, FC:FC + 1], e_sum[:], ones[:, 0:1], start=True, stop=True)
            for k in range(FC):
                last = pe.transpose(bank[4][:, k * P:(k + 1) * P], grad2[:, k * P:(k + 1) * P], ident[:])
            last.then_inc(upd_pe.sem, 1)
            pe.wait_ge(*updated.at(0))
            pe.wait_ge(*fb_ready.at(0))
            pe.wait_ge(late_loaded.sem, 16 * len(late_w))
            with pe.Fori(0, STEPS) as i:
                def x_transpose(n):
                    pe.wait_ge(*x_norm.at(i, n))
                    for c in range(NC):
                        last = pe.transpose(bank[7][:, c * P:(c + 1) * P], X[:, c, :], ident[:])
                    last.then_inc(x_tr.sem, 1)
                    pe.wait_ge(*xt_ready.at(i, n))

                pe.wait_ge(*b_x_loaded.at(i))
                pe.wait_ge(*f_added.before(i))
                for k in range(FC):
                    pe.matmul(bank[4 + k][:], w1T_new[:, k * P:(k + 1) * P], xT_in[:], start=True, stop=True).then_inc(zT_b.sem, 1)
                for k in range(FC):
                    pe.wait_ge(*hT_b.at(i, k + 1))
                    last = pe.matmul(bank[2][:], w2T_new[:, k, :], hT[:, k, 0:T], start=(k == 0), stop=(k == FC - 1))
                last.then_inc(out_mem.sem, 1)
                pe.matmul(bank[3][:], w["L0_attn_lin1T"][:], vT_all[:, bass.ds(i * T, T)], start=True, stop=True).then_inc(lin1.sem, 1)
                pe.wait_ge(*memT_ready.at(i))
                pe.matmul(bank[4][:], w["L0_attn_lin2T"][:], memT[:], start=True, stop=True).then_inc(lin_ready.sem, 1)
                pe.wait_ge(*merged.at(i))
                for c in range(NC):
                    last = pe.transpose(bank[5][:, c * P:(c + 1) * P], g1[:, c * P:(c + 1) * P], ident[:])
                last.then_inc(merged_tr.sem, 1)

                pe.wait_ge(*b_ctx_loaded.at(i))
                pe.matmul(bank[1][:], w["L0_xattn_wkT"][:], ctxT[:], start=True, stop=True).then_inc(qk_b.sem, 1)
                for c in range(NC):
                    last = pe.matmul(bank[2][:, c * P:(c + 1) * P], ctxT[:, c * P:(c + 1) * P], w["L0_xattn_wvT"][:], start=True, stop=True)
                last.then_inc(v_b.sem, 1)
                x_transpose(1)
                pe.matmul(bank[0][:], w["L0_xattn_wqT"][:], XT[:], start=True, stop=True).then_inc(q_b.sem, 1)
                pe.wait_ge(*k_stacked.at(i))
                pe.wait_ge(*q_stacked.at(i))
                pe.wait_ge(*masks_ready.at(i))
                pe.wait_ge(*v_aug_ready.at(i))
                for b in range(NB):
                    for h in range(H1):
                        n = b * H1 + h
                        if h >= 4:
                            pe.wait_ge(*s_read.at(i, n - 3))
                        elif b > 0:
                            pe.wait_ge(*exp_ready.at(i, n - H1 + 13))
                        for c in range(QC):
                            last = pe.matmul(bank[4 + h % 4][:, c * S:(c + 1) * S],
                                             q_stack[:, h // 2, b * S + c * P:b * S + (c + 1) * P],
                                             k_stack[:, h // 2, h % 2, b * S:(b + 1) * S], start=True, stop=True)
                        last.then_inc(s_ready.sem, 1)
                    pe.wait_ge(*s_read.at(i, (b + 1) * H1))
                    if b > 0:
                        pe.wait_ge(*o_tok_ready.at(i, b))
                    for c in range(QC):
                        last = pe.transpose(bank[3][0:H1, c * P:(c + 1) * P], mx[:, c, :], ident[:])
                    last.then_inc(mx_tr.sem, 1)
                    pe.wait_ge(*neg_max_ready.at(i, b + 1))

                    def scores_T(h):
                        n = b * H1 + h
                        if h >= 4:
                            pe.wait_ge(*exp_ready.at(i, n - 3))
                        for c in range(QC):
                            dst = bank[4 + h % 4][:, c * S:(c + 1) * S]
                            pe.matmul(dst, k_stack[:, h // 2, h % 2, b * S + c * P:b * S + (c + 1) * P],
                                      q_stack[:, h // 2, b * S:(b + 1) * S], start=True, stop=False)
                            pe.matmul(dst, ident_b[:], add_k[:, b * QC + c, :], start=False, stop=False)
                            last = pe.matmul(dst, head_sel[:, h, :], neg_max[:], start=False, stop=True)
                        last.then_inc(sT_ready.sem, 1)

                    def values(g):
                        pe.wait_ge(*exp_ready.at(i, b * H1 + 4 * g + 4))
                        for c in range(QC):
                            for j in range(4):
                                last = pe.matmul(bank[g // 2][32 * j:32 * j + 32, (g % 2) * S:(g % 2 + 1) * S],
                                                 v_aug[:, b * QC + c, 4 * g + j, :], pT[:, g % 2, j, c, :],
                                                 start=(c == 0), stop=(c == QC - 1))
                        last.then_inc(pv_ready.sem, 1)

                    for h in range(4):
                        scores_T(h)
                    for g in range(G):
                        if g + 1 < G:
                            for h in range(4 * g + 4, 4 * g + 8):
                                scores_T(h)
                        values(g)
                    pe.wait_ge(*o_copied.at(i, 2 * b + 2))
                    for g in range(G):
                        for c in range(QC):
                            last = pe.transpose(bank[2 + c][:, g * P:(g + 1) * P], o_heads[:, g, c * P:(c + 1) * P], ident[:])
                    last.then_inc(o_tr.sem, 1)
                pe.wait_ge(*o_tok_ready.at(i))
                for c in range(NC):
                    last = pe.transpose(bank[0][:, c * P:(c + 1) * P], o_tok[:, c, :], ident[:])
                last.then_inc(o_tok_tr.sem, 1)
                pe.wait_ge(*o_T_ready.at(i))
                for c in range(NC):
                    last = pe.matmul(bank[1][:, c * P:(c + 1) * P], o_T[:, c * P:(c + 1) * P], w["L0_xattn_woT"][:], start=True, stop=True)
                last.then_inc(wo_ready.sem, 1)
                x_transpose(2)

                for c in range(NC):
                    last = pe.matmul(bank[0][:, c * E:(c + 1) * E], XT[:, c * P:(c + 1) * P], router[:], start=True, stop=True)
                last.then_inc(r_scored.sem, 1)

                def up(n):
                    e, k = n // FC, n % FC
                    if n >= 4:
                        pe.wait_ge(*he_ready.at(i, n - 3))
                    pe.matmul(bank[4 + n % 4][:], moe_w1[:, e, k * P:(k + 1) * P], XT[:], start=True, stop=True).then_inc(up_ready.sem, 1)

                def down(e):
                    pe.wait_ge(*he_ready.at(i, (e + 1) * FC))
                    if e >= 2:
                        pe.wait_ge(*down_added.at(i, e - 1))
                    for c in range(NC):
                        for k in range(FC):
                            last = pe.matmul(bank[2 + e % 2][:, c * P:(c + 1) * P], he[:, e % 2, k, c * P:(c + 1) * P],
                                             moe_w2[:, e, k, :], start=(k == 0), stop=(k == FC - 1))
                    last.then_inc(down_ready.sem, 1)

                for n in range(FC):
                    up(n)
                pe.wait_ge(*picked.at(i))
                for c in range(NC):
                    for j in range(c + 1):
                        pe.matmul(bank[1][:, c * E:(c + 1) * E], before_b[:] if j == c else ones_b[:], picked_b[:, j, :],
                                  start=(j == 0), stop=(j == c))
                for j in range(NC):
                    last = pe.matmul(bank[1][:, NC * E:(NC + 1) * E], ones_b[:], picked_b[:, j, :], start=(j == 0), stop=(j == NC - 1))
                last.then_inc(ranks.sem, 1)
                for e in range(E):
                    if e + 1 < E:
                        for k in range(FC):
                            up((e + 1) * FC + k)
                    down(e)
                x_transpose(3)

                pe.matmul(bank[0][:], w["L1_attn_W_Q"][:], XT[:], start=True, stop=True)
                pe.matmul(bank[1][:], w["L1_attn_W_K"][:], XT[:], start=True, stop=True)
                for c in range(NC):
                    last = pe.matmul(bank[2][:, c * P:(c + 1) * P], XT[:, c * P:(c + 1) * P], w["L1_attn_W_V"][:], start=True, stop=True)
                last.then_inc(qkv_c.sem, 1)
                pe.wait_ge(*aq_ready.at(i, 1))
                pe.wait_ge(*ak_ready.at(i))
                for b in range(NB):
                    for c in range(QC):
                        col = c * P
                        pe.matmul(bank[4 + b][:, col:col + (c + 1) * P], aq[:, b * S + c * P:b * S + (c + 1) * P],
                                  ak[:, b * S:b * S + (c + 1) * P], start=True, stop=False)
                        last = pe.matmul(bank[4 + b][:, col + c * P:col + (c + 1) * P], ident_b[:], future_b[:], start=False, stop=True)
                    last.then_inc(as_ready.sem, 1)
                for b in range(NB):
                    pe.wait_ge(*aexp_ready.at(i, b + 1))
                    for j in range(3):
                        last = pe.transpose(bank[6 + b][:, j * P:(j + 1) * P], ap[:, b, j, :], ident[:])
                    last.then_inc(apT_ready.sem, 1)
                pe.wait_ge(*aq_ready.at(i))
                for b in range(NB):
                    pe.wait_ge(*apT_copied.at(i, b + 1))
                    pe.matmul(bank[3][:, 2 * b * P:(2 * b + 1) * P], apT[:, b, 0:P], av[:, b * QC, :], start=True, stop=True)
                    for j in range(2):
                        last = pe.matmul(bank[3][:, (2 * b + 1) * P:(2 * b + 2) * P], apT[:, b, (1 + j) * P:(2 + j) * P],
                                         av[:, b * QC + j, :], start=(j == 0), stop=(j == 1))
                last.then_inc(apv_ready.sem, 1)
                x_transpose(4)

                for j, src in enumerate([XT, ctxT, ctxT]):
                    last = pe.matmul(bank[0][0:40, :], gates_w[:, j, :], src[:], start=(j == 0), stop=(j == 2))
                last.then_inc(pre_ready.sem, 1)
                wait_apart(pe, passed, *pm_ready.at(i))
                for c in range(NC):
                    pe.transpose(bank[1][:, c * H2:(c + 1) * H2], ga[:, c * P:(c + 1) * P], ident[0:H2, 0:H2])
                for c in range(NC):
                    last = pe.transpose(bank[1][:, 32 + c * H2:32 + (c + 1) * H2], gm[:, c * P:(c + 1) * P], ident[0:H2, 0:H2])
                last.then_inc(cols_ready.sem, 1)
                pe.wait_ge(*neg_pm_ready.at(i))
                pe.wait_ge(*v2_ready.at(i))

                def exponents(n):
                    b, h = n // H2, n % H2
                    if n >= 2:
                        pe.wait_ge(*c_ready.at(i, n - 1))
                    eb, qb = bank[4 + n % 2], bank[6 + n % 2]
                    for lo, q0, width, c in ((0, b * S, S, 0), (S, b * S + P, P, 1)):
                        pe.matmul(eb[:, lo:lo + width], head_sel[:, h, :], neg_pm[:, q0:q0 + width], start=True, stop=False)
                        pe.matmul(eb[:, lo:lo + P], ident_b[:], past_b[:], start=False, stop=True)
                        last = pe.matmul(qb[:, lo:lo + width], kpad2[:, h, b * S + c * P:b * S + (c + 1) * P],
                                         XT[:, q0:q0 + width], start=True, stop=True)
                    last.then_inc(eu_ready.sem, 1)

                def mixed(n):
                    b, g = n // 2, n % 2
                    pe.wait_ge(*c_ready.at(i, 4 * n + 4))
                    for c, lo, q0, width in ((0, 0, 0, S), (1, S, P, P)):
                        for j in range(4):
                            last = pe.matmul(bank[2 + b][32 * j:32 * j + 32, g * S + q0:g * S + q0 + width],
                                             v2_aug[:, b * QC + c, 4 * g + j, :], cT[:, g, j, lo:lo + width],
                                             start=(c == 0), stop=(c == 1))
                    last.then_inc(pv2_ready.sem, 1)

                for n in range(MU):
                    exponents(n)
                    if n >= 5 and n % 4 == 1:
                        mixed(n // 4 - 1)
                mixed(3)
                for b in range(NB):
                    pe.wait_ge(*o5_copied.at(i, b + 1))
                    if b == 0:
                        pe.wait_ge(*cols_copied.at(i))
                    for c in range(QC):
                        for g in range(2):
                            last = pe.transpose(bank[b][:, (c * 2 + g) * P:(c * 2 + g + 1) * P], o5[:, b, g, c * P:(c + 1) * P], ident[:])
                last.then_inc(o5_tr.sem, 1)
                x_transpose(5)

                pe.wait_ge(*rep_ready.at(i))
                for b in range(NB):
                    last = pe.matmul(bank[0][:, b * E:(b + 1) * E], pooled_rep[:, b, :], ffn_gw[:], start=True, stop=True)
                last.then_inc(fl_ready.sem, 1)
                for n in range(FU):
                    c, half = n // 2, n % 2
                    if n >= 4:
                        pe.wait_ge(*f_act.at(i, n - 3))
                    pe.matmul(bank[4 + n % 4][:], XT[:, c * P:(c + 1) * P], ffn_w[:, half * 512:(half + 1) * 512], start=True, stop=False)
                    pe.matmul(bank[4 + n % 4][:], row_sel[:], fb_parts[:, half * 512:(half + 1) * 512], start=False, stop=True).then_inc(f_ready.sem, 1)

        @block.scalar
        def _(act):
            act.wait_ge(*mem_qk.at(0))
            act.copy(qT_mem[:], bank[1][:, 0:M]).then_inc(mem_q_done.sem, 1)
            with act.Fori(0, STEPS) as i:
                act.wait_ge(*qkv_ready.at(i))
                act.copy(qT[:], bank[0][:]).then_inc(q_copied.sem, 1)
                for b in range(NB):
                    for j, n in enumerate([P, P, M]):
                        act.copy(vtok[0:n, b, j, :], bank[3 + b][0:n, j * P:(j + 1) * P]).then_inc(v_copied.sem, 1)
                for u, (b, c) in enumerate(units):
                    n, keys, s = (M, M, u % 2) if c is None else (P, KB, u % 2)
                    act.wait_ge(*max_a.at(i, u + 1))
                    for h in range(H0):
                        last = act.activation(probs[0:n, s, h, 0:keys], probs[0:n, s, h, 0:keys], ACT.Exp,
                                              bias=stats[0:n, s, 4 + h:5 + h], scale=float(DH0) ** -0.5,
                                              accum_out=stats[0:n, s, 8 + h:9 + h])
                    last.then_inc(exp_a.sem, 1)
                    act.wait_ge(*pT_a.at(i, u + 1))
                    if c is None:
                        act.copy(probsT_a[0:M, s].rearrange("p (h q) -> p h q", h=H0)[:, :, 0:M],
                                 bank[3][0:M].rearrange("p (h q) -> p h q", h=H0)[:, :, 0:M]).then_inc(pTa_copied.sem, 1)
                    else:
                        act.copy(probsT_a[:, s], bank[3][:]).then_inc(pTa_copied.sem, 1)
                act.wait_ge(*pv_a.at(i))
                act.copy(oT[:, 0:T], bank[7][:]).then_inc(oT_copied.sem, 1)
                act.copy(oT[:, T:T + M], bank[1][:, 0:M]).then_inc(oT_copied.sem, 1)
                act.wait_ge(*swa_ready.at(i))
                act.copy(vT_mem[:], bank[2][:, 0:M]).then_inc(vT_copied.sem, 1)
                for k in range(FC):
                    act.wait_ge(*zT_a.at(i, k + 1))
                    act.activation(hT[:, k, 0:T], bank[5 + k % 2][:], ACT.Silu, bias=b1[:, k:k + 1]).then_inc(hT_a.sem, 1)
                act.wait_ge(*zT_a.at(i))
                for k in range(FC):
                    act.activation(hT[:, k, T:T + M], bank[1][:, M * (k + 1):M * (k + 2)], ACT.Silu, bias=b1[:, k:k + 1]).then_inc(hT_a.sem, 1)
                act.wait_ge(*eT_tr.at(i))
                act.copy(etok[:, 0:NC, :], bank[7][:].rearrange("p (c d) -> p c d", c=NC)).then_inc(etok_copied.sem, 1)
                act.copy(etok[0:M, NC, :], bank[1][0:M, 0:P]).then_inc(etok_copied.sem, 1)
                chain = Chain(act, act_a, i)
                for c in range(NC + 1):
                    n, s = (P if c < NC else M), c % 2
                    act.wait_ge(*z_biased.at(i, c + 1))
                    if c >= 2:
                        act.wait_ge(*slope_ready.at(i, c - 1))
                    chain.link(act.activation(sg[0:n, s], zt[0:n, s], ACT.Tanh, scale=0.5))
                    act.activation(sg[0:n, s], sg[0:n, s], ACT.Copy, scale=0.5, bias=0.5).then_inc(sg_ready.sem, 1)
                chain.close()
            with act.Fori(0, STEPS) as i:
                def x_copy(n):
                    act.wait_ge(*x_tr.at(i, n))
                    act.copy(XT[:], bank[7][:]).then_inc(xt_ready.sem, 1)

                for k in range(FC):
                    act.wait_ge(*zT_b.at(i, k + 1))
                    act.activation(hT[:, k, 0:T], bank[4 + k][:], ACT.Silu, bias=b1_new[:, k:k + 1]).then_inc(hT_b.sem, 1)
                act.wait_ge(*lin1.at(i))
                act.activation(g1[:], bank[3][:], ACT.Tanh, scale=0.5).then_inc(g_ready.sem, 1)
                act.wait_ge(*lin_ready.at(i))
                act.activation(g2[:], bank[4][:], ACT.Tanh, scale=0.5).then_inc(g_ready.sem, 1)
                act.wait_ge(*qk_b.at(i))
                act.activation(kf[:], bank[1][:], ACT.Identity, bias=x_bk[:, 0:1]).then_inc(kf_ready.sem, 1)
                act.wait_ge(*kf_ready.at(i))
                act.copy(k_parts[:, 0, :], kf[:]).then_inc(kh_ready.sem, 1)
                x_copy(1)
                for b in range(NB):
                    for h in range(H1):
                        n = b * H1 + h
                        g, j = h // 4, h % 4
                        act.wait_ge(*sT_ready.at(i, n + 1))
                        if h % 4 == 0 and b * G + g >= 2:
                            act.wait_ge(*pv_ready.at(i, b * G + g - 1))
                        act.activation(pT[:, g % 2, j], bank[4 + h % 4][:].rearrange("p (c q) -> p c q", c=QC), ACT.Exp).then_inc(exp_ready.sem, 1)
                    for half in range(2):
                        act.wait_ge(*pv_ready.at(i, b * G + 2 * half + 2))
                        if b > 0 and half == 0:
                            act.wait_ge(*o_tr.at(i, b))
                        act.copy(o_heads[:, 2 * half:2 * half + 2, :], bank[half][:].rearrange("p (g q) -> p g q", g=2)).then_inc(o_copied.sem, 1)
                act.wait_ge(*o_tok_tr.at(i))
                act.copy(o_T[:], bank[0][:]).then_inc(o_T_ready.sem, 1)
                x_copy(2)
                act.wait_ge(*share_diff.at(i))
                act.activation(share[:, 1, :], share[:, 0, :], ACT.Exp).then_inc(share_exp.sem, 1)
                for n in range(E * FC):
                    e, k = n // FC, n % FC
                    act.wait_ge(*up_ready.at(i, n + 1))
                    if k == 0 and e >= 2:
                        act.wait_ge(*down_ready.at(i, e - 1))
                    act.activation(he[:, e % 2, k, :], bank[4 + n % 4][:], ACT.Silu).then_inc(he_ready.sem, 1)
                x_copy(3)
                act.wait_ge(*qkv_c.at(i))
                act.copy(aq[:], bank[0][:]).then_inc(aq_ready.sem, 1)
                act.copy(av[:], bank[2][:].rearrange("p (c d) -> p c d", c=NC)).then_inc(aq_ready.sem, 1)
                scale = float(D) ** -0.5
                for b in range(NB):
                    act.wait_ge(*amax_ready.at(i, b + 1))
                    act.activation(ap[:, b, 0, :], bank[4 + b][:, 0:P], ACT.Exp, bias=ast[:, 1, 2 * b:2 * b + 1], scale=scale,
                                   accum_out=ast[:, 2, 2 * b:2 * b + 1])
                    act.activation(ap[:, b, 1:3, :], bank[4 + b][:, P:3 * P].rearrange("p (j k) -> p j k", j=2), ACT.Exp,
                                   bias=ast[:, 1, 2 * b + 1:2 * b + 2], scale=scale,
                                   accum_out=ast[:, 2, 2 * b + 1:2 * b + 2]).then_inc(aexp_ready.sem, 1)
                for b in range(NB):
                    act.wait_ge(*apT_ready.at(i, b + 1))
                    act.copy(apT[:, b, :], bank[6 + b][:, 0:3 * P]).then_inc(apT_copied.sem, 1)
                x_copy(4)
                act.wait_ge(*abs_ready.at(i))
                act.activation(cs[:], gl[:], ACT.Exp, scale=-1.0).then_inc(ef_ready.sem, 1)
                act.wait_ge(*ef_ready.at(i))
                act.activation(gl[:], cs[:], ACT.Ln, bias=1.0).then_inc(ln_ready.sem, 1)
                act.wait_ge(*cols_ready.at(i))
                act.copy(a_col[:], bank[1][:, 0:32].rearrange("p (c h) -> p c h", c=NC)).then_inc(cols_copied.sem, 1)
                act.activation(em_col[:], bank[1][:, 32:64].rearrange("p (c h) -> p c h", c=NC), ACT.Exp, scale=-1.0).then_inc(cols_copied.sem, 1)
                act.wait_ge(*cols_copied.at(i, 1))
                for n in range(MU):
                    b, h = n // H2, n % H2
                    act.wait_ge(*eu_ready.at(i, n + 1))
                    if n >= 2:
                        act.wait_ge(*c_ready.at(i, n - 1))
                    act.activation(decay[:, n % 2, 0:S], bank[4 + n % 2][:, 0:S], ACT.Exp, bias=a_col[:, b * QC, h:h + 1])
                    act.activation(decay[:, n % 2, S:S + P], bank[4 + n % 2][:, S:S + P], ACT.Exp, bias=a_col[:, b * QC + 1, h:h + 1]).then_inc(decay_ready.sem, 1)
                for b in range(NB):
                    act.wait_ge(*pv2_ready.at(i, 2 * b + 2))
                    act.copy(o5[:, b], bank[2 + b][:].rearrange("p (g q) -> p g q", g=2)).then_inc(o5_copied.sem, 1)
                x_copy(5)
                act.wait_ge(*fmax_ready.at(i))
                act.activation(fe[:], fl[:], ACT.Exp).then_inc(fe_ready.sem, 1)
                for n in range(FU):
                    act.wait_ge(*f_ready.at(i, n + 1))
                    if n >= 2:
                        act.wait_ge(*f_added.at(i, n - 1))
                    act.activation(gl_act[:, n % 2], bank[4 + n % 4][:], ACT.Gelu).then_inc(f_act.sem, 1)

        @block.vector
        def _(dve):
            for primed in (grads_added, f_added, x_in_used, ctx_used):
                primed.prime(dve)
            dve.wait_ge(*pool_zero.at(0, 1))
            dve.wait_ge(*mem_q_done.at(0))
            for h in range(H0):
                r = slice(DH0 * h, DH0 * h + DH0)
                for b in range(NB):
                    last = dve.tensor_copy(kpad[r, h, b, 0:M], bank[1][r, M:2 * M])
            last.then_inc(mem_k_done.sem, 1)
            dve.wait_ge(*const_ready.at(0))
            with dve.Fori(0, STEPS) as i:
                chain = Chain(dve, dve_a, i)
                dve.wait_ge(*qkv_ready.at(i))
                for h in range(H0):
                    r = slice(DH0 * h, DH0 * h + DH0)
                    dve.tensor_copy(kpad[r, h, :, M:KW], bank[2][r].rearrange("p (b t) -> p b t", b=NB)).then_inc(k_copied.sem, 1)

                def maxima(u):
                    b, c = units[u]
                    n, keys, s = (M, M, u % 2) if c is None else (P, KB, u % 2)
                    if u >= 2:
                        dve.wait_ge(*pT_a.at(i, u - 1))
                    wait_apart(dve, passed, *scores_a.at(i, u + 1))
                    mask = mem_mask if c is None else window
                    for h in range(H0):
                        src = s_banks(u)[h // 2][0:n, (h % 2) * KB:(h % 2) * KB + keys]
                        last = dve.tensor_tensor_reduce(probs[0:n, s, h, 0:keys], src, mask[0:n, 0:keys], 1.0, NEG,
                                                        ALU.add, ALU.max, stats[0:n, s, h:h + 1])
                    chain.link(last)
                    dve.tensor_scalar(stats[0:n, s, 4:8], stats[0:n, s, 0:4], -float(DH0) ** -0.5, None, ALU.mult).then_inc(max_a.sem, 1)

                maxima(0)
                for u, (b, c) in enumerate(units):
                    n, keys, s = (M, M, u % 2) if c is None else (P, KB, u % 2)
                    if u + 1 < NU:
                        maxima(u + 1)
                    dve.wait_ge(*exp_a.at(i, u + 1))
                    chain.link(dve.reciprocal(stats[0:n, s, 12:16], stats[0:n, s, 8:12]))
                    dve.tensor_tensor(probs[0:n, s, :, 0:keys], probs[0:n, s, :, 0:keys],
                                      stats[0:n, s, 12:16].unsqueeze(2).to_broadcast([n, H0, keys]), ALU.mult).then_inc(norm_a.sem, 1)
                    dve.wait_ge(*pT_a.at(i, u + 1))
                    if c is None:
                        dve.memset(probsT_b[:, s, 0:1], 0.0).then_inc(pTb_copied.sem, 1)
                    else:
                        dve.tensor_copy(probsT_b[:, s], bank[4][0:WIN]).then_inc(pTb_copied.sem, 1)
                dve.wait_ge(*swa_ready.at(i, 1))
                dve.tensor_copy(vT_all[:, bass.ds(i * T, T)], bank[0][:]).then_inc(vT_copied.sem, 1)
                dve.wait_ge(*vT_copied.at(i))
                dve.wait_ge(*pred_a.at(i))
                dve.scalar_tensor_tensor(eT[:, 0:T], bank[3][:], b2[:, 0:1], vT_all[:, bass.ds(i * T, T)], ALU.add, ALU.subtract)
                chain.link(dve.scalar_tensor_tensor(eT[:, T:T + M], bank[4][:, 0:M], b2[:, 0:1], vT_mem[:], ALU.add, ALU.subtract))
                dve.tensor_scalar(eT[:, T:T + M], eT[:, T:T + M], float(NB), None, ALU.mult).then_inc(e_ready.sem, 1)
                for c in range(NC + 1):
                    n, s = (P if c < NC else M), c % 2
                    zb, db = zd_banks(c)
                    dve.wait_ge(*zd_ready.at(i, c + 1))
                    if c >= 2:
                        dve.wait_ge(*grads_ready.at(i, c - 1))
                        dve.wait_ge(*slope_ready.at(i, c - 1))
                        dve.wait_ge(*bias_summed.at(i, c - 1))
                    dve.tensor_tensor(zt[0:n, s], zb[0:n], b1_rows[0:n], ALU.add).then_inc(z_biased.sem, 1)
                    dve.wait_ge(*sg_ready.at(i, c + 1))
                    dve.tensor_tensor(ht[0:n, s], zt[0:n, s], sg[0:n, s], ALU.mult).then_inc(h_ready.sem, 1)
                    dve.wait_ge(*slope_ready.at(i, c + 1))
                    dve.tensor_tensor(dz[0:n, s], db[0:n], sl[0:n, s], ALU.mult).then_inc(dz_ready.sem, 1)
                dve.wait_ge(*grads_ready.at(i))
                dve.tensor_tensor(grad1[:], grad1[:], bank[0][:], ALU.add)
                dve.tensor_tensor(grad2[:], grad2[:], bank[3][:], ALU.add).then_inc(grads_added.sem, 1)
                chain.close()
            dve.tensor_scalar(rate[:, 2:3], rate[:, 0:1], -1.0, 1.0, ALU.mult, ALU.add)
            dve.tensor_scalar(rate[:, 3:4], rate[:, 1:2], -1.0, None, ALU.mult).then_inc(upd_dve.sem, 1)
            dve.wait_ge(upd_dve.sem, 1)
            dve.wait_ge(*upd_pe.at(0))
            pairs = [(w1T_new[:], w1T[:], grad1[:]),
                     (w2T_new[:].rearrange("p k d -> p (k d)"), w2T[:].rearrange("p k d -> p (k d)"), bank[4][:]),
                     (b1_new[:], b1[:], bank[1][:, 0:FC]), (b2_new[:], b2[:], bank[1][:, FC:FC + 1])]
            for new, old, grad in pairs:
                last = dve.tensor_scalar(new, old, rate[:, 2:3], None, ALU.mult)
            last.then_inc(upd_dve.sem, 1)
            dve.wait_ge(upd_dve.sem, 2)
            for new, old, grad in pairs:
                last = dve.scalar_tensor_tensor(new, grad, rate[:, 3:4], new, ALU.mult, ALU.add)
            last.then_inc(updated.sem, 1)
            dve.wait_ge(late_loaded.sem, 16 * len(late_w))
            pro = Chain(dve, dve_pro, 0)
            pro.link(dve.tensor_copy(fb_parts[0:1, :], ffn_b[:]))
            pro.link(dve.tensor_tensor(fb_row[:, 0], ffn_b[:], fb_parts[0:1, :], ALU.subtract))
            pro.link(dve.tensor_copy(fb_m[:], fb_row[:, 0]))
            dve.tensor_copy(fb_parts[32:33, :], fb_m[:])
            dve.tensor_tensor(fb_parts[64:65, :], fb_row[:, 0], fb_m[:], ALU.subtract).then_inc(fb_ready.sem, 1)
            with dve.Fori(0, STEPS) as i:
                chain = Chain(dve, dve_b, i)

                def layernorm(n, dst):
                    for c in range(NC):
                        last = dve.bn_stats(bn[:, c, :], R[:, c, :])
                    chain.link(last, passed)
                    for c in range(NC):
                        last = dve.bn_aggr(mv[:, c, :], bn[:, c, :])
                    chain.link(last)
                    dve.tensor_scalar(var_eps[:], mv[:, :, 1], EPS, None, ALU.add).then_inc(var_ready.sem, 1)
                    dve.wait_ge(*rstd_ready.at(i, n))
                    for c in range(NC):
                        last = dve.tensor_scalar(dst[:, c, :], R[:, c, :], mv[:, c, 0:1], rstd[:, c:c + 1], ALU.subtract, ALU.mult)
                    last.then_inc(x_norm.sem, 1)

                dve.wait_ge(*out_mem.at(i))
                dve.tensor_scalar(memT[:], bank[2][:], b2_new[:, 0:1], None, ALU.add).then_inc(memT_ready.sem, 1)
                dve.wait_ge(*g_ready.at(i, 1))
                dve.scalar_tensor_tensor(g1[:], g1[:], 1.0, vT_all[:, bass.ds(i * T, T)], ALU.add, ALU.mult)
                dve.wait_ge(*g_ready.at(i))
                chain.link(dve.scalar_tensor_tensor(g2[:], g2[:], 1.0, memT[:], ALU.add, ALU.mult))
                dve.tensor_tensor(g1[:], g1[:], g2[:], ALU.add).then_inc(merged.sem, 1)
                dve.wait_ge(*merged_tr.at(i))
                r_done = dve.scalar_tensor_tensor(R[:], bank[5][:].rearrange("p (c d) -> p c d", c=NC), 0.5, x_in[:], ALU.mult, ALU.add)
                r_done.then_inc(x_in_used.sem, 1)
                dve.wait_ge(*x_in_used.at(i))
                layernorm(1, X)

                dve.wait_ge(*v_b.at(i))
                dve.tensor_tensor(v_aug[:, :, :, 0:DH1], bank[2][:].rearrange("p (c h d) -> p c h d", c=NC, h=H1),
                                  x_bv_rows[:].rearrange("p (h d) -> p h d", h=H1).unsqueeze(1).to_broadcast([P, NC, H1, DH1]), ALU.add).then_inc(v_aug_ready.sem, 1)
                dve.wait_ge(*q_b.at(i))
                chain.link(dve.tensor_scalar(qf[:], bank[0][:], x_bq[:, 0:1], float(DH1) ** -0.5, ALU.add, ALU.mult))
                chain.link(dve.tensor_copy(q_parts[:, 0, :], qf[:]))
                chain.link(dve.tensor_tensor(qr[:], qf[:], q_parts[:, 0, :], ALU.subtract))
                chain.link(dve.tensor_copy(q_parts[:, 1, :], qr[:]))
                dve.tensor_tensor(q_parts[:, 2, :], qr[:], q_parts[:, 1, :], ALU.subtract).then_inc(q_parts_ready.sem, 1)
                dve.wait_ge(*masks_ready.at(i))
                for b in range(NB):
                    if b > 0:
                        dve.wait_ge(*mx_tr.at(i, b))
                    for h in range(H1):
                        wait_apart(dve, passed, *s_ready.at(i, b * H1 + h + 1))
                        for c in range(QC):
                            sc = bank[4 + h % 4][:, c * S:(c + 1) * S]
                            last = dve.tensor_tensor_reduce(sc, sc, add_q[:, b * QC + c, :], 1.0,
                                                            2.0 * NEG, ALU.add, ALU.max, mx[:, c, h:h + 1])
                        last.then_inc(s_read.sem, 1)
                    dve.wait_ge(*mx_tr.at(i, b + 1))
                    mt = bank[3][0:H1, 0:S]
                    chain.link(dve.tensor_scalar(neg_max[0:H1, :], mt, -1.0, None, ALU.mult))
                    chain.link(dve.scalar_tensor_tensor(neg_r[:], mt, -1.0, neg_max[0:H1, :], ALU.mult, ALU.subtract))
                    chain.link(dve.tensor_copy(neg_m[:], neg_r[:]))
                    dve.tensor_copy(neg_max[32:32 + H1, :], neg_m[:])
                    dve.tensor_tensor(neg_max[64:64 + H1, :], neg_r[:], neg_m[:], ALU.subtract).then_inc(neg_max_ready.sem, 1)
                    dve.wait_ge(*o_tr.at(i, b + 1))
                    heads = [bank[2 + c][:].rearrange("p (h j) -> p h j", h=H1) for c in range(QC)]
                    for c in range(QC):
                        last = dve.reciprocal(rec[:, c, :], heads[c][:, :, DH1])
                    chain.link(last)
                    for c in range(QC):
                        last = dve.tensor_tensor(o_tok[:, b * QC + c, :].rearrange("p (h d) -> p h d", h=H1), heads[c][:, :, 0:DH1],
                                                 rec[:, c, :].unsqueeze(2).to_broadcast([P, H1, DH1]), ALU.mult)
                    last.then_inc(o_tok_ready.sem, 1)
                dve.wait_ge(*wo_ready.at(i))
                dve.wait_ge(*x_plus.at(i))
                chain.link(dve.tensor_tensor(R[:], R[:], bank[1][:].rearrange("p (c d) -> p c d", c=NC), ALU.add))
                layernorm(2, X)

                dve.wait_ge(*r_scored.at(i))
                chain.link(dve.tensor_copy(logits[:], bank[0][:, 0:NC * E].rearrange("p (c e) -> p c e", c=NC)), passed)
                for c in range(NC):
                    last = dve.max(top[:, c, :], logits[:, c, :])
                chain.link(last, passed)
                for c in range(NC):
                    last = dve.max_index(top_i[:, c, :], top[:, c, :], logits[:, c, :])
                dve.tensor_tensor(share[:, 0, :], top[:, :, 1], top[:, :, 0], ALU.subtract).then_inc(share_diff.sem, 1)
                dve.wait_ge(*share_diff.at(i))
                chain.link(dve.tensor_copy(top_f[:], top_i[:, :, 0:2]))
                for j in range(2):
                    last = dve.tensor_tensor(pick[:, j], iota_e[:].unsqueeze(1).to_broadcast([P, NC, E]),
                                             top_f[:, :, j:j + 1].to_broadcast([P, NC, E]), ALU.is_equal)
                chain.link(last)
                dve.tensor_tensor(picked_b[:], pick[:, 0], pick[:, 1], ALU.add).then_inc(picked.sem, 1)
                dve.wait_ge(*share_exp.at(i))
                chain.link(dve.tensor_scalar(share[:, 0, :], share[:, 1, :], 1.0, None, ALU.add))
                chain.link(dve.reciprocal(share[:, 2, :], share[:, 0, :]))
                chain.link(dve.tensor_tensor(share[:, 3, :], share[:, 1, :], share[:, 2, :], ALU.mult))
                for j in range(2):
                    last = dve.tensor_tensor(pick[:, j], pick[:, j], share[:, 2 + j, :].unsqueeze(2).to_broadcast([P, NC, E]), ALU.mult)
                dve.wait_ge(*ranks.at(i))
                chain.link(dve.tensor_tensor(rank[:], bank[1][:, 0:NC * E].rearrange("p (c e) -> p c e", c=NC),
                                             seen[:].unsqueeze(1).to_broadcast([P, NC, E]), ALU.add))
                dve.tensor_tensor(seen[:], bank[1][:, NC * E:(NC + 1) * E], seen[:], ALU.add)
                chain.link(dve.tensor_tensor(gate[:], pick[:, 0], pick[:, 1], ALU.add))
                dve.scalar_tensor_tensor(gate[:], rank[:], float(CAP), gate[:], ALU.is_lt, ALU.mult).then_inc(gates_ready.sem, 1)
                dve.wait_ge(*gates_ready.at(i))
                dve.wait_ge(*x_twice.at(i))
                for e in range(E):
                    dve.wait_ge(*down_ready.at(i, e + 1))
                    for c in range(NC):
                        last = dve.scalar_tensor_tensor(R[:, c, :], bank[2 + e % 2][:, c * P:(c + 1) * P], gate[:, c, e:e + 1],
                                                        R[:, c, :], ALU.mult, ALU.add)
                    last.then_inc(down_added.sem, 1)
                    dve.wait_ge(*down_added.at(i, e + 1))
                layernorm(3, X)

                dve.wait_ge(*qkv_c.at(i))
                dve.tensor_copy(ak[:], bank[1][:]).then_inc(ak_ready.sem, 1)
                for b in range(NB):
                    dve.wait_ge(*as_ready.at(i, b + 1))
                    dve.tensor_reduce(ast[:, 0, 2 * b:2 * b + 1], bank[4 + b][:, 0:P], AX.X, ALU.max)
                    chain.link(dve.tensor_reduce(ast[:, 0, 2 * b + 1:2 * b + 2], bank[4 + b][:, P:3 * P], AX.X, ALU.max))
                    dve.tensor_scalar(ast[:, 1, 2 * b:2 * b + 2], ast[:, 0, 2 * b:2 * b + 2], -float(D) ** -0.5, None, ALU.mult).then_inc(amax_ready.sem, 1)
                dve.wait_ge(*aexp_ready.at(i))
                chain.link(dve.reciprocal(ast[:, 3, :], ast[:, 2, :]))
                dve.wait_ge(*apv_ready.at(i))
                for c in range(NC):
                    last = dve.scalar_tensor_tensor(R[:, c, :], bank[3][:, c * P:(c + 1) * P], ast[:, 3, c:c + 1], X[:, c, :], ALU.mult, ALU.add)
                chain.link(last)
                layernorm(4, X)

                dve.wait_ge(*pre_ready.at(i))
                dve.tensor_scalar(gi[:], bank[0][0:8, :], gates_b[0:8, 0:1], None, ALU.add)
                chain.link(dve.tensor_scalar(gf[:], bank[0][32:40, :], gates_b[32:40, 0:1], None, ALU.add))
                dve.scalar_tensor_tensor(gl[:], gf[:], -1.0, gf[:], ALU.mult, ALU.max).then_inc(abs_ready.sem, 1)
                dve.wait_ge(*ln_ready.at(i))
                chain.link(dve.scalar_tensor_tensor(gf[:], gf[:], 0.0, gl[:], ALU.min, ALU.subtract))
                for b in range(NB):
                    q = slice(b * S, (b + 1) * S)
                    last = dve.tensor_tensor_scan(cs[:, q], ones8[:], gf[:, q], 0.0, ALU.mult, ALU.add)
                chain.link(last)
                chain.link(dve.tensor_tensor(ga[:], gi[:], cs[:], ALU.subtract))
                for b in range(NB):
                    q = slice(b * S, (b + 1) * S)
                    last = dve.tensor_tensor_scan(pm[:, q], ones8[:], ga[:, q], NEG, ALU.mult, ALU.max)
                chain.link(last)
                dve.tensor_tensor(gm[:], cs[:], pm[:], ALU.add).then_inc(pm_ready.sem, 1)
                chain.link(dve.tensor_scalar(neg_pm[0:8, :], pm[:], -1.0, None, ALU.mult))
                chain.link(dve.scalar_tensor_tensor(gi[:], pm[:], -1.0, neg_pm[0:8, :], ALU.mult, ALU.subtract))
                chain.link(dve.tensor_copy(pb2[:], gi[:]))
                dve.tensor_copy(neg_pm[32:40, :], pb2[:])
                dve.tensor_tensor(neg_pm[64:72, :], gi[:], pb2[:], ALU.subtract).then_inc(neg_pm_ready.sem, 1)
                for n in range(MU):
                    b, g, j = n // H2, (n // 4) % 2, n % 4
                    dve.wait_ge(*decay_ready.at(i, n + 1))
                    if n >= 8 and n % 4 == 0:
                        dve.wait_ge(*pv2_ready.at(i, n // 4 - 1))
                    dve.tensor_tensor(cT[:, g, j, :], bank[6 + n % 2][:, 0:S + P], decay[:, n % 2, :], ALU.mult).then_inc(c_ready.sem, 1)
                dve.wait_ge(*o5_tr.at(i))
                dve.wait_ge(*cols_copied.at(i))
                for b in range(NB):
                    src = bank[b][:].rearrange("p (c h j) -> p c h j", c=QC, h=H2)
                    last = dve.tensor_copy(den[:, b * QC:(b + 1) * QC, :], src[:, :, :, DH2])
                chain.link(last)
                chain.link(dve.scalar_tensor_tensor(den[:], den[:], -1.0, den[:], ALU.mult, ALU.max))
                chain.link(dve.tensor_tensor(den[:], den[:], em_col[:], ALU.max))
                chain.link(dve.tensor_scalar(den[:], den[:], 1e-6, None, ALU.add))
                chain.link(dve.reciprocal(den[:], den[:]))
                for b in range(NB):
                    src = bank[b][:].rearrange("p (c h j) -> p c h j", c=QC, h=H2)
                    cc = slice(b * QC, (b + 1) * QC)
                    last = dve.tensor_tensor(hh[:, cc], src[:, :, :, 0:DH2], den[:, cc].unsqueeze(3).to_broadcast([P, QC, H2, DH2]), ALU.mult)
                chain.link(last)
                h3 = hh.rearrange("p c h d -> p (c h) d")
                hs3 = R[:].rearrange("p c (h d) -> p (c h) d", d=DH2)
                wide = [P, NC * H2, DH2]
                chain.link(dve.tensor_reduce(hm[:, 0, :], h3, AX.X, ALU.add))
                chain.link(dve.tensor_scalar(hm[:, 1, :], hm[:, 0, :], 1.0 / DH2, None, ALU.mult))
                chain.link(dve.tensor_tensor(h3, h3, hm[:, 1, :].unsqueeze(2).to_broadcast(wide), ALU.subtract))
                chain.link(dve.tensor_tensor(hs3, h3, h3, ALU.mult))
                chain.link(dve.tensor_reduce(hm[:, 0, :], hs3, AX.X, ALU.add))
                dve.tensor_scalar(hm[:, 2, :], hm[:, 0, :], 1.0 / DH2, EPS, ALU.mult, ALU.add).then_inc(var2_ready.sem, 1)
                dve.wait_ge(*rstd2_ready.at(i))
                chain.link(dve.tensor_tensor(h3, h3, hrs[:].unsqueeze(2).to_broadcast(wide), ALU.mult))
                hx = hh.rearrange("p c h d -> p c (h d)")
                chain.link(dve.tensor_tensor(hx, hx, out_w_rows[:].unsqueeze(1).to_broadcast([P, NC, P]), ALU.mult))
                dve.tensor_tensor(R[:], hx, X[:], ALU.add).then_inc(ctx_used.sem, 1)
                dve.wait_ge(*ctx_used.at(i))
                layernorm(5, X)

                dve.wait_ge(*xt_ready.at(i))
                chain.link(dve.tensor_reduce(pooled[:], XT[:].rearrange("p (b t) -> p b t", b=NB), AX.X, ALU.add))
                for b in range(NB):
                    last = dve.tensor_scalar(pooled_rep[:, b, :], ones[:], pooled[:, b:b + 1], 1.0 / S, ALU.mult, ALU.mult)
                last.then_inc(rep_ready.sem, 1)
                dve.wait_ge(*fl_ready.at(i))
                chain.link(dve.tensor_tensor(fl[:], bank[0][:, 0:NB * E].rearrange("p (b e) -> p b e", b=NB),
                                             ffn_gb_rows[:].unsqueeze(1).to_broadcast([P, NB, E]), ALU.add), passed)
                for b in range(NB):
                    last = dve.max(ftop[:, b, :], fl[:, b, :])
                chain.link(last)
                dve.tensor_tensor(fgate[:], fl[:], ftop[:, :, 1:2].to_broadcast([P, NB, E]), ALU.is_ge)
                chain.link(dve.tensor_tensor(hm[:, 0, 0:NB * E].rearrange("p (b e) -> p b e", b=NB), fl[:], ftop[:, :, 0:1].to_broadcast([P, NB, E]), ALU.subtract))
                dve.tensor_copy(fl[:], hm[:, 0, 0:NB * E].rearrange("p (b e) -> p b e", b=NB)).then_inc(fmax_ready.sem, 1)
                dve.wait_ge(*fe_ready.at(i))
                chain.link(dve.tensor_tensor(fgate[:], fgate[:], fe[:], ALU.mult))
                chain.link(dve.tensor_reduce(fs[:, 0, :], fgate[:], AX.X, ALU.add))
                chain.link(dve.reciprocal(fs[:, 1, :], fs[:, 0, :]))
                chain.link(dve.tensor_tensor(fgate[:], fgate[:], fs[:, 1, :].unsqueeze(2).to_broadcast([P, NB, E]), ALU.mult))
                for n in range(FU):
                    c, half = n // 2, n % 2
                    b = c // QC
                    dve.wait_ge(*f_act.at(i, n + 1))
                    for j in range(4):
                        e = 4 * half + j
                        first = n % 2 == 0 and j == 0
                        ins = dve.scalar_tensor_tensor(R[:, c, :], gl_act[:, n % 2, j * P:(j + 1) * P], fgate[:, b, e:e + 1],
                                                       X[:, c, :] if first else R[:, c, :], ALU.mult, ALU.add)
                        if j < 3:
                            chain.link(ins)
                    ins.then_inc(f_added.sem, 1)
                    dve.wait_ge(*f_added.at(i, n + 1))
                dve.wait_ge(*out_saved.before(i))
                layernorm(6, Y)
                chain.close()


_TRANSPOSED = {"L0_attn_" + n + "T": "L0_attn_" + n for n in ("wq", "wk", "wv", "wo", "lin1", "lin2", "w1", "w2", "mem")}
_TRANSPOSED.update({"L0_xattn_" + n + "T": "L0_xattn_" + n for n in ("wq", "wk", "wv", "wo")})
_TRANSPOSED.update({"L0_ffn_router_wT": "L0_ffn_router_w", "L1_xattn_igate_wT": "L1_xattn_igate_w",
                    "L1_xattn_fgate_wT": "L1_xattn_fgate_w", "L1_ffn_gate_wT": "L1_ffn_gate_w"})
_PLAIN = ["x", "ctx_1024", "mask_BxSxS2_bf1", "L0_attn_mem", "L0_attn_w2", "L0_attn_b1", "L0_attn_b2",
          "L0_attn_alpha", "L0_attn_theta", "L0_xattn_bq", "L0_xattn_bk", "L0_xattn_bv", "L0_xattn_bo",
          "L0_ffn_w1", "L0_ffn_w2", "L1_attn_W_Q", "L1_attn_W_K", "L1_attn_W_V", "L1_xattn_igate_b",
          "L1_xattn_fgate_b", "L1_xattn_out_w", "L1_ffn_gate_b", "L1_ffn_expert_b"]


def kernel(**inputs):
    import numpy as _np
    import concourse.bacc as _bacc
    from concourse import mybir as _mybir
    from concourse.bass_utils import run_bass_kernel_spmd as _run

    laid = {n: inputs[n] for n in _PLAIN}
    for n in ("L0_attn_alpha", "L0_attn_theta"):
        laid[n] = _np.reshape(inputs[n], (1,))
    for new, old in _TRANSPOSED.items():
        laid[new] = _np.transpose(inputs[old])
    laid["xT"] = _np.transpose(_np.reshape(inputs["x"], (B * S, D)))
    laid["ctxT"] = _np.transpose(_np.reshape(inputs["ctx_1024"], (B * S, D)))
    laid["L0_attn_b1_cols"] = _np.transpose(_np.reshape(inputs["L0_attn_b1"], (FC, P)))
    laid["maskT"] = _np.transpose(inputs["mask_BxSxS2_bf1"], (0, 2, 1))
    laid["L1_ffn_expert_wT"] = _np.reshape(_np.transpose(inputs["L1_ffn_expert_w"], (2, 0, 1)), (D, E * D))

    nc = _bacc.Bacc("TRN2", target_bir_lowering=False, num_devices=1)
    arrays, args = {}, {}
    for name, value in laid.items():
        value = _np.ascontiguousarray(value)
        arrays[f"in_{name}_dram"] = value
        args[name] = nc.dram_tensor(f"in_{name}_dram", value.shape, _mybir.dt.from_np(value.dtype), kind="ExternalInput").ap()
    out = nc.dram_tensor("out_0_dram", (B, S, D), _mybir.dt.float32, kind="ExternalOutput").ap()
    parts_dram = nc.dram_tensor("parts_dram", (2, 3, D, T), _mybir.dt.bfloat16, kind="Internal").ap()
    decoder_kernel(nc, args, out, parts_dram)
    r = _run(nc, [arrays], core_ids=[0])
    return r.results[0]["out_0_dram"]
```

```python
from contextlib import ExitStack

import concourse.bass as bass
from concourse import mybir

F32 = mybir.dt.float32
BF16 = mybir.dt.bfloat16
U8 = mybir.dt.uint8
U32 = mybir.dt.uint32
ALU = mybir.AluOpType
ACT = mybir.ActivationFunctionType
AX = mybir.AxisListType

P = 128
B, S, D = 8, 256, 128
NB = 2
STEPS = B // NB
T = NB * S
NC = T // P
QC = S // P
M = 64
KW = M + S
HID = 512
FC = HID // P
H0, DH0 = 4, 32
WIN = 64
KB = P + WIN
H1, DH1 = 16, 8
E = 8
CAP = int(1.25 * B * S * 2 / E) + 1
H2, DH2 = 8, 16
EPS = 1e-5
NEG = -float(2 ** 100)
TERMS = [(0, 0), (0, 1), (0, 2), (1, 0), (1, 1), (2, 0)]


class Signal:

    def __init__(self, sem, per=1, primed=0):
        self.sem, self.per, self.primed = sem, per, primed

    def at(self, step, n=None):
        return self.sem, step * self.per + (self.per if n is None else n) + self.primed

    def before(self, step):
        return self.sem, step * self.per + self.primed

    def prime(self, eng):
        eng.sem_inc(self.sem, self.primed)


def wait_apart(eng, passed, sem, value):
    eng.wait_ge(sem, value)
    eng.sem_inc(passed.sem, 1)


class Chain:

    def __init__(self, eng, links, step):
        self.eng, self.links, self.step, self.n = eng, links, step, 0

    def link(self, ins, apart=None):
        self.n += 1
        ins.then_inc(self.links.sem, 1)
        if apart:
            wait_apart(self.eng, apart, *self.links.at(self.step, self.n))
        else:
            self.eng.wait_ge(*self.links.at(self.step, self.n))

    def close(self):
        assert self.n == self.links.per, (self.links.sem, self.n)


def decoder_kernel(nc, a, out, parts_dram):
    with ExitStack() as ctx:
        def sb(name, shape, dt=F32, scope=ctx):
            return scope.enter_context(nc.sbuf_tensor(name, shape, dt))

        def signal(name, per=1, primed=0):
            return Signal(ctx.enter_context(nc.semaphore(name)), per, primed)

        bank = [ctx.enter_context(nc.psum_tensor(f"bank{i}", [P, 512], F32)) for i in range(8)]

        square = ["L0_attn_wqT", "L0_attn_wkT", "L0_attn_wvT", "L0_attn_woT", "L0_attn_lin1T", "L0_attn_lin2T",
                  "L0_xattn_wqT", "L0_xattn_wkT", "L0_xattn_wvT", "L0_xattn_woT",
                  "L1_attn_W_Q", "L1_attn_W_K", "L1_attn_W_V"]
        w = {n: sb("w_" + n, [P, P]) for n in square}
        w1T = sb("w1T", [P, HID])
        w2 = sb("w2", [P, HID])
        w2T = sb("w2T", [P, FC, P])
        w1T_new = sb("w1T_new", [P, HID])
        w2T_new = sb("w2T_new", [P, FC, P])
        b1 = sb("b1", [P, FC])
        b1_new = sb("b1_new", [P, FC])
        b2 = sb("b2", [P, 1])
        b2_new = sb("b2_new", [P, 1])
        b1_rows = sb("b1_rows", [P, HID])
        rate = sb("rate", [P, 4])
        router = sb("router", [P, E])
        moe_w1 = sb("moe_w1", [P, E, HID])
        moe_w2 = sb("moe_w2", [P, E, FC, P])
        x_bq = sb("x_bq", [P, 1])
        x_bk = sb("x_bk", [P, 1])
        x_bv_rows = sb("x_bv_rows", [P, P])
        x_bo_rows = sb("x_bo_rows", [P, P])
        gates_w = sb("gates_w", [P, NB, 3, 32 + NB * H2])
        gates_b = sb("gates_b", [32 + NB * H2, 1])
        out_w_rows = sb("out_w_rows", [P, P])
        ffn_gw = sb("ffn_gw", [P, E])
        ffn_gb_rows = sb("ffn_gb_rows", [P, E])
        ffn_w = sb("ffn_w", [P, E * P])
        ffn_b = sb("ffn_b", [1, E * P])
        ident = sb("ident", [P, P])
        ident_b = sb("ident_b", [P, P], BF16)
        ones = sb("ones", [P, P])
        ones_b = sb("ones_b", [P, P], BF16)
        before_b = sb("before_b", [P, P], BF16)
        future_b = sb("future_b", [P, P], BF16)
        past_b = sb("past_b", [P, P], BF16)
        window = sb("window", [P, KB])
        mem_mask = sb("mem_mask", [M, M])
        head_sel = sb("head_sel", [96, H1, P], BF16)
        row_sel = sb("row_sel", [96, P], BF16)
        iota_e = sb("iota_e", [P, E])
        eps = sb("eps", [P, 1])
        vT_all = sb("vT_all", [P, STEPS * T])
        hT = sb("hT", [P, FC, T + M])

        load_w = signal("load_w", 16)
        passed = signal("passed")
        const_ready = signal("const_ready")
        zeros_made = signal("zeros_made", 6)
        masks_made = signal("masks_made", 11)
        sums_zero = signal("sums_zero")
        dve_pro = signal("dve_pro", 3)

        xin_loaded = signal("xin_loaded", 16)
        xtok_loaded = signal("xtok_loaded", 16)
        mem_qk = signal("mem_qk")
        mem_q_done = signal("mem_q_done")
        mem_k_done = signal("mem_k_done")
        qk_ready = signal("qk_ready")
        v_ready = signal("v_ready")
        q_copied = signal("q_copied", 1)
        v_copied = signal("v_copied", 6)
        k_copied = signal("k_copied", 2)
        k_copied_too = signal("k_copied_too", 2)
        NU = NB * QC + 1
        scores_a = signal("scores_a", NU)
        max_a = signal("max_a", NU)
        exp_a = signal("exp_a", NU)
        norm_a = signal("norm_a", NU)
        pT_a = signal("pT_a", NU)
        pTa_copied = signal("pTa_copied", NU)
        pTb_copied = signal("pTb_copied", NU)
        pv_a = signal("pv_a", NU)
        oT_copied = signal("oT_copied", 2)
        swa_ready = signal("swa_ready", 2)
        vT_copied = signal("vT_copied", 2)
        zT_a = signal("zT_a", FC + 1)
        hT_a = signal("hT_a", 2 * FC)
        pred_a = signal("pred_a", 1)
        e_ready = signal("e_ready", 1)
        eT_tr = signal("eT_tr", 1)
        etok_copied = signal("etok_copied", 2)
        zd_ready = signal("zd_ready", NC + 1, primed=1)
        z_biased = signal("z_biased", NC + 1)
        sg_ready = signal("sg_ready", NC + 1)
        dz_ready = signal("dz_ready", NC + 1)
        bias_summed = signal("bias_summed", NC + 1, primed=1)
        grads_ready = signal("grads_ready", NC + 1, primed=1)
        grads_added = signal("grads_added", 1, primed=1)
        dve_a = signal("dve_a", 2 * NU + 1 + 3 * (NC + 1))
        act_a = signal("act_a", NC + 1)
        upd_pe = signal("upd_pe")
        upd_dve = signal("upd_dve")
        updated = signal("updated")

        q_stack = sb("q_stack", [P, H1 // 2, T], BF16)
        k_stack = sb("k_stack", [P, H1 // 2, 2, T], BF16)
        v_aug = sb("v_aug", [P, NC, H1, 32])
        neg_max = sb("neg_max", [96, S], BF16)
        seen = sb("seen", [P, E])
        kpad2 = sb("kpad2", [P, H2, T])
        v2_aug = sb("v2_aug", [P, NC, H2, 32])
        ones16 = sb("ones16", [NB * H2, S])
        neg_pm = sb("neg_pm", [96, S], BF16)
        fb_parts = sb("fb_parts", [96, E * P], BF16)

        b_x_loaded = signal("b_x_loaded", 32)
        b_ctx_loaded = signal("b_ctx_loaded", 64 + 16 * H2)
        x_in_used = signal("x_in_used", primed=1)
        ctx_used = signal("ctx_used", primed=1)
        zT_b = signal("zT_b", FC)
        hT_b = signal("hT_b", FC)
        out_mem = signal("out_mem")
        memT_ready = signal("memT_ready")
        lin1 = signal("lin1")
        lin_ready = signal("lin_ready")
        g_ready = signal("g_ready", 2)
        merged = signal("merged")
        merged_tr = signal("merged_tr")
        LN = 6
        var_ready = signal("var_ready", LN)
        rstd_ready = signal("rstd_ready", LN)
        x_norm = signal("x_norm", LN * NC)
        x_tr = signal("x_tr", LN - 1)
        xt_ready = signal("xt_ready", LN - 1)
        masks_ready = signal("masks_ready")
        k_b = signal("k_b")
        q_b = signal("q_b")
        v_b = signal("v_b")
        kf_ready = signal("kf_ready")
        kh_ready = signal("kh_ready")
        k_parts_ready = signal("k_parts_ready")
        q_parts_ready = signal("q_parts_ready", 3)
        k_saved = signal("k_saved", 16)
        q_saved = [signal(f"q_saved{j}", 16) for j in range(3)]
        q_stacked = signal("q_stacked", 16 * 12)
        k_stacked = signal("k_stacked", 16 * 12)
        v_aug_ready = signal("v_aug_ready")
        XU = NB * H1
        s_ready = signal("s_ready", XU)
        s_read = signal("s_read", XU)
        mx_tr = signal("mx_tr", NB)
        neg_max_ready = signal("neg_max_ready", NB)
        sT_ready = signal("sT_ready", XU)
        exp_ready = signal("exp_ready", XU)
        G = 4
        pv_ready = signal("pv_ready", NB * G)
        o_copied = signal("o_copied", NB * 2)
        o_tr = signal("o_tr", NB)
        o_tok_ready = signal("o_tok_ready", NB)
        o_tok_tr = signal("o_tok_tr")
        o_T_ready = signal("o_T_ready")
        wo_ready = signal("wo_ready")
        x_plus = signal("x_plus")
        r_scored = signal("r_scored")
        share_diff = signal("share_diff")
        share_exp = signal("share_exp")
        picked = signal("picked")
        ranks = signal("ranks")
        gates_ready = signal("gates_ready")
        x_twice = signal("x_twice")
        up_ready = signal("up_ready", E * FC)
        he_ready = signal("he_ready", E * FC)
        down_ready = signal("down_ready", E)
        down_added = signal("down_added", E)
        qkv_c = signal("qkv_c")
        aq_ready = signal("aq_ready", 2)
        ak_ready = signal("ak_ready")
        as_ready = signal("as_ready", NB)
        amax_ready = signal("amax_ready", NB)
        aexp_ready = signal("aexp_ready", NB)
        apT_ready = signal("apT_ready", NB)
        apT_copied = signal("apT_copied", NB)
        apv_ready = signal("apv_ready")
        pre_ready = signal("pre_ready")
        abs_ready = signal("abs_ready")
        ef_ready = signal("ef_ready")
        ln_ready = signal("ln_ready")
        pm_ready = signal("pm_ready")
        neg_pm_ready = signal("neg_pm_ready")
        cols_ready = signal("cols_ready")
        cols_copied = signal("cols_copied", 2)
        v2_ready = signal("v2_ready")
        MU = NB * H2
        DEEP = 3
        eu_ready = signal("eu_ready", MU)
        decay_ready = signal("decay_ready", MU)
        c_ready = signal("c_ready", MU)
        pv2_ready = signal("pv2_ready", NB * 2)
        o5_copied = signal("o5_copied", NB)
        o5_tr = signal("o5_tr")
        var2_ready = signal("var2_ready")
        rstd2_ready = signal("rstd2_ready")
        rep_ready = signal("rep_ready")
        fl_ready = signal("fl_ready")
        fmax_ready = signal("fmax_ready")
        fe_ready = signal("fe_ready")
        FU = NC * 2
        f_ready = signal("f_ready", FU)
        f_act = signal("f_act", FU, primed=1)
        f_added = signal("f_added", FU, primed=1)
        out_saved = signal("out_saved", 16, primed=16)
        fb_ready = signal("fb_ready")
        dve_b = signal("dve_b", 90)
        pool_b = signal("pool_b", 2)

        scope_a = ExitStack()
        xin = sb("xin", [P, NB, KW], scope=scope_a)
        xtok = sb("xtok", [P, NC + 1, P], scope=scope_a)
        qT_mem = sb("qT_mem", [P, M], scope=scope_a)
        kpad = sb("kpad", [P, H0, NB, KW], scope=scope_a)
        stats = sb("stats", [P, 2, 16], scope=scope_a)
        oT = sb("oT", [P, T + M], scope=scope_a)
        vT_mem = sb("vT_mem", [P, M], scope=scope_a)
        eT = sb("eT", [P, T + M], scope=scope_a)
        etok = sb("etok", [P, NC + 1, P], scope=scope_a)
        grad1 = sb("grad1", [P, HID], scope=scope_a)
        grad2 = sb("grad2", [P, HID], scope=scope_a)
        dz_sum = sb("dz_sum", [P, HID], scope=scope_a)
        e_sum = sb("e_sum", [P, P], scope=scope_a)
        stage = ExitStack()
        qT = sb("qT", [P, T], scope=stage)
        vtok = sb("vtok", [P, NB, 3, P], scope=stage)
        probs = sb("probs", [P, 2, H0, KB], scope=stage)
        probsT_a = sb("probsT_a", [P, 2, H0 * P], scope=stage)
        probsT_b = sb("probsT_b", [WIN, 2, H0 * P], scope=stage)
        stage.close()
        stage = ExitStack()
        zt = sb("zt", [P, 2, HID], scope=stage)
        sg = sb("sg", [P, 2, HID], scope=stage)
        ht = sb("ht", [P, 2, HID], scope=stage)
        sl = sb("sl", [P, 2, HID], scope=stage)
        dz = sb("dz", [P, 2, HID], scope=stage)
        stage.close()
        scope_a.close()
        scope_b = ExitStack()
        x_in = sb("x_in", [P, NC, P], scope=scope_b)
        xT_in = sb("xT_in", [P, T], scope=scope_b)
        X = sb("X", [P, NC, P], scope=scope_b)
        XT = sb("XT", [P, T], scope=scope_b)
        Y = sb("Y", [P, NC, P], scope=scope_b)
        R = sb("R", [P, NC, P], scope=scope_b)
        bn = sb("bn", [P, NC, 6], scope=scope_b)
        mv = sb("mv", [P, NC, 2], scope=scope_b)
        deviation = sb("deviation", [P, NC], scope=scope_b)
        rstd = sb("rstd", [P, NC], scope=scope_b)
        ctxT = sb("ctxT", [P, T], scope=scope_b)
        ctx_tok = sb("ctx_tok", [P, NC, P], scope=scope_b)
        mask_q = sb("mask_q", [P, NC, S], U8, scope=scope_b)
        mask_k = sb("mask_k", [P, NC, S], U8, scope=scope_b)
        add_q = sb("add_q", [P, NC, S], scope=scope_b)
        add_k = sb("add_k", [P, NC, S], BF16, scope=scope_b)
        q_parts = sb("q_parts", [P, 3, T], BF16, scope=scope_b)
        k_parts = sb("k_parts", [P, 3, T], BF16, scope=scope_b)
        rec = sb("rec", [P, QC, H1], scope=scope_b)
        o_tok = sb("o_tok", [P, NC, P], scope=scope_b)
        kf, kr = XT, o_tok[:].rearrange("p c d -> p (c d)")
        logits = sb("logits", [P, NC, E], scope=scope_b)
        top = sb("top", [P, NC, 8], scope=scope_b)
        top_i = sb("top_i", [P, NC, 8], U32, scope=scope_b)
        top_f = sb("top_f", [P, NC, 2], scope=scope_b)
        pick = sb("pick", [P, 2, NC, E], scope=scope_b)
        picked_b = sb("picked_b", [P, NC, E], BF16, scope=scope_b)
        share = sb("share", [P, 4, NC], scope=scope_b)
        rank = sb("rank", [P, NC, E], scope=scope_b)
        gate = sb("gate", [P, NC, E], scope=scope_b)
        pooled = sb("pooled", [P, NB], scope=scope_b)
        pooled_rep = sb("pooled_rep", [P, NB, P], scope=scope_b)
        fl = sb("fl", [P, NB, E], scope=scope_b)
        ftop = sb("ftop", [P, NB, 8], scope=scope_b)
        fe = sb("fe", [P, NB, E], scope=scope_b)
        fs = sb("fs", [P, 2, NB], scope=scope_b)
        fgate = sb("fgate", [P, NB, E], scope=scope_b)
        stage = ExitStack()
        memT = sb("memT", [P, T], scope=stage)
        g1 = sb("g1", [P, T], scope=stage)
        g2 = sb("g2", [P, T], scope=stage)
        qr = sb("qr", [P, T], scope=stage)
        qf, o_T = g1, g2
        mx = sb("mx", [P, QC, H1], scope=stage)
        neg_r = sb("neg_r", [16, S], scope=stage)
        neg_m = sb("neg_m", [16, S], BF16, scope=stage)
        pT = sb("pT", [P, 2, 4, QC, S], scope=stage)
        o_heads = sb("o_heads", [P, 4, S], scope=stage)
        stage.close()
        stage = ExitStack()
        he = sb("he", [P, 2, FC, T], scope=stage)
        stage.close()
        stage = ExitStack()
        aq = sb("aq", [P, T], scope=stage)
        ak = sb("ak", [P, T], scope=stage)
        av = sb("av", [P, NC, P], scope=stage)
        ap = sb("ap", [P, NB, 3, P], scope=stage)
        apT = sb("apT", [P, NB, 3 * P], scope=stage)
        ast = sb("ast", [P, 4, NC], scope=stage)
        stage.close()
        stage = ExitStack()
        gi = sb("gi", [NB * H2, S], scope=stage)
        gf = sb("gf", [NB * H2, S], scope=stage)
        gl = sb("gl", [NB * H2, S], scope=stage)
        cs = sb("cs", [NB * H2, S], scope=stage)
        ga = sb("ga", [NB * H2, S], scope=stage)
        pm = sb("pm", [NB * H2, S], scope=stage)
        gm = sb("gm", [NB * H2, S], scope=stage)
        pb2 = sb("pb2", [NB * H2, S], BF16, scope=stage)
        a_col = sb("a_col", [P, NC, H2], scope=stage)
        em_col = sb("em_col", [P, NC, H2], scope=stage)
        decay = sb("decay", [P, DEEP, S + P], scope=stage)
        cT = sb("cT", [P, 2, 4, S + P], scope=stage)
        o5 = add_q[:].rearrange("p (b g) s -> p b g s", b=NB)
        den = sb("den", [P, NC, H2], scope=stage)
        hh = o_tok[:].rearrange("p c (h d) -> p c h d", d=DH2)
        hm = sb("hm", [P, 2, NC * H2], scope=stage)
        hrs = sb("hrs", [P, NC * H2], scope=stage)
        gl_act = cT[:].rearrange("p g j s -> p (g j s)")[:, 0:1024].rearrange("p (n f) -> p n f", n=2)
        stage.close()
        stage = ExitStack()
        fb_row = sb("fb_row", [1, 1, E * P], scope=stage)
        fb_m = sb("fb_m", [1, E * P], BF16, scope=stage)
        stage.close()
        scope_b.close()

        block = ctx.enter_context(nc.Block())
        units = [(b, c) for b in range(NB) for c in range(QC)] + [(0, None)]

        def s_banks(u):
            return (bank[5], bank[6]) if u % 2 == 0 else (bank[0], bank[2])

        v_banks = (bank[4], bank[7])
        mlp_banks = (bank[5], bank[6], bank[3], bank[4])

        def zd_banks(c):
            return ((bank[5], bank[6]), (bank[4], bank[2]), (bank[7], bank[1]))[c % 3]

        def q_bank(b, h):
            return bank[4 + h % 4] if b == 0 else bank[4 + h % 2]

        def m_banks(n):
            return ((bank[4], bank[6]), (bank[5], bank[7]), (bank[0], bank[1]))[n % DEEP]

        def k_bank(b, h):
            return bank[6 + h % 2] if b == 0 else bank[4 + h % 4]

        loads_w = [(w[n][:], a[n]) for n in square] + [
            (w1T[:], a["L0_attn_w1T"]), (w2[:], a["L0_attn_w2"]),
            (w2T[:], a["L0_attn_w2T"].rearrange("(k p) d -> p k d", p=P)),
            (b1[:], a["L0_attn_b1_cols"]),
            (b2[:], a["L0_attn_b2"].unsqueeze(1)),
            (b1_rows[:], a["L0_attn_b1"].partition_broadcast(P)),
            (rate[:, 0:1], a["L0_attn_alpha"].partition_broadcast(P)),
            (rate[:, 1:2], a["L0_attn_theta"].partition_broadcast(P)),
            (xtok[0:M, NC, :], a["L0_attn_mem"]),
            (xin[:, 0, 0:M], a["L0_attn_memT"]),
            (xin[:, 1, 0:M], a["L0_attn_memT"]),
        ]
        late_w = [
            (router[:], a["L0_ffn_router_wT"]),
            (moe_w1[:], a["L0_ffn_w1"].rearrange("e d f -> d e f")),
            (moe_w2[:], a["L0_ffn_w2"].rearrange("e (k p) d -> p e k d", p=P)),
            (x_bq[:], a["L0_xattn_bq"].unsqueeze(1)), (x_bk[:], a["L0_xattn_bk"].unsqueeze(1)),
            (x_bv_rows[:], a["L0_xattn_bv"].partition_broadcast(P)),
            (x_bo_rows[:], a["L0_xattn_bo"].partition_broadcast(P)),
            (out_w_rows[:], a["L1_xattn_out_w"].partition_broadcast(P)),
            (ffn_gw[:], a["L1_ffn_gate_wT"]),
            (ffn_gb_rows[:], a["L1_ffn_gate_b"].partition_broadcast(P)),
            (ffn_w[:], a["L1_ffn_expert_wT"]),
            (ffn_b[:], a["L1_ffn_expert_b"].rearrange("e o -> (e o)").unsqueeze(0)),
        ]
        for row, gate_name in ((0, "igate"), (32, "fgate")):
            for b in range(NB):
                r = slice(row + H2 * b, row + H2 * (b + 1))
                late_w.append((gates_b[r, :], a[f"L1_xattn_{gate_name}_b"].unsqueeze(1)))
                late_w.append((gates_w[:, b, :, r], a[f"L1_xattn_{gate_name}_wT"].rearrange("(j p) e -> p j e", p=P)))
        late_loaded = signal("late_loaded")

        def of_heads(n, part, s):
            return parts_dram[n, part].rearrange("(p s d) t -> s d p t", s=2, d=DH1)[s]

        @block.sync
        def _(sp):
            out_saved.prime(sp)
            for dst, src in loads_w:
                sp.dma_start(dst, src).then_inc(load_w.sem, 16)
            with sp.Fori(0, STEPS) as i:
                sp.wait_ge(*zd_ready.before(i))
                sp.dma_start(xin[:, :, M:KW], a["xT"][:, bass.ds(i * T, T)].rearrange("d (b t) -> d b t", b=NB)).then_inc(xin_loaded.sem, 16)
                sp.wait_ge(*grads_ready.before(i))
                sp.dma_start(xtok[:, 0:NC, :], a["x"].rearrange("b s d -> (b s) d")[bass.ds(i * T, T), :].rearrange("(c p) d -> p c d", p=P)).then_inc(xtok_loaded.sem, 16)
            sp.wait_ge(*updated.at(0))

            def load(i):
                rows = bass.ds(i * T, T)
                sp.wait_ge(*x_in_used.before(i))
                sp.dma_start(xT_in[:], a["xT"][:, rows]).then_inc(b_x_loaded.sem, 16)
                sp.dma_start(x_in[:], a["x"].rearrange("b s d -> (b s) d")[rows, :].rearrange("(c p) d -> p c d", p=P)).then_inc(b_x_loaded.sem, 16)
                sp.wait_ge(*ctx_used.before(i))
                sp.dma_start(ctxT[:], a["ctxT"][:, rows]).then_inc(b_ctx_loaded.sem, 16)
                sp.dma_start(ctx_tok[:], a["ctx_1024"].rearrange("b s d -> (b s) d")[rows, :].rearrange("(c p) d -> p c d", p=P)).then_inc(b_ctx_loaded.sem, 16)
                sp.dma_start(mask_q[:], a["mask_BxSxS2_bf1"].rearrange("b q k -> (b q) k")[rows, :].rearrange("(c p) k -> p c k", p=P)).then_inc(b_ctx_loaded.sem, 16)
                sp.dma_start(mask_k[:], a["maskT"].rearrange("b k q -> (b k) q")[rows, :].rearrange("(c p) q -> p c q", p=P)).then_inc(b_ctx_loaded.sem, 16)
                for h in range(H2):
                    r = slice(DH2 * h, DH2 * h + DH2)
                    sp.dma_start(kpad2[r, h, :], a["ctxT"][r, rows]).then_inc(b_ctx_loaded.sem, 16)

            def stack(i):
                sp.wait_ge(*k_parts_ready.at(i))
                sp.dma_start(parts_dram[0].rearrange("j d t -> d j t"), k_parts[:]).then_inc(k_saved.sem, 16)
                sp.wait_ge(*k_saved.at(i))
                for s in range(2):
                    for r, (_, part) in enumerate(TERMS):
                        sp.dma_start(k_stack[64 * s + DH1 * r:64 * s + DH1 * (r + 1), :, s, :], of_heads(0, part, s)).then_inc(k_stacked.sem, 16)
                for j in range(3):
                    sp.wait_ge(*q_parts_ready.at(i, j + 1))
                    sp.dma_start(parts_dram[1, j], q_parts[:, j, :]).then_inc(q_saved[j].sem, 16)
                for j in range(3):
                    sp.wait_ge(*q_saved[j].at(i))
                    for r in [r for r, term in enumerate(TERMS) if term[0] == j]:
                        for s in range(2):
                            sp.dma_start(q_stack[64 * s + DH1 * r:64 * s + DH1 * (r + 1)], of_heads(1, j, s)).then_inc(q_stacked.sem, 16)

            def save(i):
                sp.wait_ge(*x_norm.at(i))
                sp.dma_start(out.rearrange("b s d -> (b s) d")[bass.ds(i * T, T), :].rearrange("(c p) d -> p c d", p=P), Y[:]).then_inc(out_saved.sem, 16)

            load(0)
            with sp.Fori(0, STEPS - 1) as i:
                stack(i)
                load(i + 1)
                save(i)
            stack(STEPS - 1)
            save(STEPS - 1)
            sp.wait_ge(*out_saved.before(STEPS))

        @block.gpsimd
        def _(pool):
            bias_summed.prime(pool)
            def select(made, tile, op, fill, base, pattern, channel):
                made.link(pool.affine_select(out=tile, in_=tile, compare_op=op, fill=fill, base=base,
                                             pattern=pattern, channel_multiplier=channel))

            made = Chain(pool, zeros_made, 0)
            made.link(pool.memset(kpad[:], 0.0))
            pool.memset(ident[:], 0.0)
            pool.memset(window[:], 0.0)
            made.link(pool.memset(mem_mask[:], 0.0))
            select(made, ident[:], ALU.not_equal, 1.0, 0, [[-1, P]], 1)
            select(made, mem_mask[:], ALU.is_ge, NEG, 0, [[-1, M]], 1)
            select(made, window[:], ALU.is_gt, NEG, 0, [[1, KB]], -1)
            select(made, window[:], ALU.is_ge, NEG, WIN, [[-1, KB]], 1)
            made.close()
            pool.memset(ones[:], 1.0).then_inc(const_ready.sem, 1)
            pool.memset(future_b[:], 0.0)
            pool.memset(past_b[:], 0.0)
            pool.memset(before_b[:], 1.0)
            pool.memset(head_sel[:], 0.0)
            pool.memset(row_sel[:], 0.0)
            pool.memset(eps[:], EPS)
            pool.iota(iota_e[:], pattern=[[1, E]], base=0, channel_multiplier=0, allow_small_or_imprecise_dtypes=True)
            for t in (q_stack, k_stack, neg_max, neg_pm, kpad2, v_aug, v2_aug, seen, fb_parts):
                pool.memset(t[:], 0.0)
            pool.memset(ones16[:], 1.0)
            made = Chain(pool, masks_made, 0)
            made.link(pool.memset(ones_b[:], 1.0))
            pool.memset(v_aug[:, :, :, DH1:DH1 + 1], 1.0)
            pool.memset(v2_aug[:, :, :, DH2:DH2 + 1], float(DH2) ** -0.5)
            select(made, future_b[:], ALU.is_ge, NEG, 0, [[-1, P]], 1)
            select(made, past_b[:], ALU.is_ge, NEG, 0, [[1, P]], -1)
            select(made, before_b[:], ALU.is_gt, 0.0, 0, [[1, P]], -1)
            for part in range(3):
                rows = slice(32 * part, 32 * part + H1)
                select(made, head_sel[rows], ALU.not_equal, 1.0, 0, [[-1, H1], [0, P]], 1)
                select(made, row_sel[32 * part:32 * part + 1], ALU.not_equal, 1.0, 0, [[0, P]], 1)
            made.link(pool.tensor_copy(ident_b[:], ident[:]))
            made.close()
            pool.wait_ge(*sums_zero.at(0))
            with pool.Fori(0, STEPS) as i:
                for c in range(NC + 1):
                    n, s = (P if c < NC else M), c % 2
                    pool.wait_ge(*dz_ready.at(i, c + 1))
                    if c == 0:
                        pool.wait_ge(*etok_copied.at(i))
                    else:
                        pool.wait_ge(*bias_summed.at(i, c))
                    if c == 0:
                        pool.wait_ge(*bias_summed.before(i))
                    pool.tensor_tensor(e_sum[0:n], e_sum[0:n], etok[0:n, c, :], ALU.add)
                    pool.tensor_tensor(dz_sum[0:n], dz_sum[0:n], dz[0:n, s], ALU.add).then_inc(bias_summed.sem, 1)
            with pool.Fori(0, STEPS) as i:
                pool.wait_ge(*kh_ready.at(i))
                pool_chain = Chain(pool, pool_b, i)
                pool_chain.link(pool.tensor_tensor(kr, kf[:], k_parts[:, 0, :], ALU.subtract), passed)
                pool_chain.link(pool.tensor_copy(k_parts[:, 1, :], kr))
                pool.tensor_tensor(k_parts[:, 2, :], kr, k_parts[:, 1, :], ALU.subtract).then_inc(k_parts_ready.sem, 1)
                wait_apart(pool, passed, *b_ctx_loaded.at(i))
                pool.tensor_scalar(add_q[:], mask_q[:], -1.0, -NEG, ALU.add, ALU.mult)
                pool.tensor_scalar(add_k[:], mask_k[:], -1.0, -NEG, ALU.add, ALU.mult).then_inc(masks_ready.sem, 1)
                pool.wait_ge(*x_norm.at(i, NC))
                pool.tensor_tensor(R[:], X[:], x_bo_rows[:].unsqueeze(1).to_broadcast([P, NC, P]), ALU.add).then_inc(x_plus.sem, 1)
                pool.wait_ge(*x_norm.at(i, 2 * NC))
                pool.tensor_tensor(R[:], X[:], X[:], ALU.add).then_inc(x_twice.sem, 1)
                pool.tensor_scalar(v2_aug[:, :, :, 0:DH2], ctx_tok[:].rearrange("p c (h d) -> p c h d", h=H2), float(DH2) ** -0.5, None, ALU.mult).then_inc(v2_ready.sem, 1)
                pool_chain.close()

        @block.tensor
        def _(pe):
            for primed in (grads_ready, zd_ready):
                primed.prime(pe)
            pe.wait_ge(load_w.sem, 16 * len(loads_w))
            pe.wait_ge(*const_ready.at(0))
            pe.matmul(bank[1][:, 0:M], w["L0_attn_wqT"][:], xin[:, 0, 0:M], start=True, stop=True)
            pe.matmul(bank[1][:, M:2 * M], w["L0_attn_wkT"][:], xin[:, 0, 0:M], start=True, stop=True).then_inc(mem_qk.sem, 1)
            pe.wait_ge(*mem_q_done.at(0))
            pe.wait_ge(*mem_k_done.at(0))
            with pe.Fori(0, STEPS) as i:
                pe.wait_ge(*xin_loaded.at(i))
                pe.matmul(bank[5][:], w["L0_attn_wqT"][:], xin[:, :, M:KW], start=True, stop=True)
                pe.matmul(bank[6][:], w["L0_attn_wkT"][:], xin[:, :, M:KW], start=True, stop=True).then_inc(qk_ready.sem, 1)
                for b in range(NB):
                    for j, (k0, n) in enumerate([(0, P), (P, P), (2 * P, M)]):
                        last = pe.matmul(v_banks[b][0:n, j * P:(j + 1) * P], xin[:, b, k0:k0 + n],
                                         w["L0_attn_wvT"][:], start=True, stop=True)
                last.then_inc(v_ready.sem, 1)
                pe.wait_ge(*q_copied.at(i))
                pe.wait_ge(*k_copied.at(i))
                pe.wait_ge(*k_copied_too.at(i))

                def scores(u):
                    b, c = units[u]
                    if u >= 2:
                        pe.wait_ge(*max_a.at(i, u - 1))
                    for h in range(H0):
                        dst = s_banks(u)[h // 2]
                        col = (h % 2) * KB
                        if c is None:
                            last = pe.matmul(dst[0:M, col:col + M], qT_mem[:], kpad[:, h, 0, 0:M], start=True, stop=True)
                        else:
                            last = pe.matmul(dst[:, col:col + KB], qT[:, b * S + c * P:b * S + (c + 1) * P],
                                             kpad[:, h, b, c * P:c * P + KB], start=True, stop=True)
                    last.then_inc(scores_a.sem, 1)

                def transposes(u):
                    b, c = units[u]
                    if u == 0:
                        pe.wait_ge(*v_copied.at(i))
                    else:
                        pe.wait_ge(*pTa_copied.at(i, u))
                        pe.wait_ge(*pTb_copied.at(i, u))
                    wait_apart(pe, passed, *norm_a.at(i, u + 1))
                    s = u % 2
                    for h in range(H0):
                        if c is None:
                            last = pe.transpose(bank[3][0:M, h * P:h * P + M], probs[0:M, s, h, 0:M], ident[0:M, 0:M])
                        else:
                            pe.transpose(bank[3][:, h * P:(h + 1) * P], probs[:, s, h, 0:P], ident[:])
                            last = pe.transpose(bank[4][0:WIN, h * P:(h + 1) * P], probs[:, s, h, P:KB], ident[:])
                    last.then_inc(pT_a.sem, 1)

                def outputs(u):
                    b, c = units[u]
                    s = u % 2
                    pe.wait_ge(*pTb_copied.at(i, u + 1))
                    wait_apart(pe, passed, *pTa_copied.at(i, u + 1))
                    for h in range(H0):
                        r = slice(DH0 * h, DH0 * h + DH0)
                        if c is None:
                            last = pe.matmul(bank[1][r, 0:M], vtok[0:M, 0, 0, r], probsT_a[0:M, s, h * P:h * P + M], start=True, stop=True)
                        else:
                            dst = bank[7][r, (b * QC + c) * P:(b * QC + c + 1) * P]
                            pe.matmul(dst, vtok[:, b, c, r], probsT_a[:, s, h * P:(h + 1) * P], start=True, stop=False)
                            last = pe.matmul(dst, vtok[0:WIN, b, c + 1, r], probsT_b[:, s, h * P:(h + 1) * P], start=False, stop=True)
                    last.then_inc(pv_a.sem, 1)

                scores(0)
                pe.wait_ge(*grads_added.before(i))
                pe.wait_ge(*bias_summed.before(i))
                scores(1)
                for u in range(NU):
                    if u + 2 < NU:
                        scores(u + 2)
                    transposes(u)
                    outputs(u)
                pe.wait_ge(*max_a.at(i))
                for k in range(FC):
                    pe.matmul(mlp_banks[k][:], w1T[:, k * P:(k + 1) * P], xin[:, :, M:KW], start=True, stop=True).then_inc(zT_a.sem, 1)
                pe.wait_ge(*oT_copied.at(i))
                pe.matmul(bank[0][:], w["L0_attn_woT"][:], oT[:, 0:T], start=True, stop=True).then_inc(swa_ready.sem, 1)
                pe.matmul(bank[2][:, 0:M], w["L0_attn_woT"][:], oT[:, T:T + M], start=True, stop=True).then_inc(swa_ready.sem, 1)
                for k in range(FC):
                    last = pe.matmul(bank[1][:, M * (k + 1):M * (k + 2)], w1T[:, k * P:(k + 1) * P], xin[:, 0, 0:M], start=True, stop=True)
                last.then_inc(zT_a.sem, 1)
                pe.wait_ge(*hT_a.at(i))
                for k in range(FC):
                    pe.matmul(bank[3][:], w2T[:, k, :], hT[:, k, 0:T], start=(k == 0), stop=(k == FC - 1))
                for k in range(FC):
                    last = pe.matmul(bank[4][:, 0:M], w2T[:, k, :], hT[:, k, T:T + M], start=(k == 0), stop=(k == FC - 1))
                last.then_inc(pred_a.sem, 1)
                pe.wait_ge(*e_ready.at(i))
                for c in range(NC):
                    pe.transpose(bank[7][:, c * P:(c + 1) * P], eT[:, c * P:(c + 1) * P], ident[:])
                pe.transpose(bank[1][0:M, 0:P], eT[:, T:T + M], ident[:]).then_inc(eT_tr.sem, 1)
                pe.wait_ge(*vT_copied.at(i))
                pe.wait_ge(*etok_copied.at(i))

                def z_and_dh(c):
                    n = P if c < NC else M
                    zb, db = zd_banks(c)
                    if c >= 3:
                        pe.wait_ge(*dz_ready.at(i, c - 2))
                    x_c = xin[:, c // QC, M + (c % QC) * P:M + (c % QC + 1) * P] if c < NC else xin[:, 0, 0:M]
                    pe.matmul(zb[0:n], x_c, w1T[:], start=True, stop=True)
                    pe.matmul(db[0:n], eT[:, c * P:c * P + n], w2[:], start=True, stop=True).then_inc(zd_ready.sem, 1)

                for c in range(3):
                    z_and_dh(c)
                pe.wait_ge(*xtok_loaded.at(i))
                for c in range(NC + 1):
                    n, s = (P if c < NC else M), c % 2
                    pe.wait_ge(*dz_ready.at(i, c + 1))
                    pe.matmul(bank[0][:], xtok[0:n, c, :], dz[0:n, s], start=(c == 0), stop=(c == NC))
                    pe.matmul(bank[3][:], etok[0:n, c, :], ht[0:n, s], start=(c == 0), stop=(c == NC)).then_inc(grads_ready.sem, 1)
                    if c + 3 <= NC:
                        z_and_dh(c + 3)
            pe.wait_ge(*grads_added.before(STEPS))
            pe.wait_ge(*bias_summed.before(STEPS))
            for k in range(FC):
                pe.matmul(bank[1][:, k:k + 1], dz_sum[:, k * P:(k + 1) * P], ones[:, 0:1], start=True, stop=True)
            pe.matmul(bank[1][:, FC:FC + 1], e_sum[:], ones[:, 0:1], start=True, stop=True)
            for k in range(FC):
                last = pe.transpose(bank[4][:, k * P:(k + 1) * P], grad2[:, k * P:(k + 1) * P], ident[:])
            last.then_inc(upd_pe.sem, 1)
            pe.wait_ge(*updated.at(0))
            pe.wait_ge(*fb_ready.at(0))
            pe.wait_ge(late_loaded.sem, 16 * len(late_w))
            with pe.Fori(0, STEPS) as i:
                def x_transpose(n):
                    for c in range(NC):
                        pe.wait_ge(*x_norm.at(i, (n - 1) * NC + c + 1))
                        last = pe.transpose(bank[7][:, c * P:(c + 1) * P], X[:, c, :], ident[:])
                    last.then_inc(x_tr.sem, 1)
                    pe.wait_ge(*xt_ready.at(i, n))

                pe.wait_ge(*b_ctx_loaded.at(i))
                pe.matmul(bank[1][:], w["L0_xattn_wkT"][:], ctxT[:], start=True, stop=True).then_inc(k_b.sem, 1)
                for c in range(NC):
                    last = pe.matmul(bank[0][:, c * P:(c + 1) * P], ctxT[:, c * P:(c + 1) * P], w["L0_xattn_wvT"][:], start=True, stop=True)
                last.then_inc(v_b.sem, 1)
                pe.wait_ge(*f_act.before(i))
                pe.wait_ge(*b_x_loaded.at(i))
                for k in range(FC):
                    pe.matmul(bank[4 + k][:], w1T_new[:, k * P:(k + 1) * P], xT_in[:], start=True, stop=True).then_inc(zT_b.sem, 1)
                for k in range(FC):
                    pe.wait_ge(*hT_b.at(i, k + 1))
                    last = pe.matmul(bank[2][:], w2T_new[:, k, :], hT[:, k, 0:T], start=(k == 0), stop=(k == FC - 1))
                last.then_inc(out_mem.sem, 1)
                pe.matmul(bank[3][:], w["L0_attn_lin1T"][:], vT_all[:, bass.ds(i * T, T)], start=True, stop=True).then_inc(lin1.sem, 1)
                pe.wait_ge(*memT_ready.at(i))
                pe.matmul(bank[4][:], w["L0_attn_lin2T"][:], memT[:], start=True, stop=True).then_inc(lin_ready.sem, 1)
                pe.wait_ge(*merged.at(i))
                for c in range(NC):
                    last = pe.transpose(bank[5][:, c * P:(c + 1) * P], g1[:, c * P:(c + 1) * P], ident[:])
                last.then_inc(merged_tr.sem, 1)

                x_transpose(1)
                pe.wait_ge(*v_aug_ready.at(i))
                pe.matmul(bank[0][:], w["L0_xattn_wqT"][:], XT[:], start=True, stop=True).then_inc(q_b.sem, 1)
                pe.wait_ge(*k_stacked.at(i))
                pe.wait_ge(*q_stacked.at(i))
                pe.wait_ge(*masks_ready.at(i))

                def scores_q(b, h):
                    n = b * H1 + h
                    if b == 0 and h >= 4:
                        pe.wait_ge(*s_read.at(i, n - 3))
                    if b > 0 and h >= 2:
                        pe.wait_ge(*s_read.at(i, n - 1))
                    for c in range(QC):
                        last = pe.matmul(q_bank(b, h)[:, c * S:(c + 1) * S],
                                         q_stack[:, h // 2, b * S + c * P:b * S + (c + 1) * P],
                                         k_stack[:, h // 2, h % 2, b * S:(b + 1) * S], start=True, stop=True)
                    last.then_inc(s_ready.sem, 1)

                def maxima_T(b):
                    pe.wait_ge(*s_read.at(i, (b + 1) * H1))
                    for c in range(QC):
                        last = pe.transpose(bank[3][0:H1, c * P:(c + 1) * P], mx[:, c, :], ident[:])
                    last.then_inc(mx_tr.sem, 1)

                def scores_k(b, h):
                    n = b * H1 + h
                    if b == 0 and h >= 2:
                        pe.wait_ge(*exp_ready.at(i, n - 1))
                    if b > 0:
                        pe.wait_ge(*exp_ready.at(i, max(n - 3, H1)))
                    for c in range(QC):
                        dst = k_bank(b, h)[:, c * S:(c + 1) * S]
                        pe.matmul(dst, k_stack[:, h // 2, h % 2, b * S + c * P:b * S + (c + 1) * P],
                                  q_stack[:, h // 2, b * S:(b + 1) * S], start=True, stop=False)
                        pe.matmul(dst, ident_b[:], add_k[:, b * QC + c, :], start=False, stop=False)
                        last = pe.matmul(dst, head_sel[:, h, :], neg_max[:], start=False, stop=True)
                    last.then_inc(sT_ready.sem, 1)

                def values(b, g):
                    pe.wait_ge(*exp_ready.at(i, b * H1 + 4 * g + 4))
                    for c in range(QC):
                        for j in range(4):
                            last = pe.matmul(bank[g // 2][32 * j:32 * j + 32, (g % 2) * S:(g % 2 + 1) * S],
                                             v_aug[:, b * QC + c, 4 * g + j, :], pT[:, g % 2, j, c, :],
                                             start=(c == 0), stop=(c == QC - 1))
                    last.then_inc(pv_ready.sem, 1)

                def outputs_T(b):
                    pe.wait_ge(*o_copied.at(i, 2 * b + 2))
                    if b > 0:
                        pe.wait_ge(*o_tok_ready.at(i, b))
                    for g in range(G):
                        for c in range(QC):
                            last = pe.transpose(bank[2 + c][:, g * P:(g + 1) * P], o_heads[:, g, c * P:(c + 1) * P], ident[:])
                    last.then_inc(o_tr.sem, 1)

                for h in range(H1):
                    scores_q(0, h)
                maxima_T(0)
                pe.wait_ge(*neg_max_ready.at(i, 1))
                for g in range(G + 1):
                    for h in range(4 * g, 4 * g + 4):
                        if g < G:
                            scores_k(0, h)
                            scores_q(1, h)
                    if g > 0:
                        values(0, g - 1)
                maxima_T(1)
                pe.wait_ge(*neg_max_ready.at(i, 2))
                for g in range(G + 1):
                    for h in range(4 * g, 4 * g + 4):
                        if g < G:
                            scores_k(1, h)
                    if g == 0:
                        outputs_T(0)
                    if g > 0:
                        values(1, g - 1)
                outputs_T(1)
                pe.wait_ge(*o_tok_ready.at(i))
                for c in range(NC):
                    last = pe.transpose(bank[0][:, c * P:(c + 1) * P], o_tok[:, c, :], ident[:])
                last.then_inc(o_tok_tr.sem, 1)
                pe.wait_ge(*o_T_ready.at(i))
                for c in range(NC):
                    last = pe.matmul(bank[1][:, c * P:(c + 1) * P], o_T[:, c * P:(c + 1) * P], w["L0_xattn_woT"][:], start=True, stop=True)
                last.then_inc(wo_ready.sem, 1)
                x_transpose(2)

                for c in range(NC):
                    last = pe.matmul(bank[0][:, c * E:(c + 1) * E], XT[:, c * P:(c + 1) * P], router[:], start=True, stop=True)
                last.then_inc(r_scored.sem, 1)

                def up(n):
                    e, k = n // FC, n % FC
                    if n >= 4:
                        pe.wait_ge(*he_ready.at(i, n - 3))
                    pe.matmul(bank[4 + n % 4][:], moe_w1[:, e, k * P:(k + 1) * P], XT[:], start=True, stop=True).then_inc(up_ready.sem, 1)

                def down(e):
                    pe.wait_ge(*he_ready.at(i, (e + 1) * FC))
                    if e >= 2:
                        pe.wait_ge(*down_added.at(i, e - 1))
                    for c in range(NC):
                        for k in range(FC):
                            last = pe.matmul(bank[2 + e % 2][:, c * P:(c + 1) * P], he[:, e % 2, k, c * P:(c + 1) * P],
                                             moe_w2[:, e, k, :], start=(k == 0), stop=(k == FC - 1))
                    last.then_inc(down_ready.sem, 1)

                for n in range(FC):
                    up(n)
                pe.wait_ge(*picked.at(i))
                for c in range(NC):
                    for j in range(c + 1):
                        pe.matmul(bank[1][:, c * E:(c + 1) * E], before_b[:] if j == c else ones_b[:], picked_b[:, j, :],
                                  start=(j == 0), stop=(j == c))
                for j in range(NC):
                    last = pe.matmul(bank[1][:, NC * E:(NC + 1) * E], ones_b[:], picked_b[:, j, :], start=(j == 0), stop=(j == NC - 1))
                last.then_inc(ranks.sem, 1)
                for e in range(E):
                    if e + 1 < E:
                        for k in range(FC):
                            up((e + 1) * FC + k)
                    down(e)
                x_transpose(3)

                pe.matmul(bank[0][:], w["L1_attn_W_Q"][:], XT[:], start=True, stop=True)
                pe.matmul(bank[1][:], w["L1_attn_W_K"][:], XT[:], start=True, stop=True)
                for c in range(NC):
                    last = pe.matmul(bank[2][:, c * P:(c + 1) * P], XT[:, c * P:(c + 1) * P], w["L1_attn_W_V"][:], start=True, stop=True)
                last.then_inc(qkv_c.sem, 1)
                pe.wait_ge(*aq_ready.at(i, 1))
                pe.wait_ge(*ak_ready.at(i))
                for b in range(NB):
                    for c in range(QC):
                        col = c * P
                        pe.matmul(bank[4 + b][:, col:col + (c + 1) * P], aq[:, b * S + c * P:b * S + (c + 1) * P],
                                  ak[:, b * S:b * S + (c + 1) * P], start=True, stop=False)
                        last = pe.matmul(bank[4 + b][:, col + c * P:col + (c + 1) * P], ident_b[:], future_b[:], start=False, stop=True)
                    last.then_inc(as_ready.sem, 1)
                for b in range(NB):
                    pe.wait_ge(*aexp_ready.at(i, b + 1))
                    for j in range(3):
                        last = pe.transpose(bank[6 + b][:, j * P:(j + 1) * P], ap[:, b, j, :], ident[:])
                    last.then_inc(apT_ready.sem, 1)
                pe.wait_ge(*aq_ready.at(i))
                for b in range(NB):
                    pe.wait_ge(*apT_copied.at(i, b + 1))
                    pe.matmul(bank[3][:, 2 * b * P:(2 * b + 1) * P], apT[:, b, 0:P], av[:, b * QC, :], start=True, stop=True)
                    for j in range(2):
                        last = pe.matmul(bank[3][:, (2 * b + 1) * P:(2 * b + 2) * P], apT[:, b, (1 + j) * P:(2 + j) * P],
                                         av[:, b * QC + j, :], start=(j == 0), stop=(j == 1))
                last.then_inc(apv_ready.sem, 1)

                def gate_products(j):
                    for b in range(NB):
                        last = pe.matmul(bank[0][0:32 + NB * H2, 0:S], gates_w[:, b, j, :], (XT if j == 0 else ctxT)[:, b * S:(b + 1) * S],
                                         start=(j == 1 and b == 0), stop=(j == 0 and b == NB - 1))
                    return last

                gate_products(1)
                gate_products(2)
                x_transpose(4)
                last = gate_products(0)
                last.then_inc(pre_ready.sem, 1)
                wait_apart(pe, passed, *pm_ready.at(i))
                GR = NB * H2
                for c in range(QC):
                    pe.transpose(bank[1][:, c * GR:(c + 1) * GR], ga[:, c * P:(c + 1) * P], ident[0:GR, 0:GR])
                for c in range(QC):
                    last = pe.transpose(bank[1][:, (QC + c) * GR:(QC + c + 1) * GR], gm[:, c * P:(c + 1) * P], ident[0:GR, 0:GR])
                last.then_inc(cols_ready.sem, 1)
                pe.wait_ge(*neg_pm_ready.at(i))
                pe.wait_ge(*v2_ready.at(i))

                def exponents(n):
                    b, h = n // H2, n % H2
                    if n >= DEEP:
                        pe.wait_ge(*c_ready.at(i, n - DEEP + 1))
                    if n == DEEP - 1:
                        pe.wait_ge(*cols_copied.at(i))
                    eb, qb = m_banks(n)
                    for lo, q0, width, c in ((0, b * S, S, 0), (S, b * S + P, P, 1)):
                        pe.matmul(eb[:, lo:lo + width], head_sel[:, b * H2 + h, :], neg_pm[:, q0 - b * S:q0 - b * S + width], start=True, stop=False)
                        pe.matmul(eb[:, lo:lo + P], ident_b[:], past_b[:], start=False, stop=True)
                        last = pe.matmul(qb[:, lo:lo + width], kpad2[:, h, b * S + c * P:b * S + (c + 1) * P],
                                         XT[:, q0:q0 + width], start=True, stop=True)
                    last.then_inc(eu_ready.sem, 1)

                def mixed(n):
                    b, g = n // 2, n % 2
                    pe.wait_ge(*c_ready.at(i, 4 * n + 4))
                    for c, lo, q0, width in ((0, 0, 0, S), (1, S, P, P)):
                        for j in range(4):
                            last = pe.matmul(bank[2 + b][32 * j:32 * j + 32, g * S + q0:g * S + q0 + width],
                                             v2_aug[:, b * QC + c, 4 * g + j, :], cT[:, g, j, lo:lo + width],
                                             start=(c == 0), stop=(c == 1))
                    last.then_inc(pv2_ready.sem, 1)

                for n in range(MU):
                    exponents(n)
                    if n >= 5 and n % 4 == 1:
                        mixed(n // 4 - 1)
                mixed(3)
                for b in range(NB):
                    pe.wait_ge(*o5_copied.at(i, b + 1))
                    if b == 0:
                        pe.wait_ge(*c_ready.at(i))
                    for c in range(QC):
                        for g in range(2):
                            last = pe.transpose(bank[b][:, (c * 2 + g) * P:(c * 2 + g + 1) * P], o5[:, b, g, c * P:(c + 1) * P], ident[:])
                last.then_inc(o5_tr.sem, 1)
                x_transpose(5)

                pe.wait_ge(*rep_ready.at(i))
                for b in range(NB):
                    last = pe.matmul(bank[0][:, b * E:(b + 1) * E], pooled_rep[:, b, :], ffn_gw[:], start=True, stop=True)
                last.then_inc(fl_ready.sem, 1)
                for n in range(FU):
                    c, half = n // 2, n % 2
                    if n >= 4:
                        pe.wait_ge(*f_act.at(i, n - 3))
                    pe.matmul(bank[4 + n % 4][:], XT[:, c * P:(c + 1) * P], ffn_w[:, half * 512:(half + 1) * 512], start=True, stop=False)
                    pe.matmul(bank[4 + n % 4][:], row_sel[:], fb_parts[:, half * 512:(half + 1) * 512], start=False, stop=True).then_inc(f_ready.sem, 1)

        @block.scalar
        def _(act):
            f_act.prime(act)
            act.wait_ge(*sums_zero.at(0))
            for dst, src in late_w:
                act.dma_start(dst, src).then_inc(late_loaded.sem, 16)
            act.wait_ge(*mem_qk.at(0))
            act.copy(qT_mem[:], bank[1][:, 0:M]).then_inc(mem_q_done.sem, 1)
            with act.Fori(0, STEPS) as i:
                act.wait_ge(*qk_ready.at(i))
                act.copy(qT[:], bank[5][:]).then_inc(q_copied.sem, 1)
                for h in range(2, H0):
                    r = slice(DH0 * h, DH0 * h + DH0)
                    act.copy(kpad[r, h, :, M:KW], bank[6][r].rearrange("p (b t) -> p b t", b=NB)).then_inc(k_copied_too.sem, 1)
                act.wait_ge(*v_ready.at(i))
                for b in range(NB):
                    for j, n in enumerate([P, P, M]):
                        act.copy(vtok[0:n, b, j, :], v_banks[b][0:n, j * P:(j + 1) * P]).then_inc(v_copied.sem, 1)

                def exponentials(u):
                    n, keys, s = (M, M, u % 2) if units[u][1] is None else (P, KB, u % 2)
                    act.wait_ge(*max_a.at(i, u + 1))
                    for h in range(H0):
                        last = act.activation(probs[0:n, s, h, 0:keys], probs[0:n, s, h, 0:keys], ACT.Exp,
                                              bias=stats[0:n, s, 4 + h:5 + h], scale=float(DH0) ** -0.5,
                                              accum_out=stats[0:n, s, 8 + h:9 + h])
                    last.then_inc(exp_a.sem, 1)

                exponentials(0)
                exponentials(1)
                for u, (b, c) in enumerate(units):
                    s = u % 2
                    act.wait_ge(*pT_a.at(i, u + 1))
                    if c is None:
                        act.copy(probsT_a[0:M, s].rearrange("p (h q) -> p h q", h=H0)[:, :, 0:M],
                                 bank[3][0:M].rearrange("p (h q) -> p h q", h=H0)[:, :, 0:M]).then_inc(pTa_copied.sem, 1)
                    else:
                        act.copy(probsT_a[:, s], bank[3][:]).then_inc(pTa_copied.sem, 1)
                    if u + 2 < NU:
                        exponentials(u + 2)
                act.wait_ge(*pv_a.at(i))
                act.copy(oT[:, 0:T], bank[7][:]).then_inc(oT_copied.sem, 1)
                act.copy(oT[:, T:T + M], bank[1][:, 0:M]).then_inc(oT_copied.sem, 1)
                for k in range(FC):
                    act.wait_ge(*zT_a.at(i, k + 1))
                    act.activation(hT[:, k, 0:T], mlp_banks[k][:], ACT.Silu, bias=b1[:, k:k + 1]).then_inc(hT_a.sem, 1)
                act.wait_ge(*zT_a.at(i))
                for k in range(FC):
                    act.activation(hT[:, k, T:T + M], bank[1][:, M * (k + 1):M * (k + 2)], ACT.Silu, bias=b1[:, k:k + 1]).then_inc(hT_a.sem, 1)
                act.wait_ge(*swa_ready.at(i))
                act.copy(vT_mem[:], bank[2][:, 0:M]).then_inc(vT_copied.sem, 1)
                act.wait_ge(*eT_tr.at(i))
                act.copy(etok[:, 0:NC, :], bank[7][:].rearrange("p (c d) -> p c d", c=NC)).then_inc(etok_copied.sem, 1)
                act.copy(etok[0:M, NC, :], bank[1][0:M, 0:P]).then_inc(etok_copied.sem, 1)
                chain = Chain(act, act_a, i)
                for c in range(NC + 1):
                    n, s = (P if c < NC else M), c % 2
                    act.wait_ge(*z_biased.at(i, c + 1))
                    if c >= 2:
                        act.wait_ge(*dz_ready.at(i, c - 1))
                    chain.link(act.activation(sg[0:n, s], zt[0:n, s], ACT.Tanh, scale=0.5))
                    act.activation(sg[0:n, s], sg[0:n, s], ACT.Copy, scale=0.5, bias=0.5).then_inc(sg_ready.sem, 1)
                chain.close()
            with act.Fori(0, STEPS) as i:
                def root(n):
                    act.wait_ge(*var_ready.at(i, n))
                    act.activation(deviation[:], mv[:, :, 1], ACT.Sqrt, bias=eps[:, 0:1]).then_inc(rstd_ready.sem, 1)

                def x_copy(n):
                    root(n)
                    act.wait_ge(*x_tr.at(i, n))
                    act.copy(XT[:], bank[7][:]).then_inc(xt_ready.sem, 1)

                act.wait_ge(*k_b.at(i))
                act.activation(kf[:], bank[1][:], ACT.Identity, bias=x_bk[:, 0:1]).then_inc(kf_ready.sem, 1)
                act.wait_ge(*kf_ready.at(i))
                act.copy(k_parts[:, 0, :], kf[:]).then_inc(kh_ready.sem, 1)
                for k in range(FC):
                    act.wait_ge(*zT_b.at(i, k + 1))
                    act.activation(hT[:, k, 0:T], bank[4 + k][:], ACT.Silu, bias=b1_new[:, k:k + 1]).then_inc(hT_b.sem, 1)
                act.wait_ge(*lin1.at(i))
                act.activation(g1[:], bank[3][:], ACT.Tanh, scale=0.5).then_inc(g_ready.sem, 1)
                act.wait_ge(*lin_ready.at(i))
                act.activation(g2[:], bank[4][:], ACT.Tanh, scale=0.5).then_inc(g_ready.sem, 1)
                act.wait_ge(*k_parts_ready.at(i))
                x_copy(1)
                for b in range(NB):
                    for h in range(H1):
                        n = b * H1 + h
                        g, j = h // 4, h % 4
                        act.wait_ge(*sT_ready.at(i, n + 1))
                        if h % 4 == 0 and b * G + g >= 2:
                            act.wait_ge(*pv_ready.at(i, b * G + g - 1))
                        act.activation(pT[:, g % 2, j], k_bank(b, h)[:].rearrange("p (c q) -> p c q", c=QC), ACT.Exp).then_inc(exp_ready.sem, 1)
                    for half in range(2):
                        act.wait_ge(*pv_ready.at(i, b * G + 2 * half + 2))
                        if b > 0 and half == 0:
                            act.wait_ge(*o_tr.at(i, b))
                        act.copy(o_heads[:, 2 * half:2 * half + 2, :], bank[half][:].rearrange("p (g q) -> p g q", g=2)).then_inc(o_copied.sem, 1)
                act.wait_ge(*o_tok_tr.at(i))
                act.copy(o_T[:], bank[0][:]).then_inc(o_T_ready.sem, 1)
                x_copy(2)
                act.wait_ge(*share_diff.at(i))
                act.activation(share[:, 1, :], share[:, 0, :], ACT.Exp).then_inc(share_exp.sem, 1)
                for n in range(E * FC):
                    e, k = n // FC, n % FC
                    act.wait_ge(*up_ready.at(i, n + 1))
                    if k == 0 and e >= 2:
                        act.wait_ge(*down_ready.at(i, e - 1))
                    act.activation(he[:, e % 2, k, :], bank[4 + n % 4][:], ACT.Silu).then_inc(he_ready.sem, 1)
                x_copy(3)
                act.wait_ge(*qkv_c.at(i))
                act.copy(aq[:], bank[0][:]).then_inc(aq_ready.sem, 1)
                act.copy(av[:], bank[2][:].rearrange("p (c d) -> p c d", c=NC)).then_inc(aq_ready.sem, 1)
                scale = float(D) ** -0.5
                for b in range(NB):
                    act.wait_ge(*amax_ready.at(i, b + 1))
                    act.activation(ap[:, b, 0, :], bank[4 + b][:, 0:P], ACT.Exp, bias=ast[:, 1, 2 * b:2 * b + 1], scale=scale,
                                   accum_out=ast[:, 2, 2 * b:2 * b + 1])
                    act.activation(ap[:, b, 1:3, :], bank[4 + b][:, P:3 * P].rearrange("p (j k) -> p j k", j=2), ACT.Exp,
                                   bias=ast[:, 1, 2 * b + 1:2 * b + 2], scale=scale,
                                   accum_out=ast[:, 2, 2 * b + 1:2 * b + 2]).then_inc(aexp_ready.sem, 1)
                for b in range(NB):
                    act.wait_ge(*apT_ready.at(i, b + 1))
                    act.copy(apT[:, b, :], bank[6 + b][:, 0:3 * P]).then_inc(apT_copied.sem, 1)
                x_copy(4)
                act.wait_ge(*abs_ready.at(i))
                act.activation(cs[:], gl[:], ACT.Exp, scale=-1.0).then_inc(ef_ready.sem, 1)
                act.wait_ge(*ef_ready.at(i))
                act.activation(gl[:], cs[:], ACT.Ln, bias=1.0).then_inc(ln_ready.sem, 1)
                act.wait_ge(*cols_ready.at(i))
                cols = bank[1][:, 0:2 * NC * H2].rearrange("p (n c b h) -> p n c b h", n=2, c=QC, b=NB)
                act.copy(a_col[:].rearrange("p (b c) h -> p c b h", b=NB), cols[:, 0]).then_inc(cols_copied.sem, 1)
                act.activation(em_col[:].rearrange("p (b c) h -> p c b h", b=NB), cols[:, 1], ACT.Exp, scale=-1.0).then_inc(cols_copied.sem, 1)
                act.wait_ge(*cols_copied.at(i, 1))
                for n in range(MU):
                    b, h = n // H2, n % H2
                    act.wait_ge(*eu_ready.at(i, n + 1))
                    if n >= DEEP:
                        act.wait_ge(*c_ready.at(i, n - DEEP + 1))
                    eb = m_banks(n)[0]
                    act.activation(decay[:, n % DEEP, 0:S], eb[:, 0:S], ACT.Exp, bias=a_col[:, b * QC, h:h + 1])
                    act.activation(decay[:, n % DEEP, S:S + P], eb[:, S:S + P], ACT.Exp, bias=a_col[:, b * QC + 1, h:h + 1]).then_inc(decay_ready.sem, 1)
                for b in range(NB):
                    act.wait_ge(*pv2_ready.at(i, 2 * b + 2))
                    act.copy(o5[:, b], bank[2 + b][:].rearrange("p (g q) -> p g q", g=2)).then_inc(o5_copied.sem, 1)
                act.wait_ge(*var2_ready.at(i))
                act.activation(hrs[:], hm[:, 0, :], ACT.Sqrt, bias=eps[:, 0:1], scale=1.0 / DH2).then_inc(rstd2_ready.sem, 1)
                x_copy(5)
                act.wait_ge(*fmax_ready.at(i))
                act.activation(fe[:], fl[:], ACT.Exp).then_inc(fe_ready.sem, 1)
                for n in range(FU):
                    act.wait_ge(*f_ready.at(i, n + 1))
                    if n >= 2:
                        act.wait_ge(*f_added.at(i, n - 1))
                    act.activation(gl_act[:, n % 2], bank[4 + n % 4][:], ACT.Gelu).then_inc(f_act.sem, 1)
                root(6)

        @block.vector
        def _(dve):
            for primed in (grads_added, f_added, x_in_used, ctx_used):
                primed.prime(dve)
            for t in (gates_w, dz_sum, e_sum, grad1, grad2):
                last = dve.memset(t[:], 0.0)
            last.then_inc(sums_zero.sem, 1)
            dve.wait_ge(*zeros_made.at(0, 1))
            dve.wait_ge(*mem_q_done.at(0))
            for h in range(H0):
                r = slice(DH0 * h, DH0 * h + DH0)
                for b in range(NB):
                    last = dve.tensor_copy(kpad[r, h, b, 0:M], bank[1][r, M:2 * M])
            last.then_inc(mem_k_done.sem, 1)
            dve.wait_ge(*const_ready.at(0))
            with dve.Fori(0, STEPS) as i:
                chain = Chain(dve, dve_a, i)
                dve.wait_ge(*qk_ready.at(i))
                for h in range(2):
                    r = slice(DH0 * h, DH0 * h + DH0)
                    dve.tensor_copy(kpad[r, h, :, M:KW], bank[6][r].rearrange("p (b t) -> p b t", b=NB)).then_inc(k_copied.sem, 1)

                def maxima(u):
                    b, c = units[u]
                    n, keys, s = (M, M, u % 2) if c is None else (P, KB, u % 2)
                    if u >= 2:
                        dve.wait_ge(*pT_a.at(i, u - 1))
                    wait_apart(dve, passed, *scores_a.at(i, u + 1))
                    mask = mem_mask if c is None else window
                    for h in range(H0):
                        src = s_banks(u)[h // 2][0:n, (h % 2) * KB:(h % 2) * KB + keys]
                        last = dve.tensor_tensor_reduce(probs[0:n, s, h, 0:keys], src, mask[0:n, 0:keys], 1.0, NEG,
                                                        ALU.add, ALU.max, stats[0:n, s, h:h + 1])
                    chain.link(last)
                    dve.tensor_scalar(stats[0:n, s, 4:8], stats[0:n, s, 0:4], -float(DH0) ** -0.5, None, ALU.mult).then_inc(max_a.sem, 1)

                def normalise(u):
                    n, keys, s = (M, M, u % 2) if units[u][1] is None else (P, KB, u % 2)
                    dve.wait_ge(*exp_a.at(i, u + 1))
                    chain.link(dve.reciprocal(stats[0:n, s, 12:16], stats[0:n, s, 8:12]))
                    dve.tensor_tensor(probs[0:n, s, :, 0:keys], probs[0:n, s, :, 0:keys],
                                      stats[0:n, s, 12:16].unsqueeze(2).to_broadcast([n, H0, keys]), ALU.mult).then_inc(norm_a.sem, 1)

                maxima(0)
                maxima(1)
                normalise(0)
                for u, (b, c) in enumerate(units):
                    s = u % 2
                    dve.wait_ge(*pT_a.at(i, u + 1))
                    if c is None:
                        dve.memset(probsT_b[:, s, 0:1], 0.0).then_inc(pTb_copied.sem, 1)
                    else:
                        dve.tensor_copy(probsT_b[:, s], bank[4][0:WIN]).then_inc(pTb_copied.sem, 1)
                    if u + 2 < NU:
                        maxima(u + 2)
                    if u + 1 < NU:
                        normalise(u + 1)
                dve.wait_ge(*swa_ready.at(i, 1))
                dve.tensor_copy(vT_all[:, bass.ds(i * T, T)], bank[0][:]).then_inc(vT_copied.sem, 1)
                dve.wait_ge(*vT_copied.at(i))
                dve.wait_ge(*pred_a.at(i))
                dve.scalar_tensor_tensor(eT[:, 0:T], bank[3][:], b2[:, 0:1], vT_all[:, bass.ds(i * T, T)], ALU.add, ALU.subtract)
                chain.link(dve.scalar_tensor_tensor(eT[:, T:T + M], bank[4][:, 0:M], b2[:, 0:1], vT_mem[:], ALU.add, ALU.subtract))
                dve.tensor_scalar(eT[:, T:T + M], eT[:, T:T + M], float(NB), None, ALU.mult).then_inc(e_ready.sem, 1)
                def biased(c):
                    n, s = (P if c < NC else M), c % 2
                    dve.wait_ge(*zd_ready.at(i, c + 1))
                    dve.tensor_tensor(zt[0:n, s], zd_banks(c)[0][0:n], b1_rows[0:n], ALU.add).then_inc(z_biased.sem, 1)

                biased(0)
                for c in range(NC + 1):
                    n, s = (P if c < NC else M), c % 2
                    if c < NC:
                        biased(c + 1)
                    dve.wait_ge(*sg_ready.at(i, c + 1))
                    if c >= 2:
                        dve.wait_ge(*grads_ready.at(i, c - 1))
                        dve.wait_ge(*bias_summed.at(i, c - 1))
                    chain.link(dve.tensor_tensor(ht[0:n, s], zt[0:n, s], sg[0:n, s], ALU.mult))
                    chain.link(dve.scalar_tensor_tensor(sl[0:n, s], sg[0:n, s], -1.0, ht[0:n, s], ALU.add, ALU.mult))
                    chain.link(dve.tensor_tensor(sl[0:n, s], sg[0:n, s], sl[0:n, s], ALU.subtract))
                    dve.tensor_tensor(dz[0:n, s], zd_banks(c)[1][0:n], sl[0:n, s], ALU.mult).then_inc(dz_ready.sem, 1)
                dve.wait_ge(*grads_ready.at(i))
                dve.tensor_tensor(grad1[:], grad1[:], bank[0][:], ALU.add)
                dve.tensor_tensor(grad2[:], grad2[:], bank[3][:], ALU.add).then_inc(grads_added.sem, 1)
                chain.close()
            dve.tensor_scalar(rate[:, 2:3], rate[:, 0:1], -1.0, 1.0, ALU.mult, ALU.add)
            dve.tensor_scalar(rate[:, 3:4], rate[:, 1:2], -1.0, None, ALU.mult).then_inc(upd_dve.sem, 1)
            dve.wait_ge(upd_dve.sem, 1)
            dve.wait_ge(*upd_pe.at(0))
            pairs = [(w1T_new[:], w1T[:], grad1[:]),
                     (w2T_new[:].rearrange("p k d -> p (k d)"), w2T[:].rearrange("p k d -> p (k d)"), bank[4][:]),
                     (b1_new[:], b1[:], bank[1][:, 0:FC]), (b2_new[:], b2[:], bank[1][:, FC:FC + 1])]
            for new, old, grad in pairs:
                last = dve.tensor_scalar(new, old, rate[:, 2:3], None, ALU.mult)
            last.then_inc(upd_dve.sem, 1)
            dve.wait_ge(upd_dve.sem, 2)
            for new, old, grad in pairs:
                last = dve.scalar_tensor_tensor(new, grad, rate[:, 3:4], new, ALU.mult, ALU.add)
            last.then_inc(updated.sem, 1)
            dve.wait_ge(late_loaded.sem, 16 * len(late_w))
            pro = Chain(dve, dve_pro, 0)
            pro.link(dve.tensor_copy(fb_parts[0:1, :], ffn_b[:]))
            pro.link(dve.tensor_tensor(fb_row[:, 0], ffn_b[:], fb_parts[0:1, :], ALU.subtract))
            pro.link(dve.tensor_copy(fb_m[:], fb_row[:, 0]))
            dve.tensor_copy(fb_parts[32:33, :], fb_m[:])
            dve.tensor_tensor(fb_parts[64:65, :], fb_row[:, 0], fb_m[:], ALU.subtract).then_inc(fb_ready.sem, 1)
            with dve.Fori(0, STEPS) as i:
                chain = Chain(dve, dve_b, i)

                def layernorm(n, dst):
                    for c in range(NC):
                        last = dve.bn_stats(bn[:, c, :], R[:, c, :])
                    chain.link(last, passed)
                    for c in range(NC):
                        last = dve.bn_aggr(mv[:, c, :], bn[:, c, :])
                    last.then_inc(var_ready.sem, 1)
                    dve.wait_ge(*rstd_ready.at(i, n))
                    chain.link(dve.reciprocal(rstd[:], deviation[:]))
                    for c in range(NC):
                        dve.tensor_scalar(dst[:, c, :], R[:, c, :], mv[:, c, 0:1], rstd[:, c:c + 1], ALU.subtract, ALU.mult).then_inc(x_norm.sem, 1)

                dve.wait_ge(*v_b.at(i))
                dve.tensor_tensor(v_aug[:, :, :, 0:DH1], bank[0][:].rearrange("p (c h d) -> p c h d", c=NC, h=H1),
                                  x_bv_rows[:].rearrange("p (h d) -> p h d", h=H1).unsqueeze(1).to_broadcast([P, NC, H1, DH1]), ALU.add).then_inc(v_aug_ready.sem, 1)
                dve.wait_ge(*out_mem.at(i))
                dve.tensor_scalar(memT[:], bank[2][:], b2_new[:, 0:1], None, ALU.add).then_inc(memT_ready.sem, 1)
                dve.wait_ge(*g_ready.at(i, 1))
                dve.scalar_tensor_tensor(g1[:], g1[:], 1.0, vT_all[:, bass.ds(i * T, T)], ALU.add, ALU.mult)
                dve.wait_ge(*g_ready.at(i))
                chain.link(dve.scalar_tensor_tensor(g2[:], g2[:], 1.0, memT[:], ALU.add, ALU.mult))
                dve.tensor_tensor(g1[:], g1[:], g2[:], ALU.add).then_inc(merged.sem, 1)
                dve.wait_ge(*merged_tr.at(i))
                r_done = dve.scalar_tensor_tensor(R[:], bank[5][:].rearrange("p (c d) -> p c d", c=NC), 0.5, x_in[:], ALU.mult, ALU.add)
                r_done.then_inc(x_in_used.sem, 1)
                dve.wait_ge(*x_in_used.at(i))
                layernorm(1, X)

                dve.wait_ge(*q_b.at(i))
                chain.link(dve.tensor_scalar(qf[:], bank[0][:], x_bq[:, 0:1], float(DH1) ** -0.5, ALU.add, ALU.mult))
                dve.tensor_copy(q_parts[:, 0, :], qf[:]).then_inc(q_parts_ready.sem, 1)
                dve.wait_ge(*q_parts_ready.at(i, 1))
                chain.link(dve.tensor_tensor(qr[:], qf[:], q_parts[:, 0, :], ALU.subtract))
                dve.tensor_copy(q_parts[:, 1, :], qr[:]).then_inc(q_parts_ready.sem, 1)
                dve.wait_ge(*q_parts_ready.at(i, 2))
                dve.tensor_tensor(q_parts[:, 2, :], qr[:], q_parts[:, 1, :], ALU.subtract).then_inc(q_parts_ready.sem, 1)
                dve.wait_ge(*masks_ready.at(i))
                for b in range(NB):
                    for h in range(H1):
                        wait_apart(dve, passed, *s_ready.at(i, b * H1 + h + 1))
                        for c in range(QC):
                            sc = q_bank(b, h)[:, c * S:(c + 1) * S]
                            last = dve.tensor_tensor_reduce(sc, sc, add_q[:, b * QC + c, :], 1.0,
                                                            2.0 * NEG, ALU.add, ALU.max, mx[:, c, h:h + 1])
                        last.then_inc(s_read.sem, 1)
                    dve.wait_ge(*mx_tr.at(i, b + 1))
                    if b > 0:
                        dve.wait_ge(*sT_ready.at(i, b * H1))
                    mt = bank[3][0:H1, 0:S]
                    chain.link(dve.tensor_scalar(neg_max[0:H1, :], mt, -1.0, None, ALU.mult))
                    chain.link(dve.scalar_tensor_tensor(neg_r[:], mt, -1.0, neg_max[0:H1, :], ALU.mult, ALU.subtract))
                    chain.link(dve.tensor_copy(neg_m[:], neg_r[:]))
                    dve.tensor_copy(neg_max[32:32 + H1, :], neg_m[:])
                    dve.tensor_tensor(neg_max[64:64 + H1, :], neg_r[:], neg_m[:], ALU.subtract).then_inc(neg_max_ready.sem, 1)
                for b in range(NB):
                    dve.wait_ge(*o_tr.at(i, b + 1))
                    heads = [bank[2 + c][:].rearrange("p (h j) -> p h j", h=H1) for c in range(QC)]
                    for c in range(QC):
                        last = dve.reciprocal(rec[:, c, :], heads[c][:, :, DH1])
                    chain.link(last)
                    for c in range(QC):
                        last = dve.tensor_tensor(o_tok[:, b * QC + c, :].rearrange("p (h d) -> p h d", h=H1), heads[c][:, :, 0:DH1],
                                                 rec[:, c, :].unsqueeze(2).to_broadcast([P, H1, DH1]), ALU.mult)
                    last.then_inc(o_tok_ready.sem, 1)
                dve.wait_ge(*wo_ready.at(i))
                dve.wait_ge(*x_plus.at(i))
                chain.link(dve.tensor_tensor(R[:], R[:], bank[1][:].rearrange("p (c d) -> p c d", c=NC), ALU.add))
                layernorm(2, X)

                dve.wait_ge(*r_scored.at(i))
                chain.link(dve.tensor_copy(logits[:], bank[0][:, 0:NC * E].rearrange("p (c e) -> p c e", c=NC)), passed)
                for c in range(NC):
                    last = dve.max(top[:, c, :], logits[:, c, :])
                chain.link(last, passed)
                for c in range(NC):
                    last = dve.max_index(top_i[:, c, :], top[:, c, :], logits[:, c, :])
                dve.tensor_tensor(share[:, 0, :], top[:, :, 1], top[:, :, 0], ALU.subtract).then_inc(share_diff.sem, 1)
                dve.wait_ge(*share_diff.at(i))
                chain.link(dve.tensor_copy(top_f[:], top_i[:, :, 0:2]))
                for j in range(2):
                    last = dve.tensor_tensor(pick[:, j], iota_e[:].unsqueeze(1).to_broadcast([P, NC, E]),
                                             top_f[:, :, j:j + 1].to_broadcast([P, NC, E]), ALU.is_equal)
                chain.link(last)
                dve.tensor_tensor(picked_b[:], pick[:, 0], pick[:, 1], ALU.add).then_inc(picked.sem, 1)
                dve.wait_ge(*share_exp.at(i))
                chain.link(dve.tensor_scalar(share[:, 0, :], share[:, 1, :], 1.0, None, ALU.add))
                chain.link(dve.reciprocal(share[:, 2, :], share[:, 0, :]))
                chain.link(dve.tensor_tensor(share[:, 3, :], share[:, 1, :], share[:, 2, :], ALU.mult))
                for j in range(2):
                    last = dve.tensor_tensor(pick[:, j], pick[:, j], share[:, 2 + j, :].unsqueeze(2).to_broadcast([P, NC, E]), ALU.mult)
                dve.wait_ge(*ranks.at(i))
                chain.link(dve.tensor_tensor(rank[:], bank[1][:, 0:NC * E].rearrange("p (c e) -> p c e", c=NC),
                                             seen[:].unsqueeze(1).to_broadcast([P, NC, E]), ALU.add))
                dve.tensor_tensor(seen[:], bank[1][:, NC * E:(NC + 1) * E], seen[:], ALU.add)
                chain.link(dve.tensor_tensor(gate[:], pick[:, 0], pick[:, 1], ALU.add))
                dve.scalar_tensor_tensor(gate[:], rank[:], float(CAP), gate[:], ALU.is_lt, ALU.mult).then_inc(gates_ready.sem, 1)
                dve.wait_ge(*gates_ready.at(i))
                dve.wait_ge(*x_twice.at(i))
                for e in range(E):
                    dve.wait_ge(*down_ready.at(i, e + 1))
                    for c in range(NC):
                        last = dve.scalar_tensor_tensor(R[:, c, :], bank[2 + e % 2][:, c * P:(c + 1) * P], gate[:, c, e:e + 1],
                                                        R[:, c, :], ALU.mult, ALU.add)
                    last.then_inc(down_added.sem, 1)
                    dve.wait_ge(*down_added.at(i, e + 1))
                layernorm(3, X)

                dve.wait_ge(*qkv_c.at(i))
                dve.tensor_copy(ak[:], bank[1][:]).then_inc(ak_ready.sem, 1)
                for b in range(NB):
                    dve.wait_ge(*as_ready.at(i, b + 1))
                    dve.tensor_reduce(ast[:, 0, 2 * b:2 * b + 1], bank[4 + b][:, 0:P], AX.X, ALU.max)
                    chain.link(dve.tensor_reduce(ast[:, 0, 2 * b + 1:2 * b + 2], bank[4 + b][:, P:3 * P], AX.X, ALU.max))
                    dve.tensor_scalar(ast[:, 1, 2 * b:2 * b + 2], ast[:, 0, 2 * b:2 * b + 2], -float(D) ** -0.5, None, ALU.mult).then_inc(amax_ready.sem, 1)
                dve.wait_ge(*aexp_ready.at(i))
                chain.link(dve.reciprocal(ast[:, 3, :], ast[:, 2, :]))
                dve.wait_ge(*apv_ready.at(i))
                for c in range(NC):
                    last = dve.scalar_tensor_tensor(R[:, c, :], bank[3][:, c * P:(c + 1) * P], ast[:, 3, c:c + 1], X[:, c, :], ALU.mult, ALU.add)
                chain.link(last)
                layernorm(4, X)

                dve.wait_ge(*pre_ready.at(i))
                GR = NB * H2
                dve.tensor_scalar(gi[:], bank[0][0:GR, 0:S], gates_b[0:GR, 0:1], None, ALU.add)
                chain.link(dve.tensor_scalar(gf[:], bank[0][32:32 + GR, 0:S], gates_b[32:32 + GR, 0:1], None, ALU.add))
                dve.scalar_tensor_tensor(gl[:], gf[:], -1.0, gf[:], ALU.mult, ALU.max).then_inc(abs_ready.sem, 1)
                dve.wait_ge(*ln_ready.at(i))
                chain.link(dve.scalar_tensor_tensor(gf[:], gf[:], 0.0, gl[:], ALU.min, ALU.subtract))
                chain.link(dve.tensor_tensor_scan(cs[:], ones16[:], gf[:], 0.0, ALU.mult, ALU.add))
                chain.link(dve.tensor_tensor(ga[:], gi[:], cs[:], ALU.subtract))
                chain.link(dve.tensor_tensor_scan(pm[:], ones16[:], ga[:], NEG, ALU.mult, ALU.max))
                dve.tensor_tensor(gm[:], cs[:], pm[:], ALU.add).then_inc(pm_ready.sem, 1)
                chain.link(dve.tensor_scalar(neg_pm[0:GR, :], pm[:], -1.0, None, ALU.mult))
                chain.link(dve.scalar_tensor_tensor(gi[:], pm[:], -1.0, neg_pm[0:GR, :], ALU.mult, ALU.subtract))
                chain.link(dve.tensor_copy(pb2[:], gi[:]))
                dve.tensor_copy(neg_pm[32:32 + GR, :], pb2[:])
                dve.tensor_tensor(neg_pm[64:64 + GR, :], gi[:], pb2[:], ALU.subtract).then_inc(neg_pm_ready.sem, 1)
                for n in range(MU):
                    b, g, j = n // H2, (n // 4) % 2, n % 4
                    dve.wait_ge(*decay_ready.at(i, n + 1))
                    if n >= 8 and n % 4 == 0:
                        dve.wait_ge(*pv2_ready.at(i, n // 4 - 1))
                    dve.tensor_tensor(cT[:, g, j, :], m_banks(n)[1][:, 0:S + P], decay[:, n % DEEP, :], ALU.mult).then_inc(c_ready.sem, 1)
                dve.wait_ge(*o5_tr.at(i))
                dve.wait_ge(*cols_copied.at(i))
                for b in range(NB):
                    src = bank[b][:].rearrange("p (c h j) -> p c h j", c=QC, h=H2)
                    last = dve.tensor_copy(den[:, b * QC:(b + 1) * QC, :], src[:, :, :, DH2])
                chain.link(last)
                chain.link(dve.scalar_tensor_tensor(den[:], den[:], -1.0, den[:], ALU.mult, ALU.max))
                chain.link(dve.tensor_tensor(den[:], den[:], em_col[:], ALU.max))
                chain.link(dve.tensor_scalar(den[:], den[:], 1e-6, None, ALU.add))
                chain.link(dve.reciprocal(den[:], den[:]))
                for b in range(NB):
                    src = bank[b][:].rearrange("p (c h j) -> p c h j", c=QC, h=H2)
                    cc = slice(b * QC, (b + 1) * QC)
                    last = dve.tensor_tensor(hh[:, cc], src[:, :, :, 0:DH2], den[:, cc].unsqueeze(3).to_broadcast([P, QC, H2, DH2]), ALU.mult)
                chain.link(last)
                h3 = hh.rearrange("p c h d -> p (c h) d")
                hs3 = R[:].rearrange("p c (h d) -> p (c h) d", d=DH2)
                wide = [P, NC * H2, DH2]
                chain.link(dve.tensor_reduce(hm[:, 0, :], h3, AX.X, ALU.add))
                chain.link(dve.tensor_scalar(hm[:, 1, :], hm[:, 0, :], 1.0 / DH2, None, ALU.mult))
                chain.link(dve.tensor_tensor(h3, h3, hm[:, 1, :].unsqueeze(2).to_broadcast(wide), ALU.subtract))
                chain.link(dve.tensor_tensor(hs3, h3, h3, ALU.mult))
                dve.tensor_reduce(hm[:, 0, :], hs3, AX.X, ALU.add).then_inc(var2_ready.sem, 1)
                dve.wait_ge(*rstd2_ready.at(i))
                chain.link(dve.reciprocal(hrs[:], hrs[:]))
                chain.link(dve.tensor_tensor(h3, h3, hrs[:].unsqueeze(2).to_broadcast(wide), ALU.mult))
                hx = hh.rearrange("p c h d -> p c (h d)")
                chain.link(dve.tensor_tensor(hx, hx, out_w_rows[:].unsqueeze(1).to_broadcast([P, NC, P]), ALU.mult))
                dve.tensor_tensor(R[:], hx, X[:], ALU.add).then_inc(ctx_used.sem, 1)
                dve.wait_ge(*ctx_used.at(i))
                layernorm(5, X)

                dve.wait_ge(*xt_ready.at(i))
                chain.link(dve.tensor_reduce(pooled[:], XT[:].rearrange("p (b t) -> p b t", b=NB), AX.X, ALU.add))
                for b in range(NB):
                    last = dve.tensor_scalar(pooled_rep[:, b, :], ones[:], pooled[:, b:b + 1], 1.0 / S, ALU.mult, ALU.mult)
                last.then_inc(rep_ready.sem, 1)
                dve.wait_ge(*fl_ready.at(i))
                chain.link(dve.tensor_tensor(fl[:], bank[0][:, 0:NB * E].rearrange("p (b e) -> p b e", b=NB),
                                             ffn_gb_rows[:].unsqueeze(1).to_broadcast([P, NB, E]), ALU.add), passed)
                for b in range(NB):
                    last = dve.max(ftop[:, b, :], fl[:, b, :])
                chain.link(last)
                dve.tensor_tensor(fgate[:], fl[:], ftop[:, :, 1:2].to_broadcast([P, NB, E]), ALU.is_ge)
                chain.link(dve.tensor_tensor(hm[:, 0, 0:NB * E].rearrange("p (b e) -> p b e", b=NB), fl[:], ftop[:, :, 0:1].to_broadcast([P, NB, E]), ALU.subtract))
                dve.tensor_copy(fl[:], hm[:, 0, 0:NB * E].rearrange("p (b e) -> p b e", b=NB)).then_inc(fmax_ready.sem, 1)
                dve.wait_ge(*fe_ready.at(i))
                chain.link(dve.tensor_tensor(fgate[:], fgate[:], fe[:], ALU.mult))
                chain.link(dve.tensor_reduce(fs[:, 0, :], fgate[:], AX.X, ALU.add))
                chain.link(dve.reciprocal(fs[:, 1, :], fs[:, 0, :]))
                chain.link(dve.tensor_tensor(fgate[:], fgate[:], fs[:, 1, :].unsqueeze(2).to_broadcast([P, NB, E]), ALU.mult))
                for n in range(FU):
                    c, half = n // 2, n % 2
                    b = c // QC
                    dve.wait_ge(*f_act.at(i, n + 1))
                    for j in range(4):
                        e = 4 * half + j
                        first = n % 2 == 0 and j == 0
                        ins = dve.scalar_tensor_tensor(R[:, c, :], gl_act[:, n % 2, j * P:(j + 1) * P], fgate[:, b, e:e + 1],
                                                       X[:, c, :] if first else R[:, c, :], ALU.mult, ALU.add)
                        if j < 3:
                            chain.link(ins)
                    ins.then_inc(f_added.sem, 1)
                    dve.wait_ge(*f_added.at(i, n + 1))
                dve.wait_ge(*out_saved.before(i))
                layernorm(6, Y)
                chain.close()


_TRANSPOSED = {"L0_attn_" + n + "T": "L0_attn_" + n for n in ("wq", "wk", "wv", "wo", "lin1", "lin2", "w1", "w2", "mem")}
_TRANSPOSED.update({"L0_xattn_" + n + "T": "L0_xattn_" + n for n in ("wq", "wk", "wv", "wo")})
_TRANSPOSED.update({"L0_ffn_router_wT": "L0_ffn_router_w", "L1_xattn_igate_wT": "L1_xattn_igate_w",
                    "L1_xattn_fgate_wT": "L1_xattn_fgate_w", "L1_ffn_gate_wT": "L1_ffn_gate_w"})
_PLAIN = ["x", "ctx_1024", "mask_BxSxS2_bf1", "L0_attn_mem", "L0_attn_w2", "L0_attn_b1", "L0_attn_b2",
          "L0_attn_alpha", "L0_attn_theta", "L0_xattn_bq", "L0_xattn_bk", "L0_xattn_bv", "L0_xattn_bo",
          "L0_ffn_w1", "L0_ffn_w2", "L1_attn_W_Q", "L1_attn_W_K", "L1_attn_W_V", "L1_xattn_igate_b",
          "L1_xattn_fgate_b", "L1_xattn_out_w", "L1_ffn_gate_b", "L1_ffn_expert_b"]


def kernel(**inputs):
    import numpy as _np
    import concourse.bacc as _bacc
    from concourse import mybir as _mybir
    from concourse.bass_utils import run_bass_kernel_spmd as _run

    laid = {n: inputs[n] for n in _PLAIN}
    for n in ("L0_attn_alpha", "L0_attn_theta"):
        laid[n] = _np.reshape(inputs[n], (1,))
    for new, old in _TRANSPOSED.items():
        laid[new] = _np.transpose(inputs[old])
    laid["xT"] = _np.transpose(_np.reshape(inputs["x"], (B * S, D)))
    laid["ctxT"] = _np.transpose(_np.reshape(inputs["ctx_1024"], (B * S, D)))
    laid["L0_attn_b1_cols"] = _np.transpose(_np.reshape(inputs["L0_attn_b1"], (FC, P)))
    laid["maskT"] = _np.transpose(inputs["mask_BxSxS2_bf1"], (0, 2, 1))
    laid["L1_ffn_expert_wT"] = _np.reshape(_np.transpose(inputs["L1_ffn_expert_w"], (2, 0, 1)), (D, E * D))

    nc = _bacc.Bacc("TRN2", target_bir_lowering=False, num_devices=1)
    arrays, args = {}, {}
    for name, value in laid.items():
        value = _np.ascontiguousarray(value)
        arrays[f"in_{name}_dram"] = value
        args[name] = nc.dram_tensor(f"in_{name}_dram", value.shape, _mybir.dt.from_np(value.dtype), kind="ExternalInput").ap()
    out = nc.dram_tensor("out_0_dram", (B, S, D), _mybir.dt.float32, kind="ExternalOutput").ap()
    parts_dram = nc.dram_tensor("parts_dram", (2, 3, D, T), _mybir.dt.bfloat16, kind="Internal").ap()
    decoder_kernel(nc, args, out, parts_dram)
    r = _run(nc, [arrays], core_ids=[0])
    return r.results[0]["out_0_dram"]
```

```python
from contextlib import ExitStack

import concourse.bass as bass
from concourse import mybir

F32 = mybir.dt.float32
BF16 = mybir.dt.bfloat16
U8 = mybir.dt.uint8
U32 = mybir.dt.uint32
ALU = mybir.AluOpType
ACT = mybir.ActivationFunctionType
AX = mybir.AxisListType

P = 128
B, S, D = 8, 256, 128
NB = 2
STEPS = B // NB
T = NB * S
NC = T // P
QC = S // P
M = 64
KW = M + S
HID = 512
FC = HID // P
H0, DH0 = 4, 32
WIN = 64
KB = P + WIN
H1, DH1 = 16, 8
E = 8
CAP = int(1.25 * B * S * 2 / E) + 1
H2, DH2 = 8, 16
EPS = 1e-5
NEG = -float(2 ** 100)
TERMS = [(0, 0), (0, 1), (0, 2), (1, 0), (1, 1), (2, 0)]


class Signal:

    def __init__(self, sem, per=1, primed=0, extra=0):
        self.sem, self.per, self.primed, self.extra = sem, per, primed, extra

    def count(self, step):
        return self.per + (self.extra if is_first(step) else 0)

    def at(self, step, n=None):
        n = self.count(step) if n is None else n
        return self.sem, self.before(step)[1] + n

    def before(self, step):
        return self.sem, step * self.per + self.primed + (0 if is_first(step) else self.extra)

    def prime(self, eng):
        eng.sem_inc(self.sem, self.primed)


def is_first(step):
    return isinstance(step, int) and step == 0


def wait_apart(eng, passed, sem, value):
    eng.wait_ge(sem, value)
    eng.sem_inc(passed.sem, 1)


class Chain:

    def __init__(self, eng, links, step):
        self.eng, self.links, self.step, self.n = eng, links, step, 0

    def link(self, ins, apart=None):
        self.n += 1
        ins.then_inc(self.links.sem, 1)
        if apart:
            wait_apart(self.eng, apart, *self.links.at(self.step, self.n))
        else:
            self.eng.wait_ge(*self.links.at(self.step, self.n))

    def mark(self, ins):
        self.n += 1
        ins.then_inc(self.links.sem, 1)
        return self.n

    def wait(self, n):
        self.eng.wait_ge(*self.links.at(self.step, n))

    def close(self):
        assert self.n == self.links.count(self.step), (self.links.sem, self.n)


def decoder_kernel(nc, a, out, parts_dram):
    with ExitStack() as ctx:
        def sb(name, shape, dt=F32, scope=ctx):
            return scope.enter_context(nc.sbuf_tensor(name, shape, dt))

        def signal(name, per=1, primed=0, extra=0):
            return Signal(ctx.enter_context(nc.semaphore(name)), per, primed, extra)

        bank = [ctx.enter_context(nc.psum_tensor(f"bank{i}", [P, 512], F32)) for i in range(8)]

        square = ["L0_attn_wqT", "L0_attn_wkT", "L0_attn_wvT", "L0_attn_woT", "L0_attn_lin1T", "L0_attn_lin2T",
                  "L0_xattn_wqT", "L0_xattn_wkT", "L0_xattn_wvT", "L0_xattn_woT",
                  "L1_attn_W_Q", "L1_attn_W_K", "L1_attn_W_V"]
        w = {n: sb("w_" + n, [P, P]) for n in square}
        w1T = sb("w1T", [P, HID])
        w2 = sb("w2", [P, HID])
        w2T = sb("w2T", [P, FC, P])
        w1T_new = sb("w1T_new", [P, HID])
        w2T_new = sb("w2T_new", [P, FC, P])
        b1 = sb("b1", [P, FC])
        b1_new = sb("b1_new", [P, FC])
        b2 = sb("b2", [P, 1])
        b2_new = sb("b2_new", [P, 1])
        b1_rows = sb("b1_rows", [P, HID])
        rate = sb("rate", [P, 4])
        router = sb("router", [P, E])
        moe_w1 = sb("moe_w1", [P, E, HID])
        moe_w2 = sb("moe_w2", [P, E, FC, P])
        x_bq = sb("x_bq", [P, 1])
        x_bk = sb("x_bk", [P, 1])
        x_bv_rows = sb("x_bv_rows", [P, P])
        x_bo_rows = sb("x_bo_rows", [P, P])
        gates_w = sb("gates_w", [P, NB, 3, 32 + NB * H2])
        gates_b = sb("gates_b", [32 + NB * H2, 1])
        out_w_rows = sb("out_w_rows", [P, P])
        ffn_gw = sb("ffn_gw", [P, E])
        ffn_gb_rows = sb("ffn_gb_rows", [P, E])
        ffn_w = sb("ffn_w", [P, E * P])
        ffn_b = sb("ffn_b", [1, E * P])
        ident = sb("ident", [P, P])
        ident_b = sb("ident_b", [P, P], BF16)
        ones = sb("ones", [P, P])
        ones_b = sb("ones_b", [P, P], BF16)
        before_b = sb("before_b", [P, P], BF16)
        future_b = sb("future_b", [P, P], BF16)
        past_b = sb("past_b", [P, P], BF16)
        window = sb("window", [P, KB])
        mem_mask = sb("mem_mask", [M, M])
        head_sel = sb("head_sel", [96, H1, P], BF16)
        row_sel = sb("row_sel", [96, P], BF16)
        iota_e = sb("iota_e", [P, E])
        eps = sb("eps", [P, 1])
        vT_all = sb("vT_all", [P, STEPS * T])
        hT = sb("hT", [P, FC, T + M])

        first_loaded = signal("first_loaded")
        load_w = signal("load_w")
        passed = signal("passed")
        const_ready = signal("const_ready")
        zeros_made = signal("zeros_made", 6)
        masks_made = signal("masks_made", 11)
        sums_zero = signal("sums_zero")
        dve_pro = signal("dve_pro", 3)

        xin_loaded = signal("xin_loaded", 16)
        xtok_loaded = signal("xtok_loaded", 16)
        mem_qk = signal("mem_qk")
        mem_q_done = signal("mem_q_done")
        mem_k_done = signal("mem_k_done")
        qk_ready = signal("qk_ready")
        v_ready = signal("v_ready")
        q_copied = signal("q_copied", 1)
        v_copied = signal("v_copied", 6)
        k_copied = signal("k_copied", 2)
        k_copied_too = signal("k_copied_too", 2)
        NU = NB * QC
        scores_a = signal("scores_a", NU, extra=1)
        max_a = signal("max_a", NU, extra=1)
        exp_a = signal("exp_a", NU, extra=1)
        norm_a = signal("norm_a", NU, extra=1)
        pT_a = signal("pT_a", NU, extra=1)
        pTa_copied = signal("pTa_copied", NU, extra=1)
        pTb_copied = signal("pTb_copied", NU, extra=1)
        pv_a = signal("pv_a", NU, extra=1)
        oT_copied = signal("oT_copied", 1, extra=1)
        swa_ready = signal("swa_ready", 1, extra=1)
        vT_copied = signal("vT_copied", 1, extra=1)
        zT_a = signal("zT_a", FC, extra=1)
        z_copied = signal("z_copied", FC)
        hT_a = signal("hT_a", FC, extra=FC)
        pred_a = signal("pred_a", 1)
        e_ready = signal("e_ready", 1)
        eT_tr = signal("eT_tr", 1)
        etok_copied = signal("etok_copied", 1, extra=1)
        zd_ready = signal("zd_ready", NC, extra=1)
        z_biased = signal("z_biased", NC, extra=1)
        sg_ready = signal("sg_ready", NC, extra=1)
        dz_ready = signal("dz_ready", NC, extra=1)
        bias_summed = signal("bias_summed", NC, extra=1)
        grads_ready = signal("grads_ready", NC, extra=1)
        grads_added = signal("grads_added", 1)
        dve_a = signal("dve_a", 2 * NU + 3 * NC, extra=2 + 1 + 3)
        act_a = signal("act_a", NC, extra=1)
        upd_pe = signal("upd_pe")
        upd_dve = signal("upd_dve")
        updated = signal("updated")

        SR = 2 * DH1 * len(TERMS)
        q_stack = sb("q_stack", [SR, H1 // 2, T], BF16)
        k_stack = sb("k_stack", [SR, H1 // 2, 2, T], BF16)
        v_aug = sb("v_aug", [P, NC, H1, 32])
        neg_max = sb("neg_max", [96, 2, S], BF16)
        seen = sb("seen", [P, E])
        kpad2 = sb("kpad2", [P, H2, T])
        v2_aug = sb("v2_aug", [P, NC, H2, 32])
        ones16 = sb("ones16", [NB * H2, S])
        neg_pm = sb("neg_pm", [96, S], BF16)
        fb_parts = sb("fb_parts", [96, E * P], BF16)

        b_x_loaded = signal("b_x_loaded", 32)
        ctxT_loaded = signal("ctxT_loaded", 16)
        ctx_tok_loaded = signal("ctx_tok_loaded", 16)
        kpad2_loaded = signal("kpad2_loaded", 16 * H2)
        masks_loaded = signal("masks_loaded", 32)
        x_in_used = signal("x_in_used")
        zT_b = signal("zT_b", FC)
        hT_b = signal("hT_b", FC)
        out_mem = signal("out_mem")
        memT_ready = signal("memT_ready")
        lin1 = signal("lin1")
        lin_ready = signal("lin_ready")
        g_ready = signal("g_ready", 2)
        merged = signal("merged")
        merged_tr = signal("merged_tr")
        var_h = signal("var_h")
        rstd_h = signal("rstd_h")
        x_norm_h = signal("x_norm_h", NC)
        x_tr_h = signal("x_tr_h")
        xt_h = signal("xt_h")
        LN = 5
        var_ready = signal("var_ready", LN * NB)
        rstd_ready = signal("rstd_ready", LN * NB)
        x_norm = signal("x_norm", LN * NC)
        x_tr = signal("x_tr", (LN - 1) * NB)
        xt_ready = signal("xt_ready", (LN - 1) * NB)
        masks_ready = signal("masks_ready")
        k_b = signal("k_b")
        q_b = signal("q_b")
        v_b = signal("v_b")
        kf_ready = signal("kf_ready")
        kh_ready = signal("kh_ready")
        k_parts_ready = signal("k_parts_ready")
        q_parts_ready = signal("q_parts_ready", 3)
        k_saved = signal("k_saved", 16)
        q_saved = [signal(f"q_saved{j}", 16) for j in range(3)]
        q_stacked = signal("q_stacked", 16 * len(TERMS))
        k_stacked = signal("k_stacked", 16 * 12)
        v_aug_ready = signal("v_aug_ready")
        XU = NB * H1
        s_ready = signal("s_ready", XU)
        s_read = signal("s_read", XU)
        MG = XU // 8
        AHEAD = 14
        mx_tr = signal("mx_tr", MG)
        neg_max_ready = signal("neg_max_ready", MG)
        sT_ready = signal("sT_ready", XU)
        exp_ready = signal("exp_ready", XU)
        G = 4
        pv_ready = signal("pv_ready", NB * G)
        o_copied = signal("o_copied", NB * 2)
        o_tr = signal("o_tr", NB)
        o_tok_ready = signal("o_tok_ready", NB)
        o_tok_tr = signal("o_tok_tr")
        o_T_ready = signal("o_T_ready")
        wo_ready = signal("wo_ready")
        x_plus = signal("x_plus")
        r_scored = signal("r_scored")
        share_diff = signal("share_diff")
        share_exp = signal("share_exp")
        picked = signal("picked")
        ranks = signal("ranks")
        gates_ready = signal("gates_ready")
        x_twice = signal("x_twice")
        up_ready = signal("up_ready", E * FC)
        he_ready = signal("he_ready", E * FC)
        down_ready = signal("down_ready", E)
        last_down_b0 = signal("last_down_b0")
        down_added = signal("down_added", E)
        qkv_c = signal("qkv_c")
        aq_ready = signal("aq_ready", 2)
        ak_ready = signal("ak_ready")
        as_ready = signal("as_ready", NB)
        amax_ready = signal("amax_ready", NB)
        aexp_ready = signal("aexp_ready", NB)
        apT_ready = signal("apT_ready", NB)
        apT_copied = signal("apT_copied", NB)
        apv_ready = signal("apv_ready")
        pre_ready = signal("pre_ready")
        abs_ready = signal("abs_ready")
        ef_ready = signal("ef_ready")
        ln_ready = signal("ln_ready")
        pm_ready = signal("pm_ready")
        neg_pm_ready = signal("neg_pm_ready")
        cols_ready = signal("cols_ready")
        cols_copied = signal("cols_copied", 2)
        v2_ready = signal("v2_ready")
        MU = NB * H2
        DEEP = 3
        eu_ready = signal("eu_ready", MU)
        decay_ready = signal("decay_ready", MU)
        c_ready = signal("c_ready", MU)
        pv2_ready = signal("pv2_ready", NB * 2)
        o5_copied = signal("o5_copied", NB)
        o5_tr = signal("o5_tr", NB)
        var2_ready = signal("var2_ready")
        rstd2_ready = signal("rstd2_ready")
        pooled_ready = signal("pooled_ready")
        rep_ready = signal("rep_ready")
        fl_ready = signal("fl_ready")
        fmax_ready = signal("fmax_ready")
        fe_ready = signal("fe_ready")
        f_units = [(2 * cc + c, half) for cc in range(NC // 2) for half in range(2) for c in range(2)]
        FU = len(f_units)
        f_ready = signal("f_ready", FU)
        f_act = signal("f_act", FU, primed=1)
        f_added = signal("f_added", FU // 2)
        out_saved = signal("out_saved", 16, primed=32)
        fb_ready = signal("fb_ready")
        r_zero = signal("r_zero")
        dve_last = signal("dve_last", 4)
        dve_b = signal("dve_b", 119)
        dve_h = signal("dve_h", 5)
        pool_b = signal("pool_b", 2)

        scope_a = ExitStack()
        xin = sb("xin", [P, NB, KW], scope=scope_a)
        xtok = sb("xtok", [P, NC + 1, P], scope=scope_a)
        qT_mem = sb("qT_mem", [P, M], scope=scope_a)
        kpad = sb("kpad", [P, H0, NB, KW], scope=scope_a)
        stats = sb("stats", [P, 2, 16], scope=scope_a)
        oT = sb("oT", [P, T + M], scope=scope_a)
        vT_mem = sb("vT_mem", [P, M], scope=scope_a)
        eT = sb("eT", [P, T + M], scope=scope_a)
        etok = sb("etok", [P, NC + 1, P], scope=scope_a)
        grad1 = sb("grad1", [P, HID], scope=scope_a)
        grad2 = sb("grad2", [P, HID], scope=scope_a)
        dz_sum = sb("dz_sum", [P, HID], scope=scope_a)
        e_sum = sb("e_sum", [P, P], scope=scope_a)
        stage = ExitStack()
        qT = sb("qT", [P, T], scope=stage)
        vtok = sb("vtok", [P, NB, 3, P], scope=stage)
        probs = sb("probs", [P, 2, H0, KB], scope=stage)
        probsT_a = sb("probsT_a", [P, 2, H0 * P], scope=stage)
        probsT_b = sb("probsT_b", [WIN, 2, H0 * P], scope=stage)
        stage.close()
        stage = ExitStack()
        zt = sb("zt", [P, 2, HID], scope=stage)
        sg = sb("sg", [P, 2, HID], scope=stage)
        ht = sb("ht", [P, 2, HID], scope=stage)
        sl = sb("sl", [P, 2, HID], scope=stage)
        dz = sb("dz", [P, 2, HID], scope=stage)
        stage.close()
        scope_a.close()
        scope_b = ExitStack()
        x_in = sb("x_in", [P, NC, P], scope=scope_b)
        xT_in = sb("xT_in", [P, T], scope=scope_b)
        X = sb("X", [P, NC, P], scope=scope_b)
        XT = sb("XT", [P, T], scope=scope_b)
        Y = sb("Y", [P, NC, P], scope=scope_b)
        R = sb("R", [P, NC, P], scope=scope_b)
        bn = sb("bn", [P, NC, 6], scope=scope_b)
        mv = sb("mv", [P, NC, 2], scope=scope_b)
        deviation = sb("deviation", [P, NC], scope=scope_b)
        rstd = sb("rstd", [P, NC], scope=scope_b)
        ctxT = sb("ctxT", [P, T], scope=scope_b)
        ctx_tok = sb("ctx_tok", [P, NC, P], scope=scope_b)
        mask_q = sb("mask_q", [P, NC, S], U8, scope=scope_b)
        mask_k = sb("mask_k", [P, NC, S], U8, scope=scope_b)
        add_q = sb("add_q", [P, NC, S], scope=scope_b)
        add_k = sb("add_k", [P, NC, S], BF16, scope=scope_b)
        q_parts = sb("q_parts", [P, 3, T], BF16, scope=scope_b)
        k_parts = sb("k_parts", [P, 3, T], BF16, scope=scope_b)
        rec = sb("rec", [P, QC, H1], scope=scope_b)
        o_tok = sb("o_tok", [P, NC, P], scope=scope_b)
        logits = sb("logits", [P, NC, E], scope=scope_b)
        top = sb("top", [P, NC, 8], scope=scope_b)
        top_i = sb("top_i", [P, NC, 8], U32, scope=scope_b)
        top_f = sb("top_f", [P, NC, 2], scope=scope_b)
        pick = sb("pick", [P, 2, NC, E], scope=scope_b)
        picked_b = sb("picked_b", [P, NC, E], BF16, scope=scope_b)
        share = sb("share", [P, 4, NC], scope=scope_b)
        rank = sb("rank", [P, NC, E], scope=scope_b)
        gate = sb("gate", [P, NC, E], scope=scope_b)
        pooled_rep = sb("pooled_rep", [P, NB, P], scope=scope_b)
        fl = sb("fl", [P, NB, E], scope=scope_b)
        ftop = sb("ftop", [P, NB, 8], scope=scope_b)
        fe = sb("fe", [P, NB, E], scope=scope_b)
        fs = sb("fs", [P, 2, NB], scope=scope_b)
        fgate = sb("fgate", [P, NB, E], scope=scope_b)
        memT = sb("memT", [P, T], scope=scope_b)
        g1 = sb("g1", [P, T], scope=scope_b)
        g2 = sb("g2", [P, T], scope=scope_b)
        qr = sb("qr", [P, T], scope=scope_b)
        R1 = sb("R1", [P, NC, P], scope=scope_b)
        bn_h = sb("bn_h", [P, NC, 6], scope=scope_b)
        mv_h = sb("mv_h", [P, NC, 2], scope=scope_b)
        deviation_h = sb("deviation_h", [P, NC], scope=scope_b)
        recip_h = sb("recip_h", [P, NC], scope=scope_b)
        X1 = memT[:].rearrange("p (c d) -> p c d", c=NC)
        qf, kf, kr = g1, g1, qr
        XT1, o_T = g2, g2
        stage = ExitStack()
        mx = sb("mx", [P, QC, H1], scope=stage)
        neg_r = hT[0:H1, FC - 1, S:2 * S]
        neg_m = k_parts[0:8, 0, 0:S]
        pT = sb("pT", [P, 2, 4, QC, S], scope=stage)
        o_heads = sb("o_heads", [P, 4, S], scope=stage)
        stage.close()
        stage = ExitStack()
        he = sb("he", [P, 2, FC, T], scope=stage)
        stage.close()
        stage = ExitStack()
        aq = sb("aq", [P, T], scope=stage)
        ak = sb("ak", [P, T], scope=stage)
        av = sb("av", [P, NC, P], scope=stage)
        ap = sb("ap", [P, NB, 3, P], scope=stage)
        apT = sb("apT", [P, NB, 3 * P], scope=stage)
        ast = sb("ast", [P, 4, NC], scope=stage)
        stage.close()
        stage = ExitStack()
        gi, gf, gl, cs, ga, pm, gm = (hT[0:NB * H2, k, half * S:(half + 1) * S] for k in range(FC) for half in range(2) if (k, half) != (FC - 1, 1))
        pb2 = sb("pb2", [NB * H2, S], BF16, scope=stage)
        a_col = sb("a_col", [P, NC, H2], scope=stage)
        em_col = sb("em_col", [P, NC, H2], scope=stage)
        decay = sb("decay", [P, DEEP, S + P], scope=stage)
        cT = sb("cT", [P, 2, 4, S + P], scope=stage)
        o5 = add_q[:].rearrange("p (b g) s -> p b g s", b=NB)
        den = sb("den", [P, NC, H2], scope=stage)
        hh = o_tok[:].rearrange("p c (h d) -> p c h d", d=DH2)
        hm = sb("hm", [P, 2, NC * H2], scope=stage)
        hrs = sb("hrs", [P, NC * H2], scope=stage)
        gl_act = cT[:].rearrange("p g j s -> p (g j s)")[:, 0:2048].rearrange("p (n f) -> p n f", n=4)
        stage.close()
        stage = ExitStack()
        fb_row = sb("fb_row", [1, 1, E * P], scope=stage)
        fb_m = sb("fb_m", [1, E * P], BF16, scope=stage)
        stage.close()
        scope_b.close()

        block = ctx.enter_context(nc.Block())
        units = [(b, c) for b in range(NB) for c in range(QC)] + [(0, None)]

        def chunks(i):
            return NC + (1 if is_first(i) else 0)

        def s_banks(u):
            return (bank[5], bank[6]) if u % 2 == 0 else (bank[0], bank[2])

        v_banks = (bank[4], bank[7])

        def down_bank(e, c):
            return bank[0] if e == E - 1 and c >= QC else bank[2 + e % 2]

        HEAD_PARTS = 7

        def zd_banks(c):
            return ((bank[5], bank[6]), (bank[4], bank[2]), (bank[7], bank[1]))[c % 3]

        def q_bank(n):
            return bank[4 + n % 4] if n < 12 else (bank[4], bank[5], bank[2])[n % 3]

        def m_banks(n):
            return ((bank[4], bank[6]), (bank[5], bank[7]), (bank[0], bank[1]))[n % DEEP]

        def k_bank(n):
            return bank[6 + n % 2] if n < 20 else bank[4 + n % 4]

        first_w = [(w[n][:], a[n]) for n in square[:3]] + [
            (xin[:, 0, 0:M], a["L0_attn_memT"]),
            (xin[:, 1, 0:M], a["L0_attn_memT"]),
        ]
        loads_w = [(w[n][:], a[n]) for n in square[3:]] + [
            (w1T[:], a["L0_attn_w1T"]), (w2[:], a["L0_attn_w2"]),
            (w2T[:], a["L0_attn_w2T"].rearrange("(k p) d -> p k d", p=P)),
            (b1[:], a["L0_attn_b1_cols"]),
            (b2[:], a["L0_attn_b2"].unsqueeze(1)),
            (b1_rows[:], a["L0_attn_b1"].partition_broadcast(P)),
            (rate[:, 0:1], a["L0_attn_alpha"].partition_broadcast(P)),
            (rate[:, 1:2], a["L0_attn_theta"].partition_broadcast(P)),
            (xtok[0:M, NC, :], a["L0_attn_mem"]),
        ]
        late_w = [
            (router[:], a["L0_ffn_router_wT"]),
            (moe_w1[:], a["L0_ffn_w1"].rearrange("e d f -> d e f")),
            (moe_w2[:], a["L0_ffn_w2"].rearrange("e (k p) d -> p e k d", p=P)),
            (x_bq[:], a["L0_xattn_bq"].unsqueeze(1)), (x_bk[:], a["L0_xattn_bk"].unsqueeze(1)),
            (x_bv_rows[:], a["L0_xattn_bv"].partition_broadcast(P)),
            (x_bo_rows[:], a["L0_xattn_bo"].partition_broadcast(P)),
            (out_w_rows[:], a["L1_xattn_out_w"].partition_broadcast(P)),
            (ffn_gw[:], a["L1_ffn_gate_wT"]),
            (ffn_gb_rows[:], a["L1_ffn_gate_b"].partition_broadcast(P)),
            (ffn_w[:], a["L1_ffn_expert_wT"]),
            (ffn_b[:], a["L1_ffn_expert_b"].rearrange("e o -> (e o)").unsqueeze(0)),
        ]
        for row, gate_name in ((0, "igate"), (32, "fgate")):
            for b in range(NB):
                r = slice(row + H2 * b, row + H2 * (b + 1))
                late_w.append((gates_b[r, :], a[f"L1_xattn_{gate_name}_b"].unsqueeze(1)))
                late_w.append((gates_w[:, b, :, r], a[f"L1_xattn_{gate_name}_wT"].rearrange("(j p) e -> p j e", p=P)))
        late_loaded = signal("late_loaded")

        def of_heads(n, part):
            return parts_dram[n, part].rearrange("(p f) t -> f p t", f=2 * DH1)

        @block.sync
        def _(sp):
            out_saved.prime(sp)
            for dst, src in first_w:
                sp.dma_start(dst, src).then_inc(first_loaded.sem, 16)

            def load_xin(i):
                sp.dma_start(xin[:, :, M:KW], a["xT"][:, bass.ds(i * T, T)].rearrange("d (b t) -> d b t", b=NB)).then_inc(xin_loaded.sem, 16)

            def load_xtok(i):
                sp.dma_start(xtok[:, 0:NC, :], a["x"].rearrange("b s d -> (b s) d")[bass.ds(i * T, T), :].rearrange("(c p) d -> p c d", p=P)).then_inc(xtok_loaded.sem, 16)

            load_xin(0)
            for dst, src in loads_w:
                sp.dma_start(dst, src).then_inc(load_w.sem, 16)
            load_xtok(0)
            sp.wait_ge(*sums_zero.at(0))
            for dst, src in late_w:
                sp.dma_start(dst, src).then_inc(late_loaded.sem, 16)
            with sp.Fori(0, STEPS - 1) as i:
                sp.wait_ge(*zd_ready.before(i + 1))
                load_xin(i + 1)
                sp.wait_ge(*grads_ready.before(i + 1))
                load_xtok(i + 1)
            sp.wait_ge(*updated.at(0))

            def load_x(i):
                rows = bass.ds(i * T, T)
                sp.dma_start(xT_in[:], a["xT"][:, rows]).then_inc(b_x_loaded.sem, 16)
                sp.dma_start(x_in[:], a["x"].rearrange("b s d -> (b s) d")[rows, :].rearrange("(c p) d -> p c d", p=P)).then_inc(b_x_loaded.sem, 16)

            def load_masks(i):
                rows = bass.ds(i * T, T)
                sp.dma_start(mask_q[:], a["mask_BxSxS2_bf1"].rearrange("b q k -> (b q) k")[rows, :].rearrange("(c p) k -> p c k", p=P)).then_inc(masks_loaded.sem, 16)
                sp.dma_start(mask_k[:], a["maskT"].rearrange("b k q -> (b k) q")[rows, :].rearrange("(c p) q -> p c q", p=P)).then_inc(masks_loaded.sem, 16)

            def load_ctxT(i):
                sp.dma_start(ctxT[:], a["ctxT"][:, bass.ds(i * T, T)]).then_inc(ctxT_loaded.sem, 16)

            def load_ctx_tok(i):
                sp.dma_start(ctx_tok[:], a["ctx_1024"].rearrange("b s d -> (b s) d")[bass.ds(i * T, T), :].rearrange("(c p) d -> p c d", p=P)).then_inc(ctx_tok_loaded.sem, 16)

            def load_kpad2(i):
                for h in range(H2):
                    r = slice(DH2 * h, DH2 * h + DH2)
                    sp.dma_start(kpad2[r, h, :], a["ctxT"][r, bass.ds(i * T, T)]).then_inc(kpad2_loaded.sem, 16)

            def stack_k(i):
                sp.wait_ge(*k_parts_ready.at(i))
                sp.dma_start(parts_dram[0].rearrange("j d t -> d j t"), k_parts[:]).then_inc(k_saved.sem, 16)
                sp.wait_ge(*k_saved.at(i))
                for s in range(2):
                    for r, (_, part) in enumerate(TERMS):
                        lo = (2 * r + s) * DH1
                        sp.dma_start(k_stack[lo:lo + DH1, :, s, :], of_heads(0, part)[DH1 * s:DH1 * (s + 1)]).then_inc(k_stacked.sem, 16)

            def stack_q(i):
                for j in range(3):
                    sp.wait_ge(*q_parts_ready.at(i, j + 1))
                    sp.dma_start(parts_dram[1, j], q_parts[:, j, :]).then_inc(q_saved[j].sem, 16)
                for j in range(3):
                    sp.wait_ge(*q_saved[j].at(i))
                    for r in [r for r, term in enumerate(TERMS) if term[0] == j]:
                        sp.dma_start(q_stack[2 * DH1 * r:2 * DH1 * (r + 1)], of_heads(1, j)).then_inc(q_stacked.sem, 16)

            def save(i):
                sp.wait_ge(*x_norm.at(i + 1, NC))
                sp.dma_start(out.rearrange("b s d -> (b s) d")[bass.ds(i * T, T), :].rearrange("(c p) d -> p c d", p=P), Y[:]).then_inc(out_saved.sem, 16)

            load_x(0)
            load_ctxT(0)
            load_masks(0)
            stack_k(0)
            stack_q(0)
            load_ctx_tok(0)
            load_kpad2(0)

            def during(i, following):
                if following:
                    sp.wait_ge(*x_in_used.at(i))
                    load_x(i + 1)
                    wait_apart(sp, passed, *masks_ready.at(i))
                    load_masks(i + 1)
                    stack_q(i + 1)
                    sp.wait_ge(*pre_ready.at(i))
                    load_ctxT(i + 1)
                    sp.wait_ge(*v2_ready.at(i))
                    load_ctx_tok(i + 1)
                    sp.wait_ge(*c_ready.at(i))
                    load_kpad2(i + 1)
                    stack_k(i + 1)
                save(i)

            with sp.Fori(0, STEPS - 1) as i:
                during(i, True)
            during(STEPS - 1, False)
            sp.wait_ge(*out_saved.before(STEPS))

        @block.gpsimd
        def _(pool):
            def select(made, tile, op, fill, base, pattern, channel):
                made.link(pool.affine_select(out=tile, in_=tile, compare_op=op, fill=fill, base=base,
                                             pattern=pattern, channel_multiplier=channel))

            made = Chain(pool, zeros_made, 0)
            made.link(pool.memset(kpad[:], 0.0))
            pool.memset(ident[:], 0.0)
            pool.memset(window[:], 0.0)
            made.link(pool.memset(mem_mask[:], 0.0))
            select(made, ident[:], ALU.not_equal, 1.0, 0, [[-1, P]], 1)
            select(made, mem_mask[:], ALU.is_ge, NEG, 0, [[-1, M]], 1)
            select(made, window[:], ALU.is_gt, NEG, 0, [[1, KB]], -1)
            select(made, window[:], ALU.is_ge, NEG, WIN, [[-1, KB]], 1)
            made.close()
            pool.memset(ones[:], 1.0).then_inc(const_ready.sem, 1)
            pool.memset(future_b[:], 0.0)
            pool.memset(past_b[:], 0.0)
            pool.memset(before_b[:], 1.0)
            pool.memset(head_sel[:], 0.0)
            pool.memset(row_sel[:], 0.0)
            pool.memset(eps[:], EPS)
            pool.iota(iota_e[:], pattern=[[1, E]], base=0, channel_multiplier=0, allow_small_or_imprecise_dtypes=True)
            for t in (q_stack, k_stack, neg_max, neg_pm, kpad2, v_aug, v2_aug, seen, fb_parts):
                pool.memset(t[:], 0.0)
            pool.memset(ones16[:], 1.0)
            made = Chain(pool, masks_made, 0)
            made.link(pool.memset(ones_b[:], 1.0))
            pool.memset(v_aug[:, :, :, DH1:DH1 + 1], 1.0)
            pool.memset(v2_aug[:, :, :, DH2:DH2 + 1], float(DH2) ** -0.5)
            select(made, future_b[:], ALU.is_ge, NEG, 0, [[-1, P]], 1)
            select(made, past_b[:], ALU.is_ge, NEG, 0, [[1, P]], -1)
            select(made, before_b[:], ALU.is_gt, 0.0, 0, [[1, P]], -1)
            for part in range(3):
                rows = slice(32 * part, 32 * part + H1)
                select(made, head_sel[rows], ALU.not_equal, 1.0, 0, [[-1, H1], [0, P]], 1)
                select(made, row_sel[32 * part:32 * part + 1], ALU.not_equal, 1.0, 0, [[0, P]], 1)
            made.link(pool.tensor_copy(ident_b[:], ident[:]))
            made.close()
            pool.wait_ge(*sums_zero.at(0))

            def sums(i):
                for c in range(chunks(i)):
                    n, s = (P if c < NC else M), c % 2
                    pool.wait_ge(*dz_ready.at(i, c + 1))
                    if c == 0:
                        pool.wait_ge(*etok_copied.at(i))
                    if c > 0:
                        pool.wait_ge(*bias_summed.at(i, c))
                    elif not is_first(i):
                        pool.wait_ge(*bias_summed.before(i))
                    pool.tensor_tensor(e_sum[0:n], e_sum[0:n], etok[0:n, c, :], ALU.add)
                    pool.tensor_tensor(dz_sum[0:n], dz_sum[0:n], dz[0:n, s], ALU.add).then_inc(bias_summed.sem, 1)

            sums(0)
            with pool.Fori(0, STEPS - 1) as i:
                sums(i + 1)

            def residual(i):
                pool.wait_ge(*x_norm_h.at(i))
                pool.tensor_tensor(R1[:], X1, x_bo_rows[:].unsqueeze(1).to_broadcast([P, NC, P]), ALU.add).then_inc(x_plus.sem, 1)

            def k_and_masks(i):
                pool.wait_ge(*kh_ready.at(i))
                pool_chain = Chain(pool, pool_b, i)
                pool_chain.link(pool.tensor_tensor(kr[:], kf[:], k_parts[:, 0, :], ALU.subtract), passed)
                pool_chain.link(pool.tensor_copy(k_parts[:, 1, :], kr[:]))
                pool.tensor_tensor(k_parts[:, 2, :], kr[:], k_parts[:, 1, :], ALU.subtract).then_inc(k_parts_ready.sem, 1)
                wait_apart(pool, passed, *masks_loaded.at(i))
                pool.tensor_scalar(add_q[:], mask_q[:], -1.0, -NEG, ALU.add, ALU.mult)
                pool.tensor_scalar(add_k[:], mask_k[:], -1.0, -NEG, ALU.add, ALU.mult).then_inc(masks_ready.sem, 1)
                pool_chain.close()

            def step(i, following):
                pool.wait_ge(*x_norm.at(i, 2 * NC))
                pool.tensor_tensor(R[:], X[:], X[:], ALU.add).then_inc(x_twice.sem, 1)
                wait_apart(pool, passed, *ctx_tok_loaded.at(i))
                pool.tensor_scalar(v2_aug[:, :, :, 0:DH2], ctx_tok[:].rearrange("p c (h d) -> p c h d", h=H2), float(DH2) ** -0.5, None, ALU.mult).then_inc(v2_ready.sem, 1)
                if following:
                    residual(i + 1)
                    wait_apart(pool, passed, *o5_tr.at(i))
                    k_and_masks(i + 1)

            k_and_masks(0)
            residual(0)
            with pool.Fori(0, STEPS - 1) as i:
                step(i, True)
            step(STEPS - 1, False)

        @block.tensor
        def _(pe):
            pe.wait_ge(first_loaded.sem, 16 * len(first_w))
            pe.matmul(bank[1][:, 0:M], w["L0_attn_wqT"][:], xin[:, 0, 0:M], start=True, stop=True)
            pe.matmul(bank[1][:, M:2 * M], w["L0_attn_wkT"][:], xin[:, 0, 0:M], start=True, stop=True).then_inc(mem_qk.sem, 1)
            pe.wait_ge(*mem_q_done.at(0))
            pe.wait_ge(*mem_k_done.at(0))
            pe.wait_ge(*const_ready.at(0))

            def swa_and_gradients(i):
                nu, last_c = chunks(i), chunks(i) - 1
                pe.wait_ge(*xin_loaded.at(i))
                pe.matmul(bank[5][:], w["L0_attn_wqT"][:], xin[:, :, M:KW], start=True, stop=True)
                pe.matmul(bank[6][:], w["L0_attn_wkT"][:], xin[:, :, M:KW], start=True, stop=True).then_inc(qk_ready.sem, 1)
                for b in range(NB):
                    for j, (k0, n) in enumerate([(0, P), (P, P), (2 * P, M)]):
                        last = pe.matmul(v_banks[b][0:n, j * P:(j + 1) * P], xin[:, b, k0:k0 + n],
                                         w["L0_attn_wvT"][:], start=True, stop=True)
                last.then_inc(v_ready.sem, 1)
                pe.wait_ge(*q_copied.at(i))
                pe.wait_ge(*k_copied.at(i))
                pe.wait_ge(*k_copied_too.at(i))

                def scores(u):
                    b, c = units[u]
                    if u >= 2:
                        pe.wait_ge(*max_a.at(i, u - 1))
                    for h in range(H0):
                        dst = s_banks(u)[h // 2]
                        col = (h % 2) * KB
                        if c is None:
                            last = pe.matmul(dst[0:M, col:col + M], qT_mem[:], kpad[:, h, 0, 0:M], start=True, stop=True)
                        else:
                            last = pe.matmul(dst[:, col:col + KB], qT[:, b * S + c * P:b * S + (c + 1) * P],
                                             kpad[:, h, b, c * P:c * P + KB], start=True, stop=True)
                    last.then_inc(scores_a.sem, 1)

                def transposes(u):
                    b, c = units[u]
                    if u == 0:
                        pe.wait_ge(*v_copied.at(i))
                    else:
                        pe.wait_ge(*pTa_copied.at(i, u))
                        pe.wait_ge(*pTb_copied.at(i, u))
                    wait_apart(pe, passed, *norm_a.at(i, u + 1))
                    s = u % 2
                    for h in range(H0):
                        if c is None:
                            last = pe.transpose(bank[3][0:M, h * P:h * P + M], probs[0:M, s, h, 0:M], ident[0:M, 0:M])
                        else:
                            pe.transpose(bank[3][:, h * P:(h + 1) * P], probs[:, s, h, 0:P], ident[:])
                            last = pe.transpose(bank[4][0:WIN, h * P:(h + 1) * P], probs[:, s, h, P:KB], ident[:])
                    last.then_inc(pT_a.sem, 1)

                def outputs(u):
                    b, c = units[u]
                    s = u % 2
                    pe.wait_ge(*pTb_copied.at(i, u + 1))
                    wait_apart(pe, passed, *pTa_copied.at(i, u + 1))
                    if c is None:
                        pe.wait_ge(*z_copied.at(i))
                    for h in range(H0):
                        r = slice(DH0 * h, DH0 * h + DH0)
                        if c is None:
                            last = pe.matmul(bank[1][r, 0:M], vtok[0:M, 0, 0, r], probsT_a[0:M, s, h * P:h * P + M], start=True, stop=True)
                        else:
                            dst = bank[7][r, (b * QC + c) * P:(b * QC + c + 1) * P]
                            pe.matmul(dst, vtok[:, b, c, r], probsT_a[:, s, h * P:(h + 1) * P], start=True, stop=False)
                            last = pe.matmul(dst, vtok[0:WIN, b, c + 1, r], probsT_b[:, s, h * P:(h + 1) * P], start=False, stop=True)
                    last.then_inc(pv_a.sem, 1)

                scores(0)
                if not is_first(i):
                    pe.wait_ge(*grads_added.before(i))
                    pe.wait_ge(*bias_summed.before(i))
                scores(1)
                for u in range(nu):
                    if u + 2 < nu:
                        scores(u + 2)
                    transposes(u)
                    outputs(u)
                    if u == 0:
                        pe.wait_ge(load_w.sem, 16 * len(loads_w))
                    elif u < FC:
                        pe.wait_ge(*z_copied.at(i, u))
                    if u < FC:
                        pe.matmul(bank[1][:], w1T[:, u * P:(u + 1) * P], xin[:, :, M:KW], start=True, stop=True).then_inc(zT_a.sem, 1)
                pe.wait_ge(*max_a.at(i))
                pe.wait_ge(*oT_copied.at(i))
                pe.matmul(bank[0][:], w["L0_attn_woT"][:], oT[:, 0:T], start=True, stop=True).then_inc(swa_ready.sem, 1)
                if is_first(i):
                    pe.matmul(bank[2][:, 0:M], w["L0_attn_woT"][:], oT[:, T:T + M], start=True, stop=True).then_inc(swa_ready.sem, 1)
                    for k in range(FC):
                        last = pe.matmul(bank[1][:, M * (k + 1):M * (k + 2)], w1T[:, k * P:(k + 1) * P], xin[:, 0, 0:M], start=True, stop=True)
                    last.then_inc(zT_a.sem, 1)
                pe.wait_ge(*hT_a.at(i))
                for k in range(FC):
                    last = pe.matmul(bank[3][:], w2T[:, k, :], hT[:, k, 0:T], start=(k == 0), stop=(k == FC - 1))
                if is_first(i):
                    for k in range(FC):
                        last = pe.matmul(bank[4][:, 0:M], w2T[:, k, :], hT[:, k, T:T + M], start=(k == 0), stop=(k == FC - 1))
                last.then_inc(pred_a.sem, 1)
                pe.wait_ge(*e_ready.at(i))
                for c in range(NC):
                    last = pe.transpose(bank[7][:, c * P:(c + 1) * P], eT[:, c * P:(c + 1) * P], ident[:])
                if is_first(i):
                    last = pe.transpose(bank[1][0:M, 0:P], eT[:, T:T + M], ident[:])
                last.then_inc(eT_tr.sem, 1)
                pe.wait_ge(*vT_copied.at(i))
                pe.wait_ge(*etok_copied.at(i))

                def z_and_dh(c):
                    n = P if c < NC else M
                    zb, db = zd_banks(c)
                    if c >= 3:
                        pe.wait_ge(*dz_ready.at(i, c - 2))
                    x_c = xin[:, c // QC, M + (c % QC) * P:M + (c % QC + 1) * P] if c < NC else xin[:, 0, 0:M]
                    pe.matmul(zb[0:n], x_c, w1T[:], start=True, stop=True)
                    pe.matmul(db[0:n], eT[:, c * P:c * P + n], w2[:], start=True, stop=True).then_inc(zd_ready.sem, 1)

                for c in range(3):
                    z_and_dh(c)
                pe.wait_ge(*xtok_loaded.at(i))
                for c in range(last_c + 1):
                    n, s = (P if c < NC else M), c % 2
                    pe.wait_ge(*dz_ready.at(i, c + 1))
                    pe.matmul(bank[0][:], xtok[0:n, c, :], dz[0:n, s], start=(c == 0), stop=(c == last_c))
                    pe.matmul(bank[3][:], etok[0:n, c, :], ht[0:n, s], start=(c == 0), stop=(c == last_c)).then_inc(grads_ready.sem, 1)
                    if c + 3 <= last_c:
                        z_and_dh(c + 3)

            swa_and_gradients(0)
            with pe.Fori(0, STEPS - 1) as i:
                swa_and_gradients(i + 1)
            pe.wait_ge(*grads_added.before(STEPS))
            pe.wait_ge(*bias_summed.before(STEPS))
            for k in range(FC):
                pe.matmul(bank[1][:, k:k + 1], dz_sum[:, k * P:(k + 1) * P], ones[:, 0:1], start=True, stop=True)
            pe.matmul(bank[1][:, FC:FC + 1], e_sum[:], ones[:, 0:1], start=True, stop=True)
            for k in range(FC):
                last = pe.transpose(bank[4][:, k * P:(k + 1) * P], grad2[:, k * P:(k + 1) * P], ident[:])
            last.then_inc(upd_pe.sem, 1)
            pe.wait_ge(*updated.at(0))
            pe.wait_ge(late_loaded.sem, 16 * len(late_w))

            def head(i, n):
                if n == 0:
                    pe.wait_ge(*b_x_loaded.at(i))
                    for k in range(2):
                        pe.matmul(bank[k][:], w1T_new[:, k * P:(k + 1) * P], xT_in[:], start=True, stop=True).then_inc(zT_b.sem, 1)
                if n == 1:
                    for k in range(2, 4):
                        pe.wait_ge(*hT_b.at(i, k - 1))
                        pe.matmul(bank[k - 2][:], w1T_new[:, k * P:(k + 1) * P], xT_in[:], start=True, stop=True).then_inc(zT_b.sem, 1)
                if n == 2:
                    pe.wait_ge(*hT_b.at(i, 3))
                    pe.matmul(bank[0][:], w["L0_attn_lin1T"][:], vT_all[:, bass.ds(i * T, T)], start=True, stop=True).then_inc(lin1.sem, 1)
                    pe.wait_ge(*hT_b.at(i))
                    for k in range(FC):
                        last = pe.matmul(bank[1][:], w2T_new[:, k, :], hT[:, k, 0:T], start=(k == 0), stop=(k == FC - 1))
                    last.then_inc(out_mem.sem, 1)
                if n == 3:
                    pe.wait_ge(*g_ready.at(i, 1))
                    pe.wait_ge(*memT_ready.at(i))
                    pe.matmul(bank[0][:], w["L0_attn_lin2T"][:], memT[:], start=True, stop=True).then_inc(lin_ready.sem, 1)
                if n == 4:
                    pe.wait_ge(*merged.at(i))
                    for c in range(NC):
                        last = pe.transpose(bank[1][:, c * P:(c + 1) * P], g1[:, c * P:(c + 1) * P], ident[:])
                    last.then_inc(merged_tr.sem, 1)
                if n == 5:
                    for c in range(NC):
                        pe.wait_ge(*x_norm_h.at(i, c + 1))
                        last = pe.transpose(bank[0][:, c * P:(c + 1) * P], X1[:, c, :], ident[:])
                    last.then_inc(x_tr_h.sem, 1)
                if n == 6:
                    pe.wait_ge(*xt_h.at(i))
                    pe.matmul(bank[1][:], w["L0_xattn_wqT"][:], XT1[:], start=True, stop=True).then_inc(q_b.sem, 1)

            def keys_and_values(i):
                pe.wait_ge(*ctxT_loaded.at(i))
                pe.matmul(bank[4][:], w["L0_xattn_wkT"][:], ctxT[:], start=True, stop=True).then_inc(k_b.sem, 1)
                for c in range(NC):
                    last = pe.matmul(bank[5][:, c * P:(c + 1) * P], ctxT[:, c * P:(c + 1) * P], w["L0_xattn_wvT"][:], start=True, stop=True)
                last.then_inc(v_b.sem, 1)

            def step(i, following):
                def x_transpose(n):
                    for b in range(NB):
                        for c in range(QC):
                            pe.wait_ge(*x_norm.at(i, n * NC + b * QC + c + 1))
                            last = pe.transpose(bank[7 - b][:, c * P:(c + 1) * P], X[:, b * QC + c, :], ident[:])
                        last.then_inc(x_tr.sem, 1)

                def wait_XT(n, b):
                    pe.wait_ge(*xt_ready.at(i, (n - 1) * NB + b + 1))

                pe.wait_ge(*f_act.before(i))
                pe.wait_ge(*v_aug_ready.at(i))
                pe.wait_ge(*k_stacked.at(i))
                pe.wait_ge(*q_stacked.at(i))
                pe.wait_ge(*masks_ready.at(i))

                def scores_q(n):
                    b, h = n // H1, n % H1
                    if n >= 4 and n != 14:
                        pe.wait_ge(*s_read.at(i, n - 3 if n < 14 else n - 2))
                    for c in range(QC):
                        last = pe.matmul(q_bank(n)[:, c * S:(c + 1) * S],
                                         q_stack[:, h // 2, b * S + c * P:b * S + (c + 1) * P],
                                         k_stack[:, h // 2, h % 2, b * S:(b + 1) * S], start=True, stop=True)
                    last.then_inc(s_ready.sem, 1)

                def maxima_T(m):
                    pe.wait_ge(*s_read.at(i, 8 * (m + 1)))
                    if m > 0:
                        pe.wait_ge(*neg_max_ready.at(i, m))
                    for c in range(QC):
                        last = pe.transpose(bank[3][0:8, c * P:(c + 1) * P], mx[:, c, 8 * (m % 2):8 * (m % 2) + 8], ident[:])
                    last.then_inc(mx_tr.sem, 1)

                def scores_k(n):
                    b, h = n // H1, n % H1
                    if n % 8 == 0:
                        pe.wait_ge(*neg_max_ready.at(i, n // 8 + 1))
                    if n < 2:
                        pe.wait_ge(*s_read.at(i, n + 11))
                    elif n < 20:
                        pe.wait_ge(*exp_ready.at(i, n - 1))
                    else:
                        pe.wait_ge(*exp_ready.at(i, n - 3))
                        if n == 20:
                            pe.wait_ge(*s_read.at(i))
                    for c in range(QC):
                        dst = k_bank(n)[:, c * S:(c + 1) * S]
                        pe.matmul(dst, k_stack[:, h // 2, h % 2, b * S + c * P:b * S + (c + 1) * P],
                                  q_stack[:, h // 2, b * S:(b + 1) * S], start=True, stop=False)
                        pe.matmul(dst, ident_b[:], add_k[:, b * QC + c, :], start=False, stop=False)
                        last = pe.matmul(dst, head_sel[:, h % 8, :], neg_max[:, (n // 8) % 2, :], start=False, stop=True)
                    last.then_inc(sT_ready.sem, 1)

                def values(b, g):
                    pe.wait_ge(*exp_ready.at(i, b * H1 + 4 * g + 4))
                    if b > 0 and g % 2 == 0:
                        pe.wait_ge(*o_copied.at(i, g // 2 + 1))
                    for c in range(QC):
                        for j in range(4):
                            last = pe.matmul(bank[g // 2][32 * j:32 * j + 32, (g % 2) * S:(g % 2 + 1) * S],
                                             v_aug[:, b * QC + c, 4 * g + j, :], pT[:, g % 2, j, c, :],
                                             start=(c == 0), stop=(c == QC - 1))
                    last.then_inc(pv_ready.sem, 1)

                def outputs_T(b):
                    pe.wait_ge(*o_copied.at(i, 2 * b + 2))
                    if b > 0:
                        pe.wait_ge(*o_tok_ready.at(i, b))
                    for g in range(G):
                        for c in range(QC):
                            last = pe.transpose(bank[2 + c][:, g * P:(g + 1) * P], o_heads[:, g, c * P:(c + 1) * P], ident[:])
                    last.then_inc(o_tr.sem, 1)

                for n in range(AHEAD):
                    scores_q(n)
                    if n == 9:
                        maxima_T(0)
                for g in range(NB * G + 1):
                    for n in range(4 * g, min(4 * g + 4, XU)):
                        scores_k(n)
                        ahead = n + AHEAD
                        if ahead < XU:
                            scores_q(ahead)
                        if ahead % 8 == 1 and ahead <= XU + 1:
                            maxima_T(ahead // 8 - 1)
                    if g == 6:
                        outputs_T(0)
                    if g > 0:
                        values((g - 1) // G, (g - 1) % G)
                outputs_T(1)
                pe.wait_ge(*o_tok_ready.at(i))
                for c in range(NC):
                    last = pe.transpose(bank[0][:, c * P:(c + 1) * P], o_tok[:, c, :], ident[:])
                last.then_inc(o_tok_tr.sem, 1)
                pe.wait_ge(*o_T_ready.at(i))
                for c in range(NC):
                    last = pe.matmul(bank[1][:, c * P:(c + 1) * P], o_T[:, c * P:(c + 1) * P], w["L0_xattn_woT"][:], start=True, stop=True)
                last.then_inc(wo_ready.sem, 1)
                x_transpose(1)

                def route(b):
                    for c in range(b * QC, (b + 1) * QC):
                        last = pe.matmul(bank[0][:, c * E:(c + 1) * E], XT[:, c * P:(c + 1) * P], router[:], start=True, stop=True)
                    return last

                def first_up(n, b):
                    return pe.matmul(bank[4 + n][:, b * S:(b + 1) * S], moe_w1[:, 0, n * P:(n + 1) * P], XT[:, b * S:(b + 1) * S], start=True, stop=True)

                wait_XT(1, 0)
                route(0)
                for n in range(2):
                    first_up(n, 0)
                wait_XT(1, 1)
                route(1).then_inc(r_scored.sem, 1)
                for n in range(2):
                    first_up(n, 1).then_inc(up_ready.sem, 1)

                def up(n):
                    e, k = n // FC, n % FC
                    if n >= 4:
                        pe.wait_ge(*he_ready.at(i, n - 3))
                    pe.matmul(bank[4 + n % 4][:], moe_w1[:, e, k * P:(k + 1) * P], XT[:], start=True, stop=True).then_inc(up_ready.sem, 1)

                def down(e):
                    pe.wait_ge(*he_ready.at(i, (e + 1) * FC))
                    if e >= 2:
                        pe.wait_ge(*down_added.at(i, e - 1))
                    for c in range(NC):
                        if e == E - 1 and c == QC:
                            last.then_inc(last_down_b0.sem, 1)
                        for k in range(FC):
                            last = pe.matmul(down_bank(e, c)[:, c * P:(c + 1) * P], he[:, e % 2, k, c * P:(c + 1) * P],
                                             moe_w2[:, e, k, :], start=(k == 0), stop=(k == FC - 1))
                    last.then_inc(down_ready.sem, 1)

                for n in range(2, FC):
                    up(n)
                pe.wait_ge(*picked.at(i))
                for c in range(NC):
                    for j in range(c + 1):
                        pe.matmul(bank[1][:, c * E:(c + 1) * E], before_b[:] if j == c else ones_b[:], picked_b[:, j, :],
                                  start=(j == 0), stop=(j == c))
                for j in range(NC):
                    last = pe.matmul(bank[1][:, NC * E:(NC + 1) * E], ones_b[:], picked_b[:, j, :], start=(j == 0), stop=(j == NC - 1))
                last.then_inc(ranks.sem, 1)
                for e in range(E):
                    if e + 1 < E:
                        for k in range(FC):
                            up((e + 1) * FC + k)
                    if following and e == 0:
                        pe.wait_ge(*gates_ready.at(i))
                        head(i + 1, 0)
                    down(e)
                    if following and e + 1 < HEAD_PARTS:
                        head(i + 1, e + 1)
                x_transpose(2)

                for b in range(NB):
                    wait_XT(2, b)
                    cols = slice(b * S, (b + 1) * S)
                    pe.matmul(bank[0][:, cols], w["L1_attn_W_Q"][:], XT[:, cols], start=True, stop=True)
                    pe.matmul(bank[1][:, cols], w["L1_attn_W_K"][:], XT[:, cols], start=True, stop=True)
                    for c in range(b * QC, (b + 1) * QC):
                        last = pe.matmul(bank[2][:, c * P:(c + 1) * P], XT[:, c * P:(c + 1) * P], w["L1_attn_W_V"][:], start=True, stop=True)
                last.then_inc(qkv_c.sem, 1)
                pe.wait_ge(*aq_ready.at(i, 1))
                pe.wait_ge(*ak_ready.at(i))
                for b in range(NB):
                    for c in range(QC):
                        col = c * P
                        pe.matmul(bank[4 + b][:, col:col + (c + 1) * P], aq[:, b * S + c * P:b * S + (c + 1) * P],
                                  ak[:, b * S:b * S + (c + 1) * P], start=True, stop=False)
                        last = pe.matmul(bank[4 + b][:, col + c * P:col + (c + 1) * P], ident_b[:], future_b[:], start=False, stop=True)
                    last.then_inc(as_ready.sem, 1)
                for b in range(NB):
                    pe.wait_ge(*aexp_ready.at(i, b + 1))
                    for j in range(3):
                        last = pe.transpose(bank[6 + b][:, j * P:(j + 1) * P], ap[:, b, j, :], ident[:])
                    last.then_inc(apT_ready.sem, 1)
                pe.wait_ge(*aq_ready.at(i))
                for b in range(NB):
                    pe.wait_ge(*apT_copied.at(i, b + 1))
                    pe.matmul(bank[3][:, 2 * b * P:(2 * b + 1) * P], apT[:, b, 0:P], av[:, b * QC, :], start=True, stop=True)
                    for j in range(2):
                        last = pe.matmul(bank[3][:, (2 * b + 1) * P:(2 * b + 2) * P], apT[:, b, (1 + j) * P:(2 + j) * P],
                                         av[:, b * QC + j, :], start=(j == 0), stop=(j == 1))
                last.then_inc(apv_ready.sem, 1)

                def gate_products(j):
                    for b in range(NB):
                        if j == 0:
                            wait_XT(3, b)
                        last = pe.matmul(bank[0][0:32 + NB * H2, 0:S], gates_w[:, b, j, :], (XT if j == 0 else ctxT)[:, b * S:(b + 1) * S],
                                         start=(j == 1 and b == 0), stop=(j == 0 and b == NB - 1))
                    return last

                pe.wait_ge(*ctxT_loaded.at(i))
                gate_products(1)
                gate_products(2)
                x_transpose(3)
                last = gate_products(0)
                last.then_inc(pre_ready.sem, 1)

                def context_scores(n):
                    b, h = n // H2, n % H2
                    for lo, q0, width, c in ((0, b * S, S, 0), (S, b * S + P, P, 1)):
                        pe.matmul(m_banks(n)[1][:, lo:lo + width], kpad2[:, h, b * S + c * P:b * S + (c + 1) * P],
                                  XT[:, q0:q0 + width], start=True, stop=True)

                pe.wait_ge(*kpad2_loaded.at(i))
                for n in range(DEEP - 1):
                    context_scores(n)
                wait_apart(pe, passed, *pm_ready.at(i))
                GR = NB * H2
                for c in range(QC):
                    pe.transpose(bank[1][:, c * GR:(c + 1) * GR], ga[:, c * P:(c + 1) * P], ident[0:GR, 0:GR])
                for c in range(QC):
                    last = pe.transpose(bank[1][:, (QC + c) * GR:(QC + c + 1) * GR], gm[:, c * P:(c + 1) * P], ident[0:GR, 0:GR])
                last.then_inc(cols_ready.sem, 1)
                pe.wait_ge(*neg_pm_ready.at(i))
                pe.wait_ge(*v2_ready.at(i))

                def decays(n):
                    b, h = n // H2, n % H2
                    eb = m_banks(n)[0]
                    for lo, q0, width in ((0, 0, S), (S, P, P)):
                        pe.matmul(eb[:, lo:lo + width], head_sel[:, b * H2 + h, :], neg_pm[:, q0:q0 + width], start=True, stop=False)
                        last = pe.matmul(eb[:, lo:lo + P], ident_b[:], past_b[:], start=False, stop=True)
                    last.then_inc(eu_ready.sem, 1)

                def mixed(n):
                    b, g = n // 2, n % 2
                    pe.wait_ge(*c_ready.at(i, 4 * n + 4))
                    for c, lo, q0, width in ((0, 0, 0, S), (1, S, P, P)):
                        for j in range(4):
                            last = pe.matmul(bank[2 + b][32 * j:32 * j + 32, g * S + q0:g * S + q0 + width],
                                             v2_aug[:, b * QC + c, 4 * g + j, :], cT[:, g, j, lo:lo + width],
                                             start=(c == 0), stop=(c == 1))
                    last.then_inc(pv2_ready.sem, 1)

                def back_to_tokens(b):
                    pe.wait_ge(*o5_copied.at(i, b + 1))
                    for c in range(QC):
                        for g in range(2):
                            last = pe.transpose(bank[2 + b][:, (c * 2 + g) * P:(c * 2 + g + 1) * P], o5[:, b, g, c * P:(c + 1) * P], ident[:])
                    last.then_inc(o5_tr.sem, 1)

                for n in range(MU):
                    if n >= DEEP:
                        pe.wait_ge(*c_ready.at(i, n - DEEP + 1))
                    if n == DEEP - 1:
                        pe.wait_ge(*cols_copied.at(i))
                    if n >= DEEP - 1:
                        context_scores(n)
                    decays(n)
                    if n >= 5 and n % 4 == 1:
                        mixed(n // 4 - 1)
                    if n == 12:
                        back_to_tokens(0)
                mixed(3)
                back_to_tokens(1)
                if following:
                    keys_and_values(i + 1)
                x_transpose(4)

                for b in range(NB):
                    for c in range(QC):
                        last = pe.matmul(bank[0][:, b * P:(b + 1) * P], X[:, b * QC + c, :], ones[:], start=(c == 0), stop=(c == QC - 1))
                last.then_inc(pooled_ready.sem, 1)
                pe.wait_ge(*fb_ready.at(0))
                if following:
                    pe.wait_ge(*kf_ready.at(i + 1))
                for n, (c, half) in enumerate(f_units):
                    if n < NB:
                        wait_XT(4, n)
                    if n == 1:
                        pe.wait_ge(*rep_ready.at(i))
                        for b in range(NB):
                            last = pe.matmul(bank[0][:, b * E:(b + 1) * E], pooled_rep[:, b, :], ffn_gw[:], start=True, stop=True)
                        last.then_inc(fl_ready.sem, 1)
                        if following:
                            pe.wait_ge(*v_aug_ready.at(i + 1))
                    if n >= 4:
                        pe.wait_ge(*f_act.at(i, n - 3))
                    pe.matmul(bank[4 + n % 4][:], XT[:, c * P:(c + 1) * P], ffn_w[:, half * 512:(half + 1) * 512], start=True, stop=False)
                    pe.matmul(bank[4 + n % 4][:], row_sel[:], fb_parts[:, half * 512:(half + 1) * 512], start=False, stop=True).then_inc(f_ready.sem, 1)

            for n in range(HEAD_PARTS):
                head(0, n)
                if n == 0:
                    keys_and_values(0)
            with pe.Fori(0, STEPS - 1) as i:
                step(i, True)
            step(STEPS - 1, False)

        @block.scalar
        def _(act):
            f_act.prime(act)
            act.wait_ge(*mem_qk.at(0))
            act.copy(qT_mem[:], bank[1][:, 0:M]).then_inc(mem_q_done.sem, 1)

            def swa_and_gradients(i):
                nu = chunks(i)
                act.wait_ge(*qk_ready.at(i))
                act.copy(qT[:], bank[5][:]).then_inc(q_copied.sem, 1)
                for h in range(2, H0):
                    r = slice(DH0 * h, DH0 * h + DH0)
                    act.copy(kpad[r, h, :, M:KW], bank[6][r].rearrange("p (b t) -> p b t", b=NB)).then_inc(k_copied_too.sem, 1)
                act.wait_ge(*v_ready.at(i))
                for b in range(NB):
                    for j, n in enumerate([P, P, M]):
                        act.copy(vtok[0:n, b, j, :], v_banks[b][0:n, j * P:(j + 1) * P]).then_inc(v_copied.sem, 1)

                def exponentials(u):
                    n, keys, s = (M, M, u % 2) if units[u][1] is None else (P, KB, u % 2)
                    act.wait_ge(*max_a.at(i, u + 1))
                    for h in range(H0):
                        last = act.activation(probs[0:n, s, h, 0:keys], probs[0:n, s, h, 0:keys], ACT.Exp,
                                              bias=stats[0:n, s, 4 + h:5 + h], scale=float(DH0) ** -0.5,
                                              accum_out=stats[0:n, s, 8 + h:9 + h])
                    last.then_inc(exp_a.sem, 1)

                exponentials(0)
                exponentials(1)
                for u, (b, c) in enumerate(units[:nu]):
                    s = u % 2
                    act.wait_ge(*pT_a.at(i, u + 1))
                    if c is None:
                        act.copy(probsT_a[0:M, s].rearrange("p (h q) -> p h q", h=H0)[:, :, 0:M],
                                 bank[3][0:M].rearrange("p (h q) -> p h q", h=H0)[:, :, 0:M]).then_inc(pTa_copied.sem, 1)
                    else:
                        act.copy(probsT_a[:, s], bank[3][:]).then_inc(pTa_copied.sem, 1)
                    if u + 2 < nu:
                        exponentials(u + 2)
                    if u < FC:
                        act.wait_ge(*zT_a.at(i, u + 1))
                        act.activation(hT[:, u, 0:T], bank[1][:], ACT.Identity, bias=b1[:, u:u + 1]).then_inc(z_copied.sem, 1)
                act.wait_ge(*pv_a.at(i))
                act.copy(oT[:, 0:T], bank[7][:]).then_inc(oT_copied.sem, 1)
                if is_first(i):
                    act.copy(oT[:, T:T + M], bank[1][:, 0:M]).then_inc(oT_copied.sem, 1)
                act.wait_ge(*z_copied.at(i))
                for k in range(FC):
                    act.activation(hT[:, k, 0:T], hT[:, k, 0:T], ACT.Silu).then_inc(hT_a.sem, 1)
                if is_first(i):
                    act.wait_ge(*zT_a.at(i))
                for k in range(FC if is_first(i) else 0):
                    act.activation(hT[:, k, T:T + M], bank[1][:, M * (k + 1):M * (k + 2)], ACT.Silu, bias=b1[:, k:k + 1]).then_inc(hT_a.sem, 1)
                if is_first(i):
                    act.wait_ge(*swa_ready.at(i))
                    act.copy(vT_mem[:], bank[2][:, 0:M]).then_inc(vT_copied.sem, 1)
                act.wait_ge(*eT_tr.at(i))
                act.copy(etok[:, 0:NC, :], bank[7][:].rearrange("p (c d) -> p c d", c=NC)).then_inc(etok_copied.sem, 1)
                if is_first(i):
                    act.copy(etok[0:M, NC, :], bank[1][0:M, 0:P]).then_inc(etok_copied.sem, 1)
                chain = Chain(act, act_a, i)
                for c in range(chunks(i)):
                    n, s = (P if c < NC else M), c % 2
                    act.wait_ge(*z_biased.at(i, c + 1))
                    if c >= 2:
                        act.wait_ge(*dz_ready.at(i, c - 1))
                    chain.link(act.activation(sg[0:n, s], zt[0:n, s], ACT.Tanh, scale=0.5))
                    act.activation(sg[0:n, s], sg[0:n, s], ACT.Copy, scale=0.5, bias=0.5).then_inc(sg_ready.sem, 1)
                chain.close()

            swa_and_gradients(0)
            with act.Fori(0, STEPS - 1) as i:
                swa_and_gradients(i + 1)

            def roots(i, n):
                for b in range(NB):
                    cc = slice(b * QC, (b + 1) * QC)
                    act.wait_ge(*var_ready.at(i, n * NB + b + 1))
                    act.activation(deviation[:, cc], mv[:, cc, 1], ACT.Sqrt, bias=eps[:, 0:1]).then_inc(rstd_ready.sem, 1)

            def head(i, n):
                if n in (0, 1):
                    for k in range(2 * n, 2 * n + 2):
                        act.wait_ge(*zT_b.at(i, k + 1))
                        act.activation(hT[:, k, 0:T], bank[k % 2][:], ACT.Silu, bias=b1_new[:, k:k + 1]).then_inc(hT_b.sem, 1)
                if n == 2:
                    act.wait_ge(*lin1.at(i))
                    act.activation(g1[:], bank[0][:], ACT.Tanh, scale=0.5).then_inc(g_ready.sem, 1)
                if n == 3:
                    act.wait_ge(*lin_ready.at(i))
                    act.activation(g2[:], bank[0][:], ACT.Tanh, scale=0.5).then_inc(g_ready.sem, 1)
                if n == 4:
                    act.wait_ge(*var_h.at(i))
                    act.activation(deviation_h[:], mv_h[:, :, 1], ACT.Sqrt, bias=eps[:, 0:1]).then_inc(rstd_h.sem, 1)
                if n == 5:
                    act.wait_ge(*x_tr_h.at(i))
                    act.copy(XT1[:], bank[0][:]).then_inc(xt_h.sem, 1)

            def keys(i):
                act.wait_ge(*k_b.at(i))
                act.activation(kf[:], bank[4][:], ACT.Identity, bias=x_bk[:, 0:1]).then_inc(kf_ready.sem, 1)
                act.wait_ge(*kf_ready.at(i))
                act.copy(k_parts[:, 0, :], kf[:]).then_inc(kh_ready.sem, 1)

            def step(i, following):
                def root(n):
                    roots(i, n)

                def x_copy(n):
                    root(n)
                    for b in range(NB):
                        act.wait_ge(*x_tr.at(i, (n - 1) * NB + b + 1))
                        act.copy(XT[:, b * S:(b + 1) * S], bank[7 - b][:, 0:S]).then_inc(xt_ready.sem, 1)

                def copy_outputs(b, half):
                    act.wait_ge(*pv_ready.at(i, b * G + 2 * half + 2))
                    if b > 0 and half == 0:
                        act.wait_ge(*o_tr.at(i, b))
                    act.copy(o_heads[:, 2 * half:2 * half + 2, :], bank[half][:].rearrange("p (g q) -> p g q", g=2)).then_inc(o_copied.sem, 1)

                for n in range(XU):
                    g, j = n // 4, n % 4
                    act.wait_ge(*sT_ready.at(i, n + 1))
                    if j == 0 and g >= 2:
                        act.wait_ge(*pv_ready.at(i, g - 1))
                    act.activation(pT[:, g % 2, j], k_bank(n)[:].rearrange("p (c q) -> p c q", c=QC), ACT.Exp).then_inc(exp_ready.sem, 1)
                    if g >= 2 and g % 2 == 0 and j == 3:
                        copy_outputs((g - 2) // G, (g - 2) // 2 % 2)
                copy_outputs(1, 1)
                root(0)
                act.wait_ge(*o_tok_tr.at(i))
                act.copy(o_T[:], bank[0][:]).then_inc(o_T_ready.sem, 1)
                x_copy(1)
                act.wait_ge(*share_diff.at(i))
                act.activation(share[:, 1, :], share[:, 0, :], ACT.Exp).then_inc(share_exp.sem, 1)
                for n in range(E * FC):
                    e, k = n // FC, n % FC
                    act.wait_ge(*up_ready.at(i, n + 1))
                    if k == 0 and e >= 2:
                        act.wait_ge(*down_ready.at(i, e - 1))
                    act.activation(he[:, e % 2, k, :], bank[4 + n % 4][:], ACT.Silu).then_inc(he_ready.sem, 1)
                    if following and e > 0 and k == FC - 1:
                        if e == 1:
                            head(i + 1, 0)
                        head(i + 1, e)
                x_copy(2)
                act.wait_ge(*qkv_c.at(i))
                act.copy(aq[:], bank[0][:]).then_inc(aq_ready.sem, 1)
                act.copy(av[:], bank[2][:].rearrange("p (c d) -> p c d", c=NC)).then_inc(aq_ready.sem, 1)
                scale = float(D) ** -0.5
                for b in range(NB):
                    act.wait_ge(*amax_ready.at(i, b + 1))
                    act.activation(ap[:, b, 0, :], bank[4 + b][:, 0:P], ACT.Exp, bias=ast[:, 1, 2 * b:2 * b + 1], scale=scale,
                                   accum_out=ast[:, 2, 2 * b:2 * b + 1])
                    act.activation(ap[:, b, 1:3, :], bank[4 + b][:, P:3 * P].rearrange("p (j k) -> p j k", j=2), ACT.Exp,
                                   bias=ast[:, 1, 2 * b + 1:2 * b + 2], scale=scale,
                                   accum_out=ast[:, 2, 2 * b + 1:2 * b + 2]).then_inc(aexp_ready.sem, 1)
                for b in range(NB):
                    act.wait_ge(*apT_ready.at(i, b + 1))
                    act.copy(apT[:, b, :], bank[6 + b][:, 0:3 * P]).then_inc(apT_copied.sem, 1)
                x_copy(3)
                act.wait_ge(*abs_ready.at(i))
                act.activation(cs[:], gl[:], ACT.Exp, scale=-1.0).then_inc(ef_ready.sem, 1)
                act.wait_ge(*ef_ready.at(i))
                act.activation(gl[:], cs[:], ACT.Ln, bias=1.0).then_inc(ln_ready.sem, 1)
                act.wait_ge(*cols_ready.at(i))
                cols = bank[1][:, 0:2 * NC * H2].rearrange("p (n c b h) -> p n c b h", n=2, c=QC, b=NB)
                act.activation(em_col[:].rearrange("p (b c) h -> p c b h", b=NB), cols[:, 1], ACT.Exp, scale=-1.0).then_inc(cols_copied.sem, 1)
                act.copy(a_col[:].rearrange("p (b c) h -> p c b h", b=NB), cols[:, 0]).then_inc(cols_copied.sem, 1)
                act.wait_ge(*cols_copied.at(i))

                def copy_mixed(b):
                    act.wait_ge(*pv2_ready.at(i, 2 * b + 2))
                    act.copy(o5[:, b], bank[2 + b][:].rearrange("p (g q) -> p g q", g=2)).then_inc(o5_copied.sem, 1)

                for n in range(MU):
                    b, h = n // H2, n % H2
                    act.wait_ge(*eu_ready.at(i, n + 1))
                    if n >= DEEP:
                        act.wait_ge(*c_ready.at(i, n - DEEP + 1))
                    eb = m_banks(n)[0]
                    act.activation(decay[:, n % DEEP, 0:S], eb[:, 0:S], ACT.Exp, bias=a_col[:, b * QC, h:h + 1])
                    act.activation(decay[:, n % DEEP, S:S + P], eb[:, S:S + P], ACT.Exp, bias=a_col[:, b * QC + 1, h:h + 1]).then_inc(decay_ready.sem, 1)
                    if n == 10:
                        copy_mixed(0)
                copy_mixed(1)
                if following:
                    act.wait_ge(*q_parts_ready.at(i + 1))
                    keys(i + 1)
                act.wait_ge(*var2_ready.at(i))
                act.activation(hrs[:], hm[:, 0, :], ACT.Sqrt, bias=eps[:, 0:1], scale=1.0 / DH2).then_inc(rstd2_ready.sem, 1)
                x_copy(4)
                act.wait_ge(*pooled_ready.at(i))
                act.activation(pooled_rep[:], bank[0][:, 0:NB * P].rearrange("p (b q) -> p b q", b=NB), ACT.Copy, scale=1.0 / S).then_inc(rep_ready.sem, 1)
                act.wait_ge(*fmax_ready.at(i))
                act.activation(fe[:], fl[:], ACT.Exp).then_inc(fe_ready.sem, 1)
                for n in range(FU):
                    act.wait_ge(*f_ready.at(i, n + 1))
                    if n >= 4:
                        act.wait_ge(*f_added.at(i, n // 2 - 1))
                    act.activation(gl_act[:, n % 4], bank[4 + n % 4][:], ACT.Gelu).then_inc(f_act.sem, 1)

            for n in range(HEAD_PARTS):
                if n == 2:
                    act.wait_ge(*k_parts_ready.at(0))
                head(0, n)
                if n == 0:
                    keys(0)
            act.wait_ge(*fb_ready.at(0))
            with act.Fori(0, STEPS - 1) as i:
                step(i, True)
            step(STEPS - 1, False)
            roots(STEPS, 0)

        @block.vector
        def _(dve):
            for t in (gates_w, dz_sum, e_sum, grad1, grad2):
                last = dve.memset(t[:], 0.0)
            last.then_inc(sums_zero.sem, 1)
            dve.wait_ge(*zeros_made.at(0, 1))
            dve.wait_ge(*mem_q_done.at(0))
            for h in range(H0):
                r = slice(DH0 * h, DH0 * h + DH0)
                for b in range(NB):
                    last = dve.tensor_copy(kpad[r, h, b, 0:M], bank[1][r, M:2 * M])
            last.then_inc(mem_k_done.sem, 1)
            dve.wait_ge(*const_ready.at(0))

            def swa_and_gradients(i):
                nu = chunks(i)
                chain = Chain(dve, dve_a, i)
                dve.wait_ge(*qk_ready.at(i))
                for h in range(2):
                    r = slice(DH0 * h, DH0 * h + DH0)
                    dve.tensor_copy(kpad[r, h, :, M:KW], bank[6][r].rearrange("p (b t) -> p b t", b=NB)).then_inc(k_copied.sem, 1)

                def maxima(u):
                    b, c = units[u]
                    n, keys, s = (M, M, u % 2) if c is None else (P, KB, u % 2)
                    if u >= 2:
                        dve.wait_ge(*pT_a.at(i, u - 1))
                    wait_apart(dve, passed, *scores_a.at(i, u + 1))
                    mask = mem_mask if c is None else window
                    for h in range(H0):
                        src = s_banks(u)[h // 2][0:n, (h % 2) * KB:(h % 2) * KB + keys]
                        last = dve.tensor_tensor_reduce(probs[0:n, s, h, 0:keys], src, mask[0:n, 0:keys], 1.0, NEG,
                                                        ALU.add, ALU.max, stats[0:n, s, h:h + 1])
                    chain.link(last)
                    dve.tensor_scalar(stats[0:n, s, 4:8], stats[0:n, s, 0:4], -float(DH0) ** -0.5, None, ALU.mult).then_inc(max_a.sem, 1)

                def normalise(u):
                    n, keys, s = (M, M, u % 2) if units[u][1] is None else (P, KB, u % 2)
                    dve.wait_ge(*exp_a.at(i, u + 1))
                    chain.link(dve.reciprocal(stats[0:n, s, 12:16], stats[0:n, s, 8:12]))
                    dve.tensor_tensor(probs[0:n, s, :, 0:keys], probs[0:n, s, :, 0:keys],
                                      stats[0:n, s, 12:16].unsqueeze(2).to_broadcast([n, H0, keys]), ALU.mult).then_inc(norm_a.sem, 1)

                maxima(0)
                maxima(1)
                normalise(0)
                for u, (b, c) in enumerate(units[:nu]):
                    s = u % 2
                    dve.wait_ge(*pT_a.at(i, u + 1))
                    if c is None:
                        dve.memset(probsT_b[:, s, 0:1], 0.0).then_inc(pTb_copied.sem, 1)
                    else:
                        dve.tensor_copy(probsT_b[:, s], bank[4][0:WIN]).then_inc(pTb_copied.sem, 1)
                    if u + 2 < nu:
                        maxima(u + 2)
                    if u + 1 < nu:
                        normalise(u + 1)
                dve.wait_ge(*swa_ready.at(i, 1))
                dve.tensor_copy(vT_all[:, bass.ds(i * T, T)], bank[0][:]).then_inc(vT_copied.sem, 1)
                dve.wait_ge(*vT_copied.at(i))
                dve.wait_ge(*pred_a.at(i))
                last = dve.scalar_tensor_tensor(eT[:, 0:T], bank[3][:], b2[:, 0:1], vT_all[:, bass.ds(i * T, T)], ALU.add, ALU.subtract)
                if is_first(i):
                    chain.link(dve.scalar_tensor_tensor(eT[:, T:T + M], bank[4][:, 0:M], b2[:, 0:1], vT_mem[:], ALU.add, ALU.subtract))
                    last = dve.tensor_scalar(eT[:, T:T + M], eT[:, T:T + M], float(B), None, ALU.mult)
                last.then_inc(e_ready.sem, 1)

                def biased(c):
                    n, s = (P if c < NC else M), c % 2
                    dve.wait_ge(*zd_ready.at(i, c + 1))
                    dve.tensor_tensor(zt[0:n, s], zd_banks(c)[0][0:n], b1_rows[0:n], ALU.add).then_inc(z_biased.sem, 1)

                biased(0)
                for c in range(chunks(i)):
                    n, s = (P if c < NC else M), c % 2
                    if c + 1 < chunks(i):
                        biased(c + 1)
                    dve.wait_ge(*sg_ready.at(i, c + 1))
                    if c >= 2:
                        dve.wait_ge(*grads_ready.at(i, c - 1))
                        dve.wait_ge(*bias_summed.at(i, c - 1))
                    chain.link(dve.tensor_tensor(ht[0:n, s], zt[0:n, s], sg[0:n, s], ALU.mult))
                    chain.link(dve.scalar_tensor_tensor(sl[0:n, s], sg[0:n, s], -1.0, ht[0:n, s], ALU.add, ALU.mult))
                    chain.link(dve.tensor_tensor(sl[0:n, s], sg[0:n, s], sl[0:n, s], ALU.subtract))
                    dve.tensor_tensor(dz[0:n, s], zd_banks(c)[1][0:n], sl[0:n, s], ALU.mult).then_inc(dz_ready.sem, 1)
                dve.wait_ge(*grads_ready.at(i))
                dve.tensor_tensor(grad1[:], grad1[:], bank[0][:], ALU.add)
                dve.tensor_tensor(grad2[:], grad2[:], bank[3][:], ALU.add).then_inc(grads_added.sem, 1)
                chain.close()

            swa_and_gradients(0)
            with dve.Fori(0, STEPS - 1) as i:
                swa_and_gradients(i + 1)
            dve.tensor_scalar(rate[:, 2:3], rate[:, 0:1], -1.0, 1.0, ALU.mult, ALU.add)
            dve.tensor_scalar(rate[:, 3:4], rate[:, 1:2], -1.0, None, ALU.mult).then_inc(upd_dve.sem, 1)
            dve.wait_ge(upd_dve.sem, 1)
            dve.wait_ge(*upd_pe.at(0))
            pairs = [(w1T_new[:], w1T[:], grad1[:]),
                     (w2T_new[:].rearrange("p k d -> p (k d)"), w2T[:].rearrange("p k d -> p (k d)"), bank[4][:]),
                     (b1_new[:], b1[:], bank[1][:, 0:FC]), (b2_new[:], b2[:], bank[1][:, FC:FC + 1])]
            for new, old, grad in pairs:
                last = dve.tensor_scalar(new, old, rate[:, 2:3], None, ALU.mult)
            last.then_inc(upd_dve.sem, 1)
            dve.wait_ge(upd_dve.sem, 2)
            for new, old, grad in pairs:
                last = dve.scalar_tensor_tensor(new, grad, rate[:, 3:4], new, ALU.mult, ALU.add)
            last.then_inc(updated.sem, 1)
            dve.wait_ge(late_loaded.sem, 16 * len(late_w))
            pro = Chain(dve, dve_pro, 0)
            pro.link(dve.tensor_copy(fb_parts[0:1, :], ffn_b[:]))
            pro.link(dve.tensor_tensor(fb_row[:, 0], ffn_b[:], fb_parts[0:1, :], ALU.subtract))
            pro.link(dve.tensor_copy(fb_m[:], fb_row[:, 0]))
            dve.tensor_copy(fb_parts[32:33, :], fb_m[:])
            dve.tensor_tensor(fb_parts[64:65, :], fb_row[:, 0], fb_m[:], ALU.subtract).then_inc(fb_ready.sem, 1)

            def statistics(chain, x=R, st=bn, m=mv, ready=var_ready, parts=NB, done=None):
                part = [range(p * NC // parts, (p + 1) * NC // parts) for p in range(parts)]
                marks = []
                for p in range(parts):
                    if done:
                        dve.wait_ge(*done[p])
                    for c in part[p]:
                        last = dve.bn_stats(st[:, c, :], x[:, c, :])
                    marks.append(chain.mark(last))
                for p in range(parts):
                    wait_apart(dve, passed, *chain.links.at(chain.step, marks[p]))
                    for c in part[p]:
                        last = dve.bn_aggr(m[:, c, :], st[:, c, :])
                    last.then_inc(ready.sem, 1)

            def normalised(chain, i, n, dst):
                for b in range(NB):
                    dve.wait_ge(*rstd_ready.at(i, n * NB + b + 1))
                    cc = slice(b * QC, (b + 1) * QC)
                    chain.link(dve.reciprocal(rstd[:, cc], deviation[:, cc]))
                    for c in range(b * QC, (b + 1) * QC):
                        dve.tensor_scalar(dst[:, c, :], R[:, c, :], mv[:, c, 0:1], rstd[:, c:c + 1], ALU.subtract, ALU.mult).then_inc(x_norm.sem, 1)

            dve.memset(R[:], 0.0).then_inc(r_zero.sem, 1)
            dve.wait_ge(*r_zero.at(0))

            def head(i, n, chain):
                if n == 2:
                    dve.wait_ge(*g_ready.at(i, 1))
                    dve.scalar_tensor_tensor(g1[:], g1[:], 1.0, vT_all[:, bass.ds(i * T, T)], ALU.add, ALU.mult)
                    dve.wait_ge(*out_mem.at(i))
                    dve.tensor_scalar(memT[:], bank[1][:], b2_new[:, 0:1], None, ALU.add).then_inc(memT_ready.sem, 1)
                if n == 3:
                    dve.wait_ge(*g_ready.at(i))
                    chain.link(dve.scalar_tensor_tensor(g2[:], g2[:], 1.0, memT[:], ALU.add, ALU.mult))
                    dve.tensor_tensor(g1[:], g1[:], g2[:], ALU.add).then_inc(merged.sem, 1)
                if n == 4:
                    dve.wait_ge(*merged_tr.at(i))
                    dve.scalar_tensor_tensor(R1[:], bank[1][:].rearrange("p (c d) -> p c d", c=NC), 0.5, x_in[:], ALU.mult, ALU.add).then_inc(x_in_used.sem, 1)
                    dve.wait_ge(*x_in_used.at(i))
                    statistics(chain, R1, bn_h, mv_h, var_h, 1)
                    dve.wait_ge(*rstd_h.at(i))
                    chain.link(dve.reciprocal(recip_h[:], deviation_h[:]))
                    for c in range(NC):
                        dve.tensor_scalar(X1[:, c, :], R1[:, c, :], mv_h[:, c, 0:1], recip_h[:, c:c + 1], ALU.subtract, ALU.mult).then_inc(x_norm_h.sem, 1)
                if n == 6:
                    dve.wait_ge(*q_b.at(i))
                    chain.link(dve.tensor_scalar(qf[:], bank[1][:], x_bq[:, 0:1], float(DH1) ** -0.5, ALU.add, ALU.mult))
                    dve.tensor_copy(q_parts[:, 0, :], qf[:]).then_inc(q_parts_ready.sem, 1)
                    dve.wait_ge(*q_parts_ready.at(i, 1))
                    chain.link(dve.tensor_tensor(qr[:], qf[:], q_parts[:, 0, :], ALU.subtract))
                    dve.tensor_copy(q_parts[:, 1, :], qr[:]).then_inc(q_parts_ready.sem, 1)
                    dve.wait_ge(*q_parts_ready.at(i, 2))
                    dve.tensor_tensor(q_parts[:, 2, :], qr[:], q_parts[:, 1, :], ALU.subtract).then_inc(q_parts_ready.sem, 1)
                    chain.close()

            def values(i):
                dve.wait_ge(*v_b.at(i))
                dve.tensor_tensor(v_aug[:, :, :, 0:DH1], bank[5][:].rearrange("p (c h d) -> p c h d", c=NC, h=H1),
                                  x_bv_rows[:].rearrange("p (h d) -> p h d", h=H1).unsqueeze(1).to_broadcast([P, NC, H1, DH1]), ALU.add).then_inc(v_aug_ready.sem, 1)

            def step(i, following):
                chain = Chain(dve, dve_b, i)
                head_chain = Chain(dve, dve_h, i + 1) if following else None

                def layernorm(n, done):
                    statistics(chain, done=done)
                    normalised(chain, i, n, X)

                dve.wait_ge(*masks_ready.at(i))

                def negated(m):
                    dve.wait_ge(*mx_tr.at(i, m + 1))
                    if m >= 2:
                        dve.wait_ge(*sT_ready.at(i, 8 * (m - 1)))
                    mt, dst = bank[3][0:8, 0:S], neg_max[:, m % 2]
                    chain.link(dve.tensor_scalar(dst[0:8], mt, -1.0, None, ALU.mult))
                    chain.link(dve.scalar_tensor_tensor(neg_r[0:8], mt, -1.0, dst[0:8], ALU.mult, ALU.subtract))
                    chain.link(dve.tensor_copy(neg_m[0:8], neg_r[0:8]))
                    dve.tensor_copy(dst[32:40], neg_m[0:8])
                    dve.tensor_tensor(dst[64:72], neg_r[0:8], neg_m[0:8], ALU.subtract).then_inc(neg_max_ready.sem, 1)

                for n in range(XU):
                    b, h = n // H1, n % H1
                    wait_apart(dve, passed, *s_ready.at(i, n + 1))
                    for c in range(QC):
                        sc = q_bank(n)[:, c * S:(c + 1) * S]
                        last = dve.tensor_tensor_reduce(sc, sc, add_q[:, b * QC + c, :], 1.0,
                                                        2.0 * NEG, ALU.add, ALU.max, mx[:, c, h:h + 1])
                    last.then_inc(s_read.sem, 1)
                    if n % 8 == 1 and n > 8:
                        negated(n // 8 - 1)
                negated(MG - 1)
                statistics(chain)
                dve.wait_ge(out_saved.sem, 16 * i + 16)
                for b in range(NB):
                    dve.wait_ge(*o_tr.at(i, b + 1))
                    heads = [bank[2 + c][:].rearrange("p (h j) -> p h j", h=H1) for c in range(QC)]
                    for c in range(QC):
                        last = dve.reciprocal(rec[:, c, :], heads[c][:, :, DH1])
                    chain.link(last)
                    for c in range(QC):
                        last = dve.tensor_tensor(o_tok[:, b * QC + c, :].rearrange("p (h d) -> p h d", h=H1), heads[c][:, :, 0:DH1],
                                                 rec[:, c, :].unsqueeze(2).to_broadcast([P, H1, DH1]), ALU.mult)
                    last.then_inc(o_tok_ready.sem, 1)
                normalised(chain, i, 0, Y)
                dve.wait_ge(*x_norm.at(i, NC))
                dve.wait_ge(*wo_ready.at(i))
                dve.wait_ge(*x_plus.at(i))
                done = []
                for b in range(NB):
                    cc = slice(b * QC, (b + 1) * QC)
                    ins = dve.tensor_tensor(R[:, cc], R1[:, cc], bank[1][:, b * S:(b + 1) * S].rearrange("p (c d) -> p c d", c=QC), ALU.add)
                    done.append(dve_b.at(i, chain.mark(ins)))
                layernorm(1, done)

                dve.wait_ge(*r_scored.at(i))
                chain.link(dve.tensor_copy(logits[:], bank[0][:, 0:NC * E].rearrange("p (c e) -> p c e", c=NC)), passed)
                for c in range(NC):
                    last = dve.max(top[:, c, :], logits[:, c, :])
                chain.link(last, passed)
                for c in range(NC):
                    last = dve.max_index(top_i[:, c, :], top[:, c, :], logits[:, c, :])
                dve.tensor_tensor(share[:, 0, :], top[:, :, 1], top[:, :, 0], ALU.subtract).then_inc(share_diff.sem, 1)
                dve.wait_ge(*share_diff.at(i))
                chain.link(dve.tensor_copy(top_f[:], top_i[:, :, 0:2]))
                for j in range(2):
                    last = dve.tensor_tensor(pick[:, j], iota_e[:].unsqueeze(1).to_broadcast([P, NC, E]),
                                             top_f[:, :, j:j + 1].to_broadcast([P, NC, E]), ALU.is_equal)
                chain.link(last)
                dve.tensor_tensor(picked_b[:], pick[:, 0], pick[:, 1], ALU.add).then_inc(picked.sem, 1)
                dve.wait_ge(*share_exp.at(i))
                chain.link(dve.tensor_scalar(share[:, 0, :], share[:, 1, :], 1.0, None, ALU.add))
                chain.link(dve.reciprocal(share[:, 2, :], share[:, 0, :]))
                chain.link(dve.tensor_tensor(share[:, 3, :], share[:, 1, :], share[:, 2, :], ALU.mult))
                for j in range(2):
                    last = dve.tensor_tensor(pick[:, j], pick[:, j], share[:, 2 + j, :].unsqueeze(2).to_broadcast([P, NC, E]), ALU.mult)
                dve.wait_ge(*ranks.at(i))
                chain.link(dve.tensor_tensor(rank[:], bank[1][:, 0:NC * E].rearrange("p (c e) -> p c e", c=NC),
                                             seen[:].unsqueeze(1).to_broadcast([P, NC, E]), ALU.add))
                dve.tensor_tensor(seen[:], bank[1][:, NC * E:(NC + 1) * E], seen[:], ALU.add)
                chain.link(dve.tensor_tensor(gate[:], pick[:, 0], pick[:, 1], ALU.add))
                dve.scalar_tensor_tensor(gate[:], rank[:], float(CAP), gate[:], ALU.is_lt, ALU.mult).then_inc(gates_ready.sem, 1)
                dve.wait_ge(*gates_ready.at(i))
                dve.wait_ge(*x_twice.at(i))
                for e in range(E):
                    if e < E - 1:
                        dve.wait_ge(*down_ready.at(i, e + 1))
                    for c in range(NC):
                        if e == E - 1 and c == 0:
                            dve.wait_ge(*last_down_b0.at(i))
                        if e == E - 1 and c == QC:
                            b0_done = dve_b.at(i, chain.mark(last))
                            dve.wait_ge(*down_ready.at(i))
                        last = dve.scalar_tensor_tensor(R[:, c, :], down_bank(e, c)[:, c * P:(c + 1) * P], gate[:, c, e:e + 1],
                                                        R[:, c, :], ALU.mult, ALU.add)
                    last.then_inc(down_added.sem, 1)
                    if following and e + 1 < HEAD_PARTS:
                        head(i + 1, e + 1, head_chain)
                    if e < E - 1:
                        dve.wait_ge(*down_added.at(i, e + 1))
                layernorm(2, [b0_done, down_added.at(i)])

                dve.wait_ge(*qkv_c.at(i))
                dve.tensor_copy(ak[:], bank[1][:]).then_inc(ak_ready.sem, 1)
                for b in range(NB):
                    dve.wait_ge(*as_ready.at(i, b + 1))
                    dve.tensor_reduce(ast[:, 0, 2 * b:2 * b + 1], bank[4 + b][:, 0:P], AX.X, ALU.max)
                    chain.link(dve.tensor_reduce(ast[:, 0, 2 * b + 1:2 * b + 2], bank[4 + b][:, P:3 * P], AX.X, ALU.max))
                    dve.tensor_scalar(ast[:, 1, 2 * b:2 * b + 2], ast[:, 0, 2 * b:2 * b + 2], -float(D) ** -0.5, None, ALU.mult).then_inc(amax_ready.sem, 1)
                dve.wait_ge(*aexp_ready.at(i))
                chain.link(dve.reciprocal(ast[:, 3, :], ast[:, 2, :]))
                dve.wait_ge(*apv_ready.at(i))
                done = []
                for c in range(NC):
                    last = dve.scalar_tensor_tensor(R[:, c, :], bank[3][:, c * P:(c + 1) * P], ast[:, 3, c:c + 1], X[:, c, :], ALU.mult, ALU.add)
                    if c % QC == QC - 1:
                        done.append(dve_b.at(i, chain.mark(last)))
                layernorm(3, done)

                dve.wait_ge(*pre_ready.at(i))
                GR = NB * H2
                dve.tensor_scalar(gi[:], bank[0][0:GR, 0:S], gates_b[0:GR, 0:1], None, ALU.add)
                chain.link(dve.tensor_scalar(gf[:], bank[0][32:32 + GR, 0:S], gates_b[32:32 + GR, 0:1], None, ALU.add))
                dve.scalar_tensor_tensor(gl[:], gf[:], -1.0, gf[:], ALU.mult, ALU.max).then_inc(abs_ready.sem, 1)
                dve.wait_ge(*ln_ready.at(i))
                chain.link(dve.scalar_tensor_tensor(gf[:], gf[:], 0.0, gl[:], ALU.min, ALU.subtract))
                chain.link(dve.tensor_tensor_scan(cs[:], ones16[:], gf[:], 0.0, ALU.mult, ALU.add))
                chain.link(dve.tensor_tensor(ga[:], gi[:], cs[:], ALU.subtract))
                chain.link(dve.tensor_tensor_scan(pm[:], ones16[:], ga[:], NEG, ALU.mult, ALU.max))
                dve.tensor_tensor(gm[:], cs[:], pm[:], ALU.add).then_inc(pm_ready.sem, 1)
                chain.link(dve.tensor_scalar(neg_pm[0:GR, :], pm[:], -1.0, None, ALU.mult))
                chain.link(dve.scalar_tensor_tensor(gi[:], pm[:], -1.0, neg_pm[0:GR, :], ALU.mult, ALU.subtract))
                chain.link(dve.tensor_copy(pb2[:], gi[:]))
                dve.tensor_copy(neg_pm[32:32 + GR, :], pb2[:])
                dve.tensor_tensor(neg_pm[64:64 + GR, :], gi[:], pb2[:], ALU.subtract).then_inc(neg_pm_ready.sem, 1)
                h3 = hh.rearrange("p c h d -> p (c h) d")
                hs3 = R[:].rearrange("p c (h d) -> p (c h) d", d=DH2)

                def normaliser(b, part):
                    src = bank[2 + b][:].rearrange("p (c h j) -> p c h j", c=QC, h=H2)
                    cc = slice(b * QC, (b + 1) * QC)
                    ch = slice(b * QC * H2, (b + 1) * QC * H2)
                    wide = [P, QC * H2, DH2]
                    if part == 0:
                        dve.wait_ge(*o5_tr.at(i, b + 1))
                        if b == 0:
                            dve.wait_ge(*cols_copied.at(i))
                        chain.link(dve.tensor_copy(den[:, cc, :], src[:, :, :, DH2]))
                        chain.link(dve.scalar_tensor_tensor(den[:, cc], den[:, cc], -1.0, den[:, cc], ALU.mult, ALU.max))
                        chain.link(dve.tensor_tensor(den[:, cc], den[:, cc], em_col[:, cc], ALU.max))
                    if part == 1:
                        chain.link(dve.tensor_scalar(den[:, cc], den[:, cc], 1e-6, None, ALU.add))
                        chain.link(dve.reciprocal(den[:, cc], den[:, cc]))
                        chain.link(dve.tensor_tensor(hh[:, cc], src[:, :, :, 0:DH2], den[:, cc].unsqueeze(3).to_broadcast([P, QC, H2, DH2]), ALU.mult))
                    if part == 2:
                        chain.link(dve.tensor_reduce(hm[:, 0, ch], h3[:, ch], AX.X, ALU.add))
                        chain.link(dve.tensor_scalar(hm[:, 1, ch], hm[:, 0, ch], 1.0 / DH2, None, ALU.mult))
                        chain.link(dve.tensor_tensor(h3[:, ch], h3[:, ch], hm[:, 1, ch].unsqueeze(2).to_broadcast(wide), ALU.subtract))
                    if part == 3:
                        chain.link(dve.tensor_tensor(hs3[:, ch], h3[:, ch], h3[:, ch], ALU.mult))
                        last = dve.tensor_reduce(hm[:, 0, ch], hs3[:, ch], AX.X, ALU.add)
                        if b == NB - 1:
                            last.then_inc(var2_ready.sem, 1)

                for n in range(MU):
                    b, g, j = n // H2, (n // 4) % 2, n % 4
                    dve.wait_ge(*decay_ready.at(i, n + 1))
                    if n >= 8 and n % 4 == 0:
                        dve.wait_ge(*pv2_ready.at(i, n // 4 - 1))
                    dve.tensor_tensor(cT[:, g, j, :], m_banks(n)[1][:, 0:S + P], decay[:, n % DEEP, :], ALU.mult).then_inc(c_ready.sem, 1)
                    if n >= MU - 3:
                        normaliser(0, n - (MU - 3))
                normaliser(0, 3)
                for part in range(4):
                    normaliser(1, part)
                wide = [P, NC * H2, DH2]
                dve.wait_ge(*rstd2_ready.at(i))
                chain.link(dve.reciprocal(hrs[:], hrs[:]))
                chain.link(dve.tensor_tensor(h3, h3, hrs[:].unsqueeze(2).to_broadcast(wide), ALU.mult))
                hx = hh.rearrange("p c h d -> p c (h d)")
                chain.link(dve.tensor_tensor(hx, hx, out_w_rows[:].unsqueeze(1).to_broadcast([P, NC, P]), ALU.mult))
                done = []
                for b in range(NB):
                    cc = slice(b * QC, (b + 1) * QC)
                    done.append(dve_b.at(i, chain.mark(dve.tensor_tensor(R[:, cc], hx[:, cc], X[:, cc], ALU.add))))
                layernorm(4, done)

                if following:
                    values(i + 1)
                dve.wait_ge(*fl_ready.at(i))
                chain.link(dve.tensor_tensor(fl[:], bank[0][:, 0:NB * E].rearrange("p (b e) -> p b e", b=NB),
                                             ffn_gb_rows[:].unsqueeze(1).to_broadcast([P, NB, E]), ALU.add), passed)
                for b in range(NB):
                    last = dve.max(ftop[:, b, :], fl[:, b, :])
                chain.link(last)
                dve.tensor_tensor(fgate[:], fl[:], ftop[:, :, 1:2].to_broadcast([P, NB, E]), ALU.is_ge)
                chain.link(dve.tensor_tensor(hm[:, 0, 0:NB * E].rearrange("p (b e) -> p b e", b=NB), fl[:], ftop[:, :, 0:1].to_broadcast([P, NB, E]), ALU.subtract))
                dve.tensor_copy(fl[:], hm[:, 0, 0:NB * E].rearrange("p (b e) -> p b e", b=NB)).then_inc(fmax_ready.sem, 1)
                dve.wait_ge(*fe_ready.at(i))
                chain.link(dve.tensor_tensor(fgate[:], fgate[:], fe[:], ALU.mult))
                chain.link(dve.tensor_reduce(fs[:, 0, :], fgate[:], AX.X, ALU.add))
                chain.link(dve.reciprocal(fs[:, 1, :], fs[:, 0, :]))
                chain.link(dve.tensor_tensor(fgate[:], fgate[:], fs[:, 1, :].unsqueeze(2).to_broadcast([P, NB, E]), ALU.mult))
                for n in range(0, FU, 2):
                    dve.wait_ge(*f_act.at(i, n + 2))
                    marks = [None, None]
                    for j in range(4):
                        for u in range(2):
                            c, half = f_units[n + u]
                            e = 4 * half + j
                            if j > 0:
                                chain.wait(marks[u])
                            ins = dve.scalar_tensor_tensor(R[:, c, :], gl_act[:, (n + u) % 4, j * P:(j + 1) * P], fgate[:, c // QC, e:e + 1],
                                                           X[:, c, :] if e == 0 else R[:, c, :], ALU.mult, ALU.add)
                            if j < 3 or u == 0:
                                marks[u] = chain.mark(ins)
                    ins.then_inc(f_added.sem, 1)
                    dve.wait_ge(*f_added.at(i, n // 2 + 1))
                chain.close()

            head_chain = Chain(dve, dve_h, 0)
            for n in range(HEAD_PARTS):
                head(0, n, head_chain)
                if n == 0:
                    values(0)
            with dve.Fori(0, STEPS - 1) as i:
                step(i, True)
            step(STEPS - 1, False)
            chain = Chain(dve, dve_last, 0)
            dve.wait_ge(out_saved.sem, 16 * STEPS + 16)
            statistics(chain)
            normalised(chain, STEPS, 0, Y)


_TRANSPOSED = {"L0_attn_" + n + "T": "L0_attn_" + n for n in ("wq", "wk", "wv", "wo", "lin1", "lin2", "w1", "w2", "mem")}
_TRANSPOSED.update({"L0_xattn_" + n + "T": "L0_xattn_" + n for n in ("wq", "wk", "wv", "wo")})
_TRANSPOSED.update({"L0_ffn_router_wT": "L0_ffn_router_w", "L1_xattn_igate_wT": "L1_xattn_igate_w",
                    "L1_xattn_fgate_wT": "L1_xattn_fgate_w", "L1_ffn_gate_wT": "L1_ffn_gate_w"})
_PLAIN = ["x", "ctx_1024", "mask_BxSxS2_bf1", "L0_attn_mem", "L0_attn_w2", "L0_attn_b1", "L0_attn_b2",
          "L0_attn_alpha", "L0_attn_theta", "L0_xattn_bq", "L0_xattn_bk", "L0_xattn_bv", "L0_xattn_bo",
          "L0_ffn_w1", "L0_ffn_w2", "L1_attn_W_Q", "L1_attn_W_K", "L1_attn_W_V", "L1_xattn_igate_b",
          "L1_xattn_fgate_b", "L1_xattn_out_w", "L1_ffn_gate_b", "L1_ffn_expert_b"]


def kernel(**inputs):
    import numpy as _np
    import concourse.bacc as _bacc
    from concourse import mybir as _mybir
    from concourse.bass_utils import run_bass_kernel_spmd as _run

    laid = {n: inputs[n] for n in _PLAIN}
    for n in ("L0_attn_alpha", "L0_attn_theta"):
        laid[n] = _np.reshape(inputs[n], (1,))
    for new, old in _TRANSPOSED.items():
        laid[new] = _np.transpose(inputs[old])
    laid["xT"] = _np.transpose(_np.reshape(inputs["x"], (B * S, D)))
    laid["ctxT"] = _np.transpose(_np.reshape(inputs["ctx_1024"], (B * S, D)))
    laid["L0_attn_b1_cols"] = _np.transpose(_np.reshape(inputs["L0_attn_b1"], (FC, P)))
    laid["maskT"] = _np.transpose(inputs["mask_BxSxS2_bf1"], (0, 2, 1))
    laid["L1_ffn_expert_wT"] = _np.reshape(_np.transpose(inputs["L1_ffn_expert_w"], (2, 0, 1)), (D, E * D))

    nc = _bacc.Bacc("TRN2", target_bir_lowering=False, num_devices=1)
    arrays, args = {}, {}
    for name, value in laid.items():
        value = _np.ascontiguousarray(value)
        arrays[f"in_{name}_dram"] = value
        args[name] = nc.dram_tensor(f"in_{name}_dram", value.shape, _mybir.dt.from_np(value.dtype), kind="ExternalInput").ap()
    out = nc.dram_tensor("out_0_dram", (B, S, D), _mybir.dt.float32, kind="ExternalOutput").ap()
    parts_dram = nc.dram_tensor("parts_dram", (2, 3, D, T), _mybir.dt.bfloat16, kind="Internal").ap()
    decoder_kernel(nc, args, out, parts_dram)
    r = _run(nc, [arrays], core_ids=[0])
    return r.results[0]["out_0_dram"]
```
